# Optimizing a Trainium2 kernel written in Bass

```python
import numpy as np
import jax
import jax.numpy as jnp

def _softmax(x, axis=-1):
    return jax.nn.softmax(x, axis=axis)

def _gelu(x):
    return jax.nn.gelu(x, approximate=True)

def _silu(x):
    return jax.nn.silu(x)

def _sigmoid(x):
    return jax.nn.sigmoid(x)

def _layernorm(x, axis=-1, eps=1e-05):
    m = jnp.mean(x, axis=axis, keepdims=True)
    v = jnp.var(x, axis=axis, keepdims=True)
    return (x - m) / jnp.sqrt(v + eps)

def _scatter_add(tgt, idx, src, axis=0):
    return tgt.at[idx].add(src)

def _segment_sum(src, seg, n):
    return jax.ops.segment_sum(src, seg, n)
kernel_name = 'mk_early_fusion_embed_d1_tok_img768_r4_a48635'

def setup_inputs(seed: int=0):
    np.random.seed(seed)
    _w = jnp.asarray

    def _rec_inputs():
        import jax
        import jax.numpy as jnp
        _rk = jax.random.key(seed)
        x = -0.00016672 + 0.999947 * jax.random.normal(jax.random.fold_in(_rk, 1), (64, 3, 64, 64), jnp.float32)
        x_txt = jax.random.randint(jax.random.fold_in(_rk, 51), (64, 32), 0, 8000, jnp.int32)
        fside_BS_position = 498.436 + 289.021 * jax.random.normal(jax.random.fold_in(_rk, 71), (64, 32), jnp.float32)
        fside_BS_age = 50.119 + 28.9252 * jax.random.normal(jax.random.fold_in(_rk, 72), (64, 32), jnp.float32)
        itok_BS_0_3 = jax.random.randint(jax.random.fold_in(_rk, 73), (64, 32), 0, 4, jnp.int32)
        return (x, x_txt, fside_BS_position, fside_BS_age, itok_BS_0_3)
    x, x_txt, fside_BS_position, fside_BS_age, itok_BS_0_3 = _rec_inputs()

    def _L0_tok_setup():
        import jax, jax.numpy as jnp
        import numpy as np
        PH = PW = 16
        DIM = 192
        EPS = 1e-05

        def _patchify(x):
            B, C, H, W = x.shape
            h, w = (H // PH, W // PW)
            x = x.reshape(B, C, h, PH, w, PW)
            x = x.transpose(0, 2, 4, 3, 5, 1)
            return x.reshape(B, h * w, PH * PW * C)
        key = jax.random.key(seed)
        k1, k2, k3, k4, k5 = jax.random.split(key, 5)
        B, C, H, W = (64, 3, 96, 96)
        patch_dim = C * PH * PW
        x = jax.random.normal(k1, (B, C, H, W), dtype=jnp.float32)
        gamma = jnp.ones((patch_dim,), dtype=jnp.float32)
        beta = jnp.zeros((patch_dim,), dtype=jnp.float32)
        W_proj = jax.random.normal(k2, (DIM, patch_dim), dtype=jnp.float32) * (1.0 / np.sqrt(patch_dim))
        b_proj = jax.random.normal(k3, (DIM,), dtype=jnp.float32) * 0.01
        return {'x': x, 'gamma': gamma, 'beta': beta, 'W_proj': W_proj, 'b_proj': b_proj}
    _L0_tok_all = _L0_tok_setup()
    _L0_tok_in = {k: v for k, v in _L0_tok_all.items() if k in ('gamma', 'beta', 'W_proj', 'b_proj')}
    del _L0_tok_all

    def _L0_txt_setup():
        import jax, jax.numpy as jnp
        import numpy as np
        VOCAB, H, B, S = (8000, 192, 32, 512)
        T2V_ZERO_PREFIX = 5

        def t2v(tau, f, w, b, w0, b0):
            v1 = f(tau * w[0] + b[0])
            v2 = tau * w0[0] + b0[0]
            return jnp.concatenate([v1, v2], axis=-1)
        key = jax.random.key(seed)
        ks = jax.random.split(key, 16)
        d = 0.01
        token_emb = jax.random.uniform(ks[0], (VOCAB, H), jnp.float32, -d, d)
        token_emb = token_emb.at[0].set(0.0)
        seg_emb = jax.random.uniform(ks[1], (4, H), jnp.float32, -d, d)
        seg_emb = seg_emb.at[0].set(0.0)
        return {'tokens': jax.random.randint(ks[2], (B, S), 0, VOCAB), 'position': jax.random.uniform(ks[3], (B, S), jnp.float32) * 1000.0, 'age': jax.random.uniform(ks[4], (B, S), jnp.float32) * 100.0, 'segment': jax.random.randint(ks[5], (B, S), 0, 4), 'token_emb': token_emb, 'seg_emb': seg_emb, 'w_age': jax.random.uniform(ks[6], (1, H - 1), jnp.float32, -d, d), 'b_age': jax.random.uniform(ks[7], (1, H - 1), jnp.float32, -d, d), 'w0_age': jax.random.uniform(ks[8], (1, 1), jnp.float32, -d, d), 'b0_age': jax.random.uniform(ks[9], (1, 1), jnp.float32, -d, d), 'w_abs': jax.random.uniform(ks[10], (1, H - 1), jnp.float32, -d, d), 'b_abs': jax.random.uniform(ks[11], (1, H - 1), jnp.float32, -d, d), 'w0_abs': jax.random.uniform(ks[12], (1, 1), jnp.float32, -d, d), 'b0_abs': jax.random.uniform(ks[13], (1, 1), jnp.float32, -d, d), 'alpha_age': jax.random.normal(ks[14], (), jnp.float32) * 0.1, 'alpha_abs': jax.random.normal(ks[15], (), jnp.float32) * 0.1, 'alpha_seg': jax.random.normal(jax.random.fold_in(key, 99), (), jnp.float32) * 0.1}
    _L0_txt_all = _L0_txt_setup()
    _L0_txt_in = {k: v for k, v in _L0_txt_all.items() if k in ('token_emb', 'seg_emb', 'w_age', 'b_age', 'w0_age', 'b0_age', 'w_abs', 'b_abs', 'w0_abs', 'b0_abs', 'alpha_age', 'alpha_abs', 'alpha_seg')}
    del _L0_txt_all

    def _L0_attn_setup():
        import jax, jax.numpy as jnp
        import numpy as np
        D_MODEL = 192
        D_STATE = 16
        D_CONV = 4
        EXPAND = 2
        D_INNER = EXPAND * D_MODEL
        DT_RANK = (D_MODEL + 15) // 16
        BATCH = 2
        SEQLEN = 256

        def _mamba(x, in_w, conv_w, conv_b, xproj_w, dt_w, dt_b, A_log, Dp, out_w):
            B, L, _ = x.shape
            xz = x @ in_w.T
            xc, z = jnp.split(xz, 2, axis=-1)
            K = conv_w.shape[1]
            xpad = jnp.pad(xc, ((0, 0), (K - 1, 0), (0, 0)))
            xconv = conv_b + sum((conv_w[:, k] * xpad[:, k:k + L, :] for k in range(K)))
            u = jax.nn.silu(xconv)
            proj = u @ xproj_w.T
            dt_rank = dt_w.shape[1]
            n = A_log.shape[1]
            dtx, Bm, Cm = jnp.split(proj, [dt_rank, dt_rank + n], axis=-1)
            dt = jax.nn.softplus(dtx @ dt_w.T + dt_b)
            A = -jnp.exp(A_log)
            dA = jnp.exp(dt[..., None] * A)
            dBu = dt[..., None] * Bm[:, :, None, :] * u[..., None]

            def step(h, inp):
                dA_t, dBu_t, C_t = inp
                h = dA_t * h + dBu_t
                y = jnp.einsum('bdn,bn->bd', h, C_t)
                return (h, y)
            h0 = jnp.zeros((B, u.shape[-1], n), x.dtype)
            _, ys = jax.lax.scan(step, h0, (dA.transpose(1, 0, 2, 3), dBu.transpose(1, 0, 2, 3), Cm.transpose(1, 0, 2)))
            y = ys.transpose(1, 0, 2) + u * Dp
            y = y * jax.nn.silu(z)
            return y @ out_w.T
        key = jax.random.key(seed)
        ks = jax.random.split(key, 10)
        s = 0.02
        f32 = jnp.float32
        x = jax.random.normal(ks[0], (BATCH, SEQLEN, D_MODEL), f32)
        bm_in_w = jax.random.normal(ks[1], (2 * D_MODEL, D_MODEL), f32) * s
        bm_in_b = jnp.zeros((2 * D_MODEL,), f32)
        bm_out_w = jax.random.normal(ks[2], (D_MODEL, D_MODEL), f32) * s
        bm_out_b = jnp.zeros((D_MODEL,), f32)
        m_in_w = jax.random.normal(ks[3], (2 * D_INNER, D_MODEL), f32) * s
        m_conv_w = jax.random.normal(ks[4], (D_INNER, D_CONV), f32) * s
        m_conv_b = jnp.zeros((D_INNER,), f32)
        m_xproj_w = jax.random.normal(ks[5], (DT_RANK + 2 * D_STATE, D_INNER), f32) * s
        m_dt_w = jax.random.normal(ks[6], (D_INNER, DT_RANK), f32) * s
        m_dt_b = jnp.full((D_INNER,), -4.6, f32)
        m_A_log = jnp.log(jnp.broadcast_to(jnp.arange(1, D_STATE + 1, dtype=f32), (D_INNER, D_STATE)))
        m_D = jnp.ones((D_INNER,), f32)
        m_out_w = jax.random.normal(ks[7], (D_MODEL, D_INNER), f32) * s
        ln_g = jnp.ones((D_MODEL,), f32)
        ln_b = jnp.zeros((D_MODEL,), f32)
        return {'x': x, 'bm_in_w': bm_in_w, 'bm_in_b': bm_in_b, 'bm_out_w': bm_out_w, 'bm_out_b': bm_out_b, 'm_in_w': m_in_w, 'm_conv_w': m_conv_w, 'm_conv_b': m_conv_b, 'm_xproj_w': m_xproj_w, 'm_dt_w': m_dt_w, 'm_dt_b': m_dt_b, 'm_A_log': m_A_log, 'm_D': m_D, 'm_out_w': m_out_w, 'ln_g': ln_g, 'ln_b': ln_b}
    _L0_attn_all = _L0_attn_setup()
    _L0_attn_in = {k: v for k, v in _L0_attn_all.items() if k in ('bm_in_w', 'bm_in_b', 'bm_out_w', 'bm_out_b', 'm_in_w', 'm_conv_w', 'm_conv_b', 'm_xproj_w', 'm_dt_w', 'm_dt_b', 'm_A_log', 'm_D', 'm_out_w', 'ln_g', 'ln_b')}
    del _L0_attn_all

    def _L0_ffn_setup():
        import jax, jax.numpy as jnp
        import numpy as np
        B, T, D, E, K = (4, 512, 192, 8, 2)
        H = 4 * D
        key = jax.random.key(seed)
        k0, k1, k2, k3, k4 = jax.random.split(key, 5)
        s = 0.02
        return {'x': jax.random.normal(k0, (B, T, D), jnp.float32), 'router_w': jax.random.uniform(k1, (E, D), jnp.float32, -s * 0.1, s * 0.1), 'Wg': jax.random.uniform(k2, (E, H, D), jnp.float32, -s * 0.4, s * 0.4), 'Wu': jax.random.uniform(k3, (E, H, D), jnp.float32, -s * 0.4, s * 0.4), 'Wd': jax.random.normal(k4, (E, D, H), jnp.float32) * 0.01}
    _L0_ffn_all = _L0_ffn_setup()
    _L0_ffn_in = {k: v for k, v in _L0_ffn_all.items() if k in ('router_w', 'Wg', 'Wu', 'Wd')}
    del _L0_ffn_all
    return {'x': x, 'x_txt': x_txt, 'fside_BS_position': fside_BS_position, 'fside_BS_age': fside_BS_age, 'itok_BS_0_3': itok_BS_0_3, 'L0_tok_gamma': _L0_tok_in['gamma'], 'L0_tok_beta': _L0_tok_in['beta'], 'L0_tok_W_proj': _L0_tok_in['W_proj'], 'L0_tok_b_proj': _L0_tok_in['b_proj'], 'L0_txt_token_emb': _L0_txt_in['token_emb'], 'L0_txt_seg_emb': _L0_txt_in['seg_emb'], 'L0_txt_w_age': _L0_txt_in['w_age'], 'L0_txt_b_age': _L0_txt_in['b_age'], 'L0_txt_w0_age': _L0_txt_in['w0_age'], 'L0_txt_b0_age': _L0_txt_in['b0_age'], 'L0_txt_w_abs': _L0_txt_in['w_abs'], 'L0_txt_b_abs': _L0_txt_in['b_abs'], 'L0_txt_w0_abs': _L0_txt_in['w0_abs'], 'L0_txt_b0_abs': _L0_txt_in['b0_abs'], 'L0_txt_alpha_age': _L0_txt_in['alpha_age'], 'L0_txt_alpha_abs': _L0_txt_in['alpha_abs'], 'L0_txt_alpha_seg': _L0_txt_in['alpha_seg'], 'L0_attn_bm_in_w': _L0_attn_in['bm_in_w'], 'L0_attn_bm_in_b': _L0_attn_in['bm_in_b'], 'L0_attn_bm_out_w': _L0_attn_in['bm_out_w'], 'L0_attn_bm_out_b': _L0_attn_in['bm_out_b'], 'L0_attn_m_in_w': _L0_attn_in['m_in_w'], 'L0_attn_m_conv_w': _L0_attn_in['m_conv_w'], 'L0_attn_m_conv_b': _L0_attn_in['m_conv_b'], 'L0_attn_m_xproj_w': _L0_attn_in['m_xproj_w'], 'L0_attn_m_dt_w': _L0_attn_in['m_dt_w'], 'L0_attn_m_dt_b': _L0_attn_in['m_dt_b'], 'L0_attn_m_A_log': _L0_attn_in['m_A_log'], 'L0_attn_m_D': _L0_attn_in['m_D'], 'L0_attn_m_out_w': _L0_attn_in['m_out_w'], 'L0_attn_ln_g': _L0_attn_in['ln_g'], 'L0_attn_ln_b': _L0_attn_in['ln_b'], 'L0_ffn_router_w': _L0_ffn_in['router_w'], 'L0_ffn_Wg': _L0_ffn_in['Wg'], 'L0_ffn_Wu': _L0_ffn_in['Wu'], 'L0_ffn_Wd': _L0_ffn_in['Wd']}

def reference(x, x_txt, fside_BS_position, fside_BS_age, itok_BS_0_3, L0_tok_gamma, L0_tok_beta, L0_tok_W_proj, L0_tok_b_proj, L0_txt_token_emb, L0_txt_seg_emb, L0_txt_w_age, L0_txt_b_age, L0_txt_w0_age, L0_txt_b0_age, L0_txt_w_abs, L0_txt_b_abs, L0_txt_w0_abs, L0_txt_b0_abs, L0_txt_alpha_age, L0_txt_alpha_abs, L0_txt_alpha_seg, L0_attn_bm_in_w, L0_attn_bm_in_b, L0_attn_bm_out_w, L0_attn_bm_out_b, L0_attn_m_in_w, L0_attn_m_conv_w, L0_attn_m_conv_b, L0_attn_m_xproj_w, L0_attn_m_dt_w, L0_attn_m_dt_b, L0_attn_m_A_log, L0_attn_m_D, L0_attn_m_out_w, L0_attn_ln_g, L0_attn_ln_b, L0_ffn_router_w, L0_ffn_Wg, L0_ffn_Wu, L0_ffn_Wd):
    import jax
    import jax.numpy as jnp

    def _L0_tok_ref(x, gamma, beta, W_proj, b_proj):
        import jax, jax.numpy as jnp
        import numpy as np
        PH = PW = 16
        DIM = 192
        EPS = 1e-05

        def _patchify(x):
            B, C, H, W = x.shape
            h, w = (H // PH, W // PW)
            x = x.reshape(B, C, h, PH, w, PW)
            x = x.transpose(0, 2, 4, 3, 5, 1)
            return x.reshape(B, h * w, PH * PW * C)
        p = _patchify(x)
        mu = jnp.mean(p, axis=-1, keepdims=True)
        var = jnp.mean(jnp.square(p - mu), axis=-1, keepdims=True)
        p = (p - mu) * jax.lax.rsqrt(var + EPS) * gamma + beta
        return jnp.einsum('bnd,ed->bne', p, W_proj) + b_proj

    def _L0_txt_ref(tokens, position, age, segment, token_emb, seg_emb, w_age, b_age, w0_age, b0_age, w_abs, b_abs, w0_abs, b0_abs, alpha_age, alpha_abs, alpha_seg):
        import jax, jax.numpy as jnp
        import numpy as np
        VOCAB, H, B, S = (8000, 192, 32, 512)
        T2V_ZERO_PREFIX = 5

        def t2v(tau, f, w, b, w0, b0):
            v1 = f(tau * w[0] + b[0])
            v2 = tau * w0[0] + b0[0]
            return jnp.concatenate([v1, v2], axis=-1)
        x = token_emb[tokens]
        seq_mask = (jnp.arange(tokens.shape[1]) >= T2V_ZERO_PREFIX)[None, :, None]
        pos = t2v(age[..., None], jnp.cos, w_age, b_age, w0_age, b0_age)
        pos = jnp.where(seq_mask, pos, 0.0)
        x = x + alpha_age * pos
        pos = t2v(position[..., None], jnp.sin, w_abs, b_abs, w0_abs, b0_abs)
        pos = jnp.where(seq_mask, pos, 0.0)
        x = x + alpha_abs * pos
        x = x + alpha_seg * seg_emb[segment]
        return x

    def _L0_attn_ref(x, bm_in_w, bm_in_b, bm_out_w, bm_out_b, m_in_w, m_conv_w, m_conv_b, m_xproj_w, m_dt_w, m_dt_b, m_A_log, m_D, m_out_w, ln_g, ln_b):
        import jax, jax.numpy as jnp
        import numpy as np
        D_MODEL = 192
        D_STATE = 16
        D_CONV = 4
        EXPAND = 2
        D_INNER = EXPAND * D_MODEL
        DT_RANK = (D_MODEL + 15) // 16
        BATCH = 2
        SEQLEN = 256

        def _mamba(x, in_w, conv_w, conv_b, xproj_w, dt_w, dt_b, A_log, Dp, out_w):
            B, L, _ = x.shape
            xz = x @ in_w.T
            xc, z = jnp.split(xz, 2, axis=-1)
            K = conv_w.shape[1]
            xpad = jnp.pad(xc, ((0, 0), (K - 1, 0), (0, 0)))
            xconv = conv_b + sum((conv_w[:, k] * xpad[:, k:k + L, :] for k in range(K)))
            u = jax.nn.silu(xconv)
            proj = u @ xproj_w.T
            dt_rank = dt_w.shape[1]
            n = A_log.shape[1]
            dtx, Bm, Cm = jnp.split(proj, [dt_rank, dt_rank + n], axis=-1)
            dt = jax.nn.softplus(dtx @ dt_w.T + dt_b)
            A = -jnp.exp(A_log)
            dA = jnp.exp(dt[..., None] * A)
            dBu = dt[..., None] * Bm[:, :, None, :] * u[..., None]

            def step(h, inp):
                dA_t, dBu_t, C_t = inp
                h = dA_t * h + dBu_t
                y = jnp.einsum('bdn,bn->bd', h, C_t)
                return (h, y)
            h0 = jnp.zeros((B, u.shape[-1], n), x.dtype)
            _, ys = jax.lax.scan(step, h0, (dA.transpose(1, 0, 2, 3), dBu.transpose(1, 0, 2, 3), Cm.transpose(1, 0, 2)))
            y = ys.transpose(1, 0, 2) + u * Dp
            y = y * jax.nn.silu(z)
            return y @ out_w.T
        mparams = (m_in_w, m_conv_w, m_conv_b, m_xproj_w, m_dt_w, m_dt_b, m_A_log, m_D, m_out_w)
        xp = x @ bm_in_w.T + bm_in_b
        x_f, x_b = jnp.split(xp, 2, axis=-1)
        out_f = _mamba(x_f, *mparams)
        out_b = jnp.flip(_mamba(jnp.flip(x_b, axis=1), *mparams), axis=1)
        mo = (out_f + out_b) @ bm_out_w.T + bm_out_b
        h = mo + x
        mu = jnp.mean(h, axis=-1, keepdims=True)
        var = jnp.mean(jnp.square(h - mu), axis=-1, keepdims=True)
        return (h - mu) * jax.lax.rsqrt(var + 1e-05) * ln_g + ln_b

    def _L0_ffn_ref(x, router_w, Wg, Wu, Wd):
        import jax, jax.numpy as jnp
        import numpy as np
        B, T, D, E, K = (4, 512, 192, 8, 2)
        H = 4 * D
        Bv, Tv, Dv = x.shape
        N = Bv * Tv
        xf = x.reshape(N, Dv)
        logits = (xf @ router_w.T).astype(jnp.float32)
        top_logits, top_idx = jax.lax.top_k(logits, K)
        top_w = jax.nn.softmax(top_logits, axis=-1).astype(x.dtype)
        out = jnp.zeros_like(xf)
        for e in range(E):
            w_e = jnp.sum(top_w * (top_idx == e), axis=-1)
            h = jax.nn.silu(xf @ Wg[e].T) * (xf @ Wu[e].T)
            out = out + h @ Wd[e].T * w_e[:, None]
        return out.reshape(Bv, Tv, Dv)
    h = _L0_tok_ref(x, L0_tok_gamma, L0_tok_beta, L0_tok_W_proj, L0_tok_b_proj)
    h = jnp.concatenate([h, _L0_txt_ref(x_txt, fside_BS_position, fside_BS_age, itok_BS_0_3, L0_txt_token_emb, L0_txt_seg_emb, L0_txt_w_age, L0_txt_b_age, L0_txt_w0_age, L0_txt_b0_age, L0_txt_w_abs, L0_txt_b_abs, L0_txt_w0_abs, L0_txt_b0_abs, L0_txt_alpha_age, L0_txt_alpha_abs, L0_txt_alpha_seg)], axis=1)
    h = h + _L0_attn_ref(_layernorm(h, axis=-1), L0_attn_bm_in_w, L0_attn_bm_in_b, L0_attn_bm_out_w, L0_attn_bm_out_b, L0_attn_m_in_w, L0_attn_m_conv_w, L0_attn_m_conv_b, L0_attn_m_xproj_w, L0_attn_m_dt_w, L0_attn_m_dt_b, L0_attn_m_A_log, L0_attn_m_D, L0_attn_m_out_w, L0_attn_ln_g, L0_attn_ln_b)
    h = h + _L0_ffn_ref(_layernorm(h, axis=-1), L0_ffn_router_w, L0_ffn_Wg, L0_ffn_Wu, L0_ffn_Wd)
    return h

_drawn_inputs = setup_inputs


def setup_inputs(seed=0):
    import zlib

    import numpy as np

    out = dict(_drawn_inputs(seed))
    spreads = {'L0_tok_gamma': (1.0, 0.2),
     'L0_tok_beta': (0.0, 0.1),
     'L0_attn_bm_in_b': (0.0, 0.8),
     'L0_attn_bm_out_b': (0.0, 0.1),
     'L0_attn_m_conv_b': (0.0, 0.8),
     'L0_attn_m_dt_b': (-4.599999904632568, 0.6),
     'L0_attn_m_D': (1.0, 0.6),
     'L0_attn_ln_g': (1.0, 0.2),
     'L0_attn_ln_b': (0.0, 0.1)}
    factors = {'L0_tok_b_proj': 7.033,
     'L0_txt_seg_emb': 8.0,
     'L0_txt_b_age': 8.0,
     'L0_txt_b_abs': 8.0,
     'L0_attn_bm_in_w': 8.0,
     'L0_attn_bm_out_w': 8.0,
     'L0_attn_m_in_w': 8.0,
     'L0_attn_m_conv_w': 8.0,
     'L0_attn_m_xproj_w': 8.0,
     'L0_attn_m_dt_w': 8.0,
     'L0_attn_m_A_log': 8.0,
     'L0_attn_m_out_w': 8.0,
     'L0_ffn_router_w': 8.0,
     'L0_ffn_Wg': 8.0,
     'L0_ffn_Wu': 8.0,
     'L0_ffn_Wd': 8.0}
    for name, (base, spread) in spreads.items():
        noise = np.random.default_rng([zlib.crc32(name.encode()), seed]).standard_normal(out[name].shape)
        drawn = base * np.exp(spread * noise) if base else spread * noise
        out[name] = jnp.asarray(drawn.astype(out[name].dtype))
    for name, factor in factors.items():
        out[name] = (out[name] * factor).astype(out[name].dtype)
    return out
```

```python
from contextlib import ExitStack
import math

import concourse.bass as bass
from concourse import mybir

F32 = mybir.dt.float32
BF16 = mybir.dt.bfloat16
I32 = mybir.dt.int32
ALU = mybir.AluOpType
ACT = mybir.ActivationFunctionType
AX = mybir.AxisListType

B, L, LI, LT = 64, 48, 16, 32
D, DI, NS, R = 192, 384, 16, 12
KH = D // 2
PD = 768
CB = 8
NCH = B // CB
T = CB * L
NT = T // 128
NC = DI // 128
NG = 4
GN = NS // NG
UD = NG * NC
U2 = 2 * UD
NRING = 4
KC = 3
EPS = 1e-5
E, HF = 8, 768
NTOK = B * L
NTT = NTOK // 128
NJ = 2 * NTT + E - 1
SPARES = 5
XW = D + 4

TWO_PI = 2 * math.pi
C1 = 6.28125
C2 = 0.0019350051879882812
C3 = TWO_PI - C1 - C2
MAGIC = 12582912.0
PI_IN = 3.1415925


class Steps:

    def __init__(self, sem, names):
        self.sem, self.names = sem, names.split()

    def after(self, name, turn):
        return len(self.names) * turn + self.names.index(name) + 1


def wait(eng, sem, value):
    if isinstance(value, int) and value <= 0:
        return
    eng.wait_ge(sem, value)


def build_mamba(nc, a, dram, ident, logits, sem):
    with ExitStack() as ctx:
        def sb(name, shape, dt=F32):
            return ctx.enter_context(nc.sbuf_tensor(name, shape, dt))

        def pb(name, shape, dt=F32):
            return ctx.enter_context(nc.psum_tensor(name, shape, dt))

        ones = sb("ones", [128, 128])
        sel = sb("sel", [96, 2 * NS, 128], BF16)
        wxz = sb("wxz", [KH, 2, 2, 2 * DI])
        bxz = sb("bxz", [128, 2, 2 * NC])
        gw = sb("gw", [128, PD // 128, D])
        proj_sum = sb("proj_sum", [128, D])
        proj_bias = sb("proj_bias", [128, D])
        w2t = sb("w2t", [128, NC, D])
        xpw_bc = sb("xpw_bc", [128, NC, 96])
        xpw_dt = sb("xpw_dt", [128, NC, R])
        dtw = sb("dtw", [R, DI])
        dtb = sb("dtb", [128, NC])
        cw = sb("cw", [128, NC, KC + 1])
        cb = sb("cb", [128, NC])
        dskip = sb("dskip", [128, NC])
        aneg = sb("aneg", [128, NC, NS])
        w_tau = sb("w_tau", [128, 2, D])
        b_tau = sb("b_tau", [128, 2, D])
        alpha = sb("alpha", [128, 3])
        mask = sb("mask", [128, 1])
        am = sb("am", [128, 2])
        outb = sb("outb", [1, D])
        ln_g = sb("ln_g", [128, D])
        ln_b = sb("ln_b", [128, D])
        rw = sb("rw", [KH, 2, E])
        eps = sb("eps", [128, 1])
        spare_i = sb("spare_i", [128, SPARES], I32)
        halfpi = sb("halfpi", [128, 1])
        ptok = sb("ptok", [128, PD])
        pT = sb("pT", [128, PD // 128, 128])
        ids = sb("ids", [128, 4], I32)
        taus = sb("taus", [128, 4])
        tok_rows = sb("tok_rows", [128, 2, D])
        seg_rows = sb("seg_rows", [128, 2, D])
        theta = sb("theta", [128, 2, 2, D])
        turns = sb("turns", [128, 2, 2, D])
        resid = sb("resid", [128, 2, 2, D])
        img_t = sb("img_t", [128, D])
        pst = sb("pst", [128, 2, 6])
        pmv = sb("pmv", [128, 2])
        pneg = sb("pneg", [128, 1])
        prs = sb("prs", [128, 2])
        hst = sb("hst", [128, NT, 6])
        hmv = sb("hmv", [128, NT, 2])
        hrs = sb("hrs", [128, 2, NT])
        h_new = sb("h_new", [128, NT, D])
        x1_new = sb("x1_new", [128, NT, D])
        xT = sb("xT", [KH, 2, CB, L])
        xc = sb("xc", [128, 2, NC, CB, L + KC])
        u = sb("u", [128, 2, NC, T])
        zs = sb("zs", [128, 2, NC, T])
        dt_ = sb("dt_", [128, 2, NC, T])
        dtu = sb("dtu", [128, 2, NC, T])
        stk = sb("stk", [96, 2, T], BF16)
        mid = sb("mid", [96, T], BF16)
        rr = sb("rr", [96, T])
        dtx = sb("dtx", [R, T])
        ea = sb("ea", [128, NC, T])
        lg1 = sb("lg1", [128, NC, T])
        da = sb("da", [128, 2, GN, T])
        ring = sb("ring", [128, NRING, GN, T])
        zero_cols = sb("zero_cols", [128, GN * CB])
        brep = sb("brep", [128, 2, GN, T])
        crep = sb("crep", [128, 2, GN, T])
        yg = sb("yg", [128, 2, NC, T])
        hb = sb("hb", [128, NT, D])
        x1 = sb("x1", [128, NT, D])
        h2 = sb("h2", [128, NT, D])
        x3 = sb("x3", [128, NT, D])
        qst = sb("qst", [128, NT, 6])
        qmv = sb("qmv", [128, NT, 2])
        qrs = sb("qrs", [128, 2, NT])
        x3T = sb("x3T", [KH, 2, T])
        spare = yg[:].rearrange("p d o t -> p (d o t)")[:, 0:SPARES * XW].rearrange("p (q x) -> p q x", q=SPARES)
        bm_in = ring[0:KH, 0, :, :].rearrange("p n t -> p (n t)")[:, 0:2 * 2 * D].rearrange("p (d j k) -> p d j k", d=2, j=2)
        bm_b = ring[0:KH, 0, 3, 0:4].rearrange("p (d j) -> p d j", d=2)
        inT = ring[0:KH, 1, :, :].rearrange("p n t -> p (n t)")[:, 0:2 * 2 * DI].rearrange("p (j o) -> p j o", j=2)
        outw = ring[0:KH, 2, :, :].rearrange("p n t -> p (n t)")[:, 0:2 * DI].rearrange("p (j o) -> p j o", j=2)
        bmoT = ring[0:KH, 3, :, :].rearrange("p n t -> p (n t)")[:, 0:2 * D].rearrange("p (j o) -> p j o", j=2)
        projT = brep[:, 0, :, :].rearrange("p n t -> p (n t)")[:, 0:6 * D].rearrange("p (k o) -> p k o", k=6)
        tgam = crep[:, 0, 0, 0:6]
        tbet = crep[:, 0, 0, 8:14]
        betas = crep[:, 1, :, :].rearrange("p n t -> p (n t)")[:, 0:768].rearrange("p (k m) -> p k m", k=6)
        projb = crep[0:1, 0, 1, 0:D]
        sel1 = da[0:96, 0, 0, 0:2 * NS]

        py = [pb(f"py{i}", [128, 512]) for i in range(NC)]
        prep = pb("prep", [128, 2, 512])
        pf = [pb(f"pf{i}", [128, 512]) for i in range(2)]
        pq = pb("pq", [128, 512])

        w_in = sem("weights_loaded")
        set_pool = sem("setup_pool")
        set_dve = sem("setup_dve")
        set_pe = sem("setup_pe")
        set_act = sem("setup_act")
        patch_in = sem("patches_loaded")
        ids_in = sem("ids_loaded")
        rows_in = sem("rows_gathered")
        rep_ps = sem("rep_in_psum")
        rep_sb = sem("rep_in_sbuf")
        da_ok = sem("decay_ready")
        dbu_ok = sem("dbu_ready")
        scan_ok = sem("scan_done")
        hc_ok = sem("hc_ready")
        y_ok = sem("states_summed")
        y_out = sem("y_evacuated")
        yg_ok = sem("y_gated")
        hb_ok = sem("h_kept")
        x1_ok = sem("x1_kept")
        full = [sem(f"front{i}_filled") for i in range(2)]
        free = [sem(f"front{i}_freed") for i in range(2)]
        qfull = sem("back_filled")
        qfree = sem("back_freed")
        passes = {e: sem(f"passes_{e}") for e in ("SP", "Pool", "DVE")}
        h2_out = sem("h2_stored")
        filled = sem("slots_filled")
        x3_out = sem("x3_stored")
        fv = Steps(sem("front_dve"), "pstat paggr pneg theta turn round res1 res2 res3 clamp img txt1 txt2 txt3 hstat haggr x1")
        fa = Steps(sem("front_act"), "lnp rsp sin lin lnh rsh")
        dv = Steps(sem("dir_dve"), "conv0 conv1 conv2 conv3 split2 split3 w1 r m dt dtu")
        da_s = Steps(sem("dir_act"), "silu exp ln")
        qv = Steps(sem("back_dve"), "stat aggr norm gain h2 stat3 aggr3 x3")
        qa = Steps(sem("back_act"), "ln rs ln3 rs3")

        FJOBS = [("img", 1), ("xT0", 1), ("xT1", 1)]
        for d in range(2):
            FJOBS += [(f"xz{d}_{o}", 1) for o in range(2 * NC)]
            FJOBS += [(f"bc{d}", 2), (f"dtx{d}", 1)] + [(f"dt{d}_{o}", 2) for o in range(NC)]
        JOB = {}
        nfull, nfree = [0, 0], [0, 0]
        for i, (name, readers) in enumerate(FJOBS):
            b = i % 2
            JOB[name] = (b, nfull[b], nfree[b])
            nfull[b] += 1
            nfree[b] += readers

        def job_start(pe, name, c):
            b, _, fr = JOB[name]
            wait(pe, free[b], nfree[b] * c + fr)
            return pf[b]

        def job_wait(eng, name, c):
            b, fu, _ = JOB[name]
            eng.wait_ge(full[b], nfull[b] * c + fu + 1)
            return pf[b]

        def job_read(eng, name, c):
            b, _, fr = JOB[name]
            eng.wait_ge(free[b], nfree[b] * c + fr + dict(FJOBS)[name])

        def jsem(name, which):
            return (full if which == "full" else free)[JOB[name][0]]

        QJ = NT + 2 + 1

        def alone(eng):
            eng.sem_inc(passes[eng.engine.name], 1)

        def sp_front(sp, c):
            if not isinstance(c, int) or c > 0:
                wait(sp, fv.sem, fv.after("txt3", c - 1))
                alone(sp)
                wait(sp, free[0], nfree[0] * (c - 1) + 1)
                alone(sp)
                wait(sp, rows_in, 64 * c)
                alone(sp)
            sp.dma_start(ids[:], a["ids"][bass.ds(c, 1)].rearrange("a p k -> p (a k)")).then_inc(ids_in, 16)
            sp.dma_start(taus[:], a["taus"][bass.ds(c, 1)].rearrange("a p k -> p (a k)")).then_inc(ids_in, 16)
            sp.dma_start(ptok[:], a["p_tok"][bass.ds(c, 1)].rearrange("a p k -> p (a k)")).then_inc(patch_in, 16)
            sp.dma_start(pT[:].rearrange("p k t -> p (k t)"), a["p_T"][bass.ds(c, 1)].rearrange("a p k -> p (a k)")).then_inc(patch_in, 16)

        def pool_front(gp, c):
            gp.wait_ge(ids_in, 32 * c + 32)
            wait(gp, fv.sem, fv.after("txt3", c - 1))
            alone(gp)
            for t in range(2):
                gp.indirect_dma_start(tok_rows[:, t, :], None, a["tok_emb"], bass.IndirectOffsetOnAxis(ap=ids[:, t:t + 1], axis=0)).then_inc(rows_in, 16)
                gp.indirect_dma_start(seg_rows[:, t, :], None, a["seg_emb"], bass.IndirectOffsetOnAxis(ap=ids[:, 2 + t:3 + t], axis=0)).then_inc(rows_in, 16)

        def pool_keep(gp, c):
            gp.wait_ge(fv.sem, fv.after("x1", c))
            wait(gp, qv.sem, qv.after("h2", c - 1))
            gp.tensor_tensor(hb[:], h_new[:], ln_b[:].unsqueeze(1).to_broadcast([128, NT, D]), ALU.add).then_inc(hb_ok, 1)

        def act_keep(act, c):
            act.wait_ge(fv.sem, fv.after("x1", c))
            wait(act, qfree, QJ * (c - 1) + NT)
            act.activation(x1[:], x1_new[:], ACT.Copy).then_inc(x1_ok, 1)

        def pe_front(pe, c):
            pe.wait_ge(patch_in, 32 * c + 32)
            p = job_start(pe, "img", c)
            for k in range(PD // 128):
                mm = pe.matmul(p[:, 0:D], pT[:, k, :], gw[:, k, :], start=(k == 0), stop=(k == PD // 128 - 1))
            mm.then_inc(jsem("img", "full"), 1)

        def dve_front1(v, c):
            v.wait_ge(patch_in, 32 * c + 32)
            wait(v, fv.sem, fv.after("paggr", c - 1))
            for i in range(2):
                o = v.bn_stats(pst[:, i, :], ptok[:, 384 * i:384 * i + 384])
            o.then_inc(fv.sem, 1)
            v.wait_ge(fv.sem, fv.after("pstat", c))
            wait(v, fa.sem, fa.after("lnp", c - 1))
            alone(v)
            v.bn_aggr(pmv[:], pst[:].rearrange("p a k -> p (a k)")).then_inc(fv.sem, 1)
            v.wait_ge(fv.sem, fv.after("paggr", c))
            v.tensor_scalar(pneg[:], pmv[:, 0:1], -1.0, None, ALU.mult).then_inc(fv.sem, 1)
            v.wait_ge(ids_in, 32 * c + 32)
            wait(v, fa.sem, fa.after("lin", c - 1))
            for s in range(2):
                for t in range(2):
                    o = v.scalar_tensor_tensor(theta[:, s, t, :], w_tau[:, s, :], taus[:, 2 * s + t:2 * s + t + 1], b_tau[:, s, :], ALU.mult, ALU.add)
            o.then_inc(fv.sem, 1)
            v.wait_ge(fv.sem, fv.after("theta", c))
            for s in range(2):
                o = v.tensor_scalar(turns[:, s], theta[:, s], 1.0 / TWO_PI, 0.25 if s == 0 else 0.0, ALU.mult, ALU.add)
            o.then_inc(fv.sem, 1)
            v.wait_ge(fv.sem, fv.after("turn", c))
            v.tensor_scalar(turns[:], turns[:], MAGIC, -MAGIC, ALU.add, ALU.add).then_inc(fv.sem, 1)
            v.wait_ge(fv.sem, fv.after("round", c))
            wait(v, fv.sem, fv.after("txt2", c - 1))
            v.scalar_tensor_tensor(fl(resid), fl(turns), -C1, fl(theta), ALU.mult, ALU.add).then_inc(fv.sem, 1)
            v.wait_ge(fv.sem, fv.after("res1", c))
            v.scalar_tensor_tensor(fl(resid), fl(turns), -C2, fl(resid), ALU.mult, ALU.add).then_inc(fv.sem, 1)
            v.wait_ge(fv.sem, fv.after("res2", c))
            v.scalar_tensor_tensor(fl(resid), fl(turns), -C3, fl(resid), ALU.mult, ALU.add).then_inc(fv.sem, 1)
            v.wait_ge(fv.sem, fv.after("res3", c))
            for s in range(2):
                sh = math.pi / 2 if s == 0 else 0.0
                o = v.tensor_scalar(resid[:, s], resid[:, s], PI_IN - sh, -PI_IN - sh, ALU.min, ALU.max)
            o.then_inc(fv.sem, 1)

        def fl(t):
            return t[:].rearrange("p a b c -> p (a b c)")

        def act_front1(act, c):
            act.wait_ge(fv.sem, fv.after("paggr", c))
            wait(act, fv.sem, fv.after("img", c - 1))
            act.activation(prs[:, 0:1], pmv[:, 1:2], ACT.Ln, bias=eps[:]).then_inc(fa.sem, 1)
            act.wait_ge(fa.sem, fa.after("lnp", c))
            act.activation(prs[:, 1:2], prs[:, 0:1], ACT.Exp, scale=-0.5).then_inc(fa.sem, 1)
            act.wait_ge(fv.sem, fv.after("clamp", c))
            for s in range(2):
                o = act.activation(resid[:, s, :, 0:D - 1], resid[:, s, :, 0:D - 1], ACT.Sin, bias=halfpi[:] if s == 0 else 0.0)
            o.then_inc(fa.sem, 1)
            act.activation(resid[:, :, :, D - 1:D], theta[:, :, :, D - 1:D], ACT.Copy).then_inc(fa.sem, 1)

        def dve_front2(v, c):
            job_wait(v, "img", c)
            wait(v, fv.sem, fv.after("img", c - 1))
            v.wait_ge(fv.sem, fv.after("pneg", c))
            v.scalar_tensor_tensor(img_t[:], proj_sum[:], pneg[:], pf[JOB["img"][0]][:, 0:D], ALU.mult, ALU.add).then_inc(jsem("img", "free"), 1)
            job_read(v, "img", c)
            v.wait_ge(fa.sem, fa.after("rsp", c))
            wait(v, fv.sem, fv.after("x1", c - 1))
            wait(v, hb_ok, c)
            v.scalar_tensor_tensor(h_new[:, 0, :], img_t[:], prs[:, 1:2], proj_bias[:], ALU.mult, ALU.add).then_inc(fv.sem, 1)
            v.wait_ge(fa.sem, fa.after("lin", c))
            v.wait_ge(rows_in, 64 * c + 64)
            for t in range(2):
                o = v.scalar_tensor_tensor(h_new[:, 1 + t, :], resid[:, 0, t, :], am[:, 0:1], tok_rows[:, t, :], ALU.mult, ALU.add)
            o.then_inc(fv.sem, 1)
            v.wait_ge(fv.sem, fv.after("txt1", c))
            for t in range(2):
                o = v.scalar_tensor_tensor(h_new[:, 1 + t, :], resid[:, 1, t, :], am[:, 1:2], h_new[:, 1 + t, :], ALU.mult, ALU.add)
            o.then_inc(fv.sem, 1)
            v.wait_ge(fv.sem, fv.after("txt2", c))
            for t in range(2):
                o = v.scalar_tensor_tensor(h_new[:, 1 + t, :], seg_rows[:, t, :], alpha[:, 2:3], h_new[:, 1 + t, :], ALU.mult, ALU.add)
            o.then_inc(fv.sem, 1)
            v.wait_ge(fv.sem, fv.after("txt3", c))
            for t in range(NT):
                o = v.bn_stats(hst[:, t, :], h_new[:, t, :])
            o.then_inc(fv.sem, 1)
            v.wait_ge(fv.sem, fv.after("hstat", c))
            wait(v, fa.sem, fa.after("lnh", c - 1))
            wait(v, fv.sem, fv.after("x1", c - 1))
            alone(v)
            for t in range(NT):
                o = v.bn_aggr(hmv[:, t, :], hst[:, t, :])
            o.then_inc(fv.sem, 1)

        def act_front2(act, c):
            act.wait_ge(fv.sem, fv.after("haggr", c))
            act.activation(hrs[:, 0, :], hmv[:, :, 1], ACT.Ln, bias=eps[:]).then_inc(fa.sem, 1)
            act.wait_ge(fa.sem, fa.after("lnh", c))
            act.activation(hrs[:, 1, :], hrs[:, 0, :], ACT.Exp, scale=-0.5).then_inc(fa.sem, 1)

        def dve_front3(v, c):
            v.wait_ge(fa.sem, fa.after("rsh", c))
            v.wait_ge(fv.sem, fv.after("haggr", c))
            wait(v, x1_ok, c)
            if not isinstance(c, int) or c > 0:
                wait(v, full[JOB["xT1"][0]], nfull[JOB["xT1"][0]] * (c - 1) + JOB["xT1"][1] + 1)
            for t in range(NT):
                o = v.tensor_scalar(x1_new[:, t, :], h_new[:, t, :], hmv[:, t, 0:1], hrs[:, 1, t:t + 1], ALU.subtract, ALU.mult)
            o.then_inc(fv.sem, 1)

        def pe_front2(pe, c):
            pe.wait_ge(fv.sem, fv.after("x1", c))
            for k in range(2):
                p = job_start(pe, f"xT{k}", c)
                for t in range(NT):
                    mm = pe.transpose(p[0:KH, 128 * t:128 * t + 128], x1_new[:, t, k * KH:(k + 1) * KH], ident[:])
                mm.then_inc(jsem(f"xT{k}", "full"), 1)

        def act_front3(act, c):
            if not isinstance(c, int) or c > 0:
                wait(act, full[JOB[f"xz1_{2 * NC - 1}"][0]], nfull[JOB[f"xz1_{2 * NC - 1}"][0]] * (c - 1) + JOB[f"xz1_{2 * NC - 1}"][1] + 1)
                wait(act, full[JOB[f"xz1_{2 * NC - 2}"][0]], nfull[JOB[f"xz1_{2 * NC - 2}"][0]] * (c - 1) + JOB[f"xz1_{2 * NC - 2}"][1] + 1)
            for k in range(2):
                p = job_wait(act, f"xT{k}", c)
                act.activation(xT[:, k, :, 0:LI], p[0:KH, 0:128].rearrange("p (b l) -> p b l", b=CB), ACT.Copy)
                o = act.activation(xT[:, k, :, LI:L], p[0:KH, 128:T].rearrange("p (b l) -> p b l", b=CB), ACT.Copy)
                o.then_inc(jsem(f"xT{k}", "free"), 1)

        def pe_dir1(pe, c, d):
            job_read(pe, "xT1", c)
            for o in range(2 * NC):
                p = job_start(pe, f"xz{d}_{o}", c)
                for k in range(2):
                    mm = pe.matmul(p[:, 0:T], wxz[:, d, k, 128 * o:128 * o + 128], xT[:, k].rearrange("p b l -> p (b l)"), start=(k == 0), stop=(k == 1))
                mm.then_inc(jsem(f"xz{d}_{o}", "full"), 1)

        def act_dir1(act, c, d):
            e = 2 * c + d
            wait(act, dv.sem, dv.after("conv3", e - 2))
            wait(act, yg_ok, e - 1)
            for o in range(2 * NC):
                p = job_wait(act, f"xz{d}_{o}", c)
                if o < NC:
                    base = KC if d == 0 else 0
                    out = xc[:, d, o, :, base:base + L]
                    op = act.activation(out, p[:, 0:T].rearrange("p (b l) -> p b l", b=CB), ACT.Identity, bias=bxz[:, d, o:o + 1])
                else:
                    op = act.activation(zs[:, d, o - NC, :], p[:, 0:T], ACT.Identity, bias=bxz[:, d, o:o + 1])
                op.then_inc(jsem(f"xz{d}_{o}", "free"), 1)

        def dve_dir1(v, c, d):
            e = 2 * c + d
            job_read(v, f"xz{d}_{2 * NC - 1}", c)
            wait(v, yg_ok, e - 1)
            wait(v, dv.sem, dv.after("dtu", e - 2))
            for k in range(KC + 1):
                if k:
                    v.wait_ge(dv.sem, dv.after(f"conv{k - 1}", e))
                for o in range(NC):
                    at = k if d == 0 else KC - k
                    x = xc[:, d, o, :, at:at + L]
                    uo = u[:, d, o, :].rearrange("p (b l) -> p b l", b=CB)
                    if k == 0:
                        op = v.tensor_scalar(uo, x, cw[:, o, 0:1], cb[:, o:o + 1], ALU.mult, ALU.add)
                    else:
                        op = v.scalar_tensor_tensor(uo, x, cw[:, o, k:k + 1], uo, ALU.mult, ALU.add)
                op.then_inc(dv.sem, 1)

        def act_dir2(act, c, d):
            e = 2 * c + d
            act.wait_ge(dv.sem, dv.after("conv3", e))
            job_read(act, f"xz{d}_{2 * NC - 1}", c)
            act.activation(u[:, d], u[:, d], ACT.Silu)
            act.activation(zs[:, d], zs[:, d], ACT.Silu).then_inc(da_s.sem, 1)

        def pe_dir2(pe, c, d):
            e = 2 * c + d
            pe.wait_ge(da_s.sem, da_s.after("silu", e))
            p = job_start(pe, f"bc{d}", c)
            for i in range(NC):
                mm = pe.matmul(p[0:96, 0:T], xpw_bc[:, i, :], u[:, d, i, :], start=(i == 0), stop=(i == NC - 1))
            mm.then_inc(jsem(f"bc{d}", "full"), 1)
            p = job_start(pe, f"dtx{d}", c)
            for i in range(NC):
                mm = pe.matmul(p[0:R, 0:T], xpw_dt[:, i, :], u[:, d, i, :], start=(i == 0), stop=(i == NC - 1))
            mm.then_inc(jsem(f"dtx{d}", "full"), 1)

        def act_dir3(act, c, d):
            e = 2 * c + d
            p = job_wait(act, f"bc{d}", c)
            wait(act, rep_ps, 4 * NG * (e - 1))
            act.activation(stk[:, d, :], p[0:96, 0:T], ACT.Copy).then_inc(jsem(f"bc{d}", "free"), 1)
            p = job_wait(act, f"dtx{d}", c)
            act.activation(dtx[:], p[0:R, 0:T], ACT.Copy).then_inc(jsem(f"dtx{d}", "free"), 1)

        def dve_dir2(v, c, d):
            e = 2 * c + d
            p = job_wait(v, f"bc{d}", c)
            b, _, fr = JOB[f"bc{d}"]
            v.wait_ge(free[b], nfree[b] * c + fr + 1)
            wait(v, dv.sem, dv.after("split3", e - 1))
            v.tensor_tensor(rr[:], p[0:96, 0:T], stk[:, d, :], ALU.subtract).then_inc(jsem(f"bc{d}", "free"), 1)
            job_read(v, f"bc{d}", c)
            v.tensor_copy(mid[64:96, :], rr[64:96, :])
            v.tensor_copy(stk[32:64, d, :], rr[32:64, :]).then_inc(dv.sem, 1)
            v.wait_ge(dv.sem, dv.after("split2", e))
            v.tensor_tensor(stk[64:96, d, :], rr[64:96, :], mid[64:96, :], ALU.subtract).then_inc(dv.sem, 1)

        def pe_dir3(pe, c, d):
            e = 2 * c + d
            job_read(pe, f"dtx{d}", c)
            for o in range(NC):
                p = job_start(pe, f"dt{d}_{o}", c)
                pe.matmul(p[:, 0:T], dtw[:, 128 * o:128 * o + 128], dtx[:], start=True, stop=True).then_inc(jsem(f"dt{d}_{o}", "full"), 1)

        def act_dir4(act, c, d):
            e = 2 * c + d
            wait(act, dv.sem, dv.after("r", e - 1))
            for o in range(NC):
                p = job_wait(act, f"dt{d}_{o}", c)
                act.activation(ea[:, o, :], p[:, 0:T], ACT.Abs, bias=dtb[:, o:o + 1]).then_inc(jsem(f"dt{d}_{o}", "free"), 1)
            job_read(act, f"dt{d}_{NC - 2}", c)
            job_read(act, f"dt{d}_{NC - 1}", c)
            act.activation(ea[:], ea[:], ACT.Exp, scale=-1.0).then_inc(da_s.sem, 1)
            act.wait_ge(da_s.sem, da_s.after("exp", e))
            wait(act, dv.sem, dv.after("m", e - 1))
            act.activation(lg1[:], ea[:], ACT.Ln, bias=1.0).then_inc(da_s.sem, 1)

        def dve_dir3a(v, c, d):
            e = 2 * c + d
            wait(v, da_ok, UD * (e - 1))
            for o in range(NC):
                p = job_wait(v, f"dt{d}_{o}", c)
                b, _, fr = JOB[f"dt{d}_{o}"]
                v.wait_ge(free[b], nfree[b] * c + fr + 1)
                op = v.tensor_scalar(dt_[:, d, o, :], p[:, 0:T], dtb[:, o:o + 1], 0.0, ALU.add, ALU.max)
                op.then_inc(jsem(f"dt{d}_{o}", "free"), 1)

        def dve_dir3(v, c, d):
            e = 2 * c + d
            v.wait_ge(da_s.sem, da_s.after("exp", e))
            wait(v, dbu_ok, UD * (e - 1))
            v.tensor_scalar(dtu[:, d], ea[:], 1.0, -1.0, ALU.add, ALU.add).then_inc(dv.sem, 1)
            v.wait_ge(dv.sem, dv.after("w1", e))
            v.wait_ge(da_s.sem, da_s.after("ln", e))
            v.tensor_tensor(ea[:], ea[:], dtu[:, d], ALU.subtract).then_inc(dv.sem, 1)
            job_read(v, f"dt{d}_{NC - 2}", c)
            job_read(v, f"dt{d}_{NC - 1}", c)
            v.tensor_tensor(dt_[:, d], dt_[:, d], lg1[:], ALU.add).then_inc(dv.sem, 1)
            v.wait_ge(dv.sem, dv.after("m", e))
            v.tensor_tensor(dt_[:, d], dt_[:, d], ea[:], ALU.add).then_inc(dv.sem, 1)
            v.wait_ge(dv.sem, dv.after("dt", e))
            v.tensor_tensor(dtu[:, d], dt_[:, d], u[:, d], ALU.mult).then_inc(dv.sem, 1)

        def pe_rep(pe, c, g):
            d, ng = g // NG, g % NG
            G = 2 * NG * c + g
            e = 2 * c + d
            pe.wait_ge(dv.sem, dv.after("split3", e))
            for bc in range(2):
                for pair in range(2):
                    q = 4 * G + 2 * bc + pair
                    wait(pe, rep_sb, q)
                    for i in range(2):
                        j = bc * NS + ng * GN + 2 * pair + i
                        mm = pe.matmul(prep[:, i, 0:T], sel[:, j, :], stk[:, d, :], start=True, stop=True)
                    mm.then_inc(rep_ps, 1)

        def act_rep(act, c, g):
            G = 2 * NG * c + g
            for bc in range(2):
                wait(act, dbu_ok if bc == 0 else hc_ok, NC * (G - 1))
                for pair in range(2):
                    q = 4 * G + 2 * bc + pair
                    act.wait_ge(rep_ps, q + 1)
                    dst = (brep if bc == 0 else crep)[:, g % 2, 2 * pair:2 * pair + 2, :]
                    act.activation(dst, prep[:, :, 0:T], ACT.Copy).then_inc(rep_sb, 1)

        def unit(w):
            d, r = divmod(w, UD)
            ng, o = divmod(r, NC)
            return d, ng, o, d * NG + ng

        def act_unit(act, c, w):
            d, ng, o, g = unit(w)
            U = U2 * c + w
            act.wait_ge(dv.sem, dv.after("dt", 2 * c + d))
            wait(act, scan_ok, U - 1)
            lo = 1 if d == 0 else 0
            if w % UD < 2:
                start = da[:, w % 2].rearrange("p n (b l) -> p (n b) l", b=CB)[:, :, (L - 1) * d:(L - 1) * d + 1]
                act.activation(start, zero_cols[:].unsqueeze(2), ACT.Copy)
            src = dt_[:, d, o, :].rearrange("p (b l) -> p b l", b=CB)[:, :, lo:lo + L - 1]
            for i in range(GN):
                n = ng * GN + i
                dst = da[:, w % 2, i, :].rearrange("p (b l) -> p b l", b=CB)[:, :, lo:lo + L - 1]
                op = act.activation(dst, src, ACT.Exp, scale=aneg[:, o, n:n + 1])
            op.then_inc(da_ok, 1)

        def pool_unit(gp, c, w):
            d, ng, o, g = unit(w)
            U, G = U2 * c + w, 2 * NG * c + g
            gp.wait_ge(dv.sem, dv.after("dtu", 2 * c + d))
            gp.wait_ge(rep_sb, 4 * G + 2)
            wait(gp, y_ok, U + 1 - NRING)
            gp.tensor_tensor(ring[:, w % NRING], dtu[:, d, o, :].unsqueeze(1).to_broadcast([128, GN, T]), brep[:, g % 2], ALU.mult).then_inc(dbu_ok, 1)

        def dve_scan(v, c, w):
            d, ng, o, g = unit(w)
            U = U2 * c + w
            v.wait_ge(da_ok, U + 1)
            v.wait_ge(dbu_ok, U + 1)
            x0 = da[:, w % 2].rearrange("p n t -> p (n t)")
            h = ring[:, w % NRING].rearrange("p n t -> p (n t)")
            if d == 1:
                x0, h = x0[:, ::-1], h[:, ::-1]
            v.tensor_tensor_scan(h, x0, h, 0.0, ALU.mult, ALU.add).then_inc(scan_ok, 1)

        def dve_hc(v, c, w):
            d, ng, o, g = unit(w)
            U, G = U2 * c + w, 2 * NG * c + g
            v.wait_ge(scan_ok, U + 1)
            v.wait_ge(rep_sb, 4 * G + 4)
            v.tensor_tensor(ring[:, w % NRING], ring[:, w % NRING], crep[:, g % 2], ALU.mult).then_inc(hc_ok, 1)

        def pe_unit(pe, c, w):
            d, ng, o, g = unit(w)
            U = U2 * c + w
            pe.wait_ge(hc_ok, U + 1)
            if ng == 0:
                wait(pe, y_out, NC * (2 * c + d - 1) + o + 1)
            for i in range(GN):
                mm = pe.matmul(py[o][:, 0:T], ident[:], ring[:, w % NRING, i, :], start=(ng == 0 and i == 0), stop=(ng == NG - 1 and i == GN - 1))
            mm.then_inc(y_ok, 1)

        def dve_gate(v, c, d):
            e = 2 * c + d
            for o in range(NC):
                v.wait_ge(y_ok, U2 * c + UD * d + UD - NC + o + 1)
                v.scalar_tensor_tensor(u[:, d, o, :], u[:, d, o, :], dskip[:, o:o + 1], py[o][:, 0:T], ALU.mult, ALU.add).then_inc(y_out, 1)
            v.wait_ge(y_out, NC * (e + 1))
            wait(v, qfull, QJ * (c - 1) + NT)
            v.wait_ge(filled, 16 * SPARES)
            for lo, hi in ((0, LI), (LI, L)):
                yv, zv = (x[:, d].rearrange("p o (b l) -> p o b l", b=CB)[:, :, :, lo:hi] for x in (u, zs))
                ov = yg[:, d, :, CB * lo:CB * hi].rearrange("p o (b l) -> p o b l", b=CB)
                op = v.tensor_tensor(ov, yv, zv, ALU.mult)
            op.then_inc(yg_ok, 1)

        def pe_back1(pe, c):
            pe.wait_ge(yg_ok, 2 * c + 2)
            for t in range(NT):
                wait(pe, qfree, QJ * c + t)
                first = True
                for d in range(2):
                    for i in range(NC):
                        pe.matmul(pq[:, 0:D], yg[:, d, i, 128 * t:128 * t + 128], w2t[:, i, :], start=first, stop=False)
                        first = False
                pe.matmul(pq[:, 0:D], ones[0:1, :], outb[:], start=False, stop=True).then_inc(qfull, 1)

        def dve_back1(v, c):
            v.wait_ge(x1_ok, c + 1)
            wait(v, h2_out, 16 * c)
            for t in range(NT):
                v.wait_ge(qfull, QJ * c + t + 1)
                v.tensor_tensor(h2[:, t, :], pq[:, 0:D], x1[:, t, :], ALU.add).then_inc(qfree, 1)
            v.wait_ge(qfree, QJ * c + NT)
            for t in range(NT):
                o = v.bn_stats(qst[:, t, :], h2[:, t, :])
            o.then_inc(qv.sem, 1)
            v.wait_ge(qv.sem, qv.after("stat", c))
            alone(v)
            for t in range(NT):
                o = v.bn_aggr(qmv[:, t, :], qst[:, t, :])
            o.then_inc(qv.sem, 1)

        def act_back1(act, c):
            act.wait_ge(qv.sem, qv.after("aggr", c))
            act.activation(qrs[:, 0, :], qmv[:, :, 1], ACT.Ln, bias=eps[:]).then_inc(qa.sem, 1)
            act.wait_ge(qa.sem, qa.after("ln", c))
            act.activation(qrs[:, 1, :], qrs[:, 0, :], ACT.Exp, scale=-0.5).then_inc(qa.sem, 1)

        def dve_back2(v, c):
            v.wait_ge(qa.sem, qa.after("rs", c))
            for t in range(NT):
                o = v.tensor_scalar(h2[:, t, :], h2[:, t, :], qmv[:, t, 0:1], qrs[:, 1, t:t + 1], ALU.subtract, ALU.mult)
            o.then_inc(qv.sem, 1)
            v.wait_ge(qv.sem, qv.after("norm", c))
            v.tensor_tensor(h2[:], h2[:], ln_g[:].unsqueeze(1).to_broadcast([128, NT, D]), ALU.mult).then_inc(qv.sem, 1)
            v.wait_ge(qv.sem, qv.after("gain", c))
            v.wait_ge(hb_ok, c + 1)
            v.tensor_tensor(h2[:], h2[:], hb[:], ALU.add).then_inc(qv.sem, 1)
            v.wait_ge(qv.sem, qv.after("h2", c))
            for t in range(NT):
                o = v.bn_stats(qst[:, t, :], h2[:, t, :])
            o.then_inc(qv.sem, 1)
            v.wait_ge(qv.sem, qv.after("stat3", c))
            alone(v)
            for t in range(NT):
                o = v.bn_aggr(qmv[:, t, :], qst[:, t, :])
            o.then_inc(qv.sem, 1)

        def act_back2(act, c):
            act.wait_ge(qv.sem, qv.after("aggr3", c))
            act.activation(qrs[:, 0, :], qmv[:, :, 1], ACT.Ln, bias=eps[:]).then_inc(qa.sem, 1)
            act.wait_ge(qa.sem, qa.after("ln3", c))
            act.activation(qrs[:, 1, :], qrs[:, 0, :], ACT.Exp, scale=-0.5).then_inc(qa.sem, 1)

        def dve_back3(v, c):
            v.wait_ge(qa.sem, qa.after("rs3", c))
            wait(v, x3_out, 16 * c)
            wait(v, qfull, QJ * (c - 1) + NT + 2)
            for t in range(NT):
                o = v.tensor_scalar(x3[:, t, :], h2[:, t, :], qmv[:, t, 0:1], qrs[:, 1, t:t + 1], ALU.subtract, ALU.mult)
            o.then_inc(qv.sem, 1)

        def sp_back(sp, c):
            sp.wait_ge(qv.sem, qv.after("h2", c))
            alone(sp)
            sp.dma_start(dram["h2"][bass.ds(c, 1)].rearrange("a p k -> p (a k)"), h2[:].rearrange("p t k -> p (t k)")).then_inc(h2_out, 16)
            sp.wait_ge(qv.sem, qv.after("x3", c))
            alone(sp)
            sp.dma_start(dram["x3"][bass.ds(c, 1)].rearrange("a p k -> p (a k)"), x3[:].rearrange("p t k -> p (t k)")).then_inc(x3_out, 16)

        def pe_back2(pe, c):
            pe.wait_ge(qv.sem, qv.after("x3", c))
            for k in range(2):
                wait(pe, qfree, QJ * c + NT + k)
                for t in range(NT):
                    mm = pe.transpose(pq[0:KH, 128 * t:128 * t + 128], x3[:, t, k * KH:(k + 1) * KH], ident[:])
                mm.then_inc(qfull, 1)

        def act_back3(act, c):
            for k in range(2):
                act.wait_ge(qfull, QJ * c + NT + k + 1)
                if k == 0:
                    wait(act, qfull, QJ * c)
                act.activation(x3T[:, k, :], pq[0:KH, 0:T], ACT.Copy).then_inc(qfree, 1)

        def pe_back3(pe, c):
            wait(pe, qfree, QJ * c + NT + 2)
            for t in range(NT):
                for k in range(2):
                    mm = pe.matmul(pq[:, E * t:E * t + E], x3T[:, k, 128 * t:128 * t + 128], rw[:, k, :], start=(k == 0), stop=(k == 1))
            mm.then_inc(qfull, 1)

        def dve_back4(v, c):
            v.wait_ge(qfull, QJ * c + QJ)
            v.tensor_copy(logits[:, bass.ds(NT * c, NT), :].rearrange("p t e -> p (t e)"), pq[:, 0:NT * E]).then_inc(qfree, 1)


        block = ctx.enter_context(nc.Block())
        loads = [
            (bm_in.rearrange("p d j k -> p (d j k)"), a["bm_in"]), (bm_b.rearrange("p d j -> p (d j)"), a["bm_b"]),
            (inT.rearrange("p j o -> p (j o)"), a["inT"]), (outw.rearrange("p j o -> p (j o)"), a["outw"]),
            (bmoT.rearrange("p j o -> p (j o)"), a["bmoT"]), (projT.rearrange("p k o -> p (k o)"), a["projT"]),
            (tgam, a["tgam"]), (tbet, a["tbet"]), (projb, a["projb"]),
            (xpw_bc[:, :, 0:2 * NS], a["xpw_bc"]), (xpw_bc[:, :, 2 * NS:4 * NS], a["xpw_bc"]), (xpw_bc[:, :, 4 * NS:6 * NS], a["xpw_bc"]),
            (xpw_dt[:], a["xpw_dt"]), (dtw[:], a["dtw"]), (dtb[:], a["dtb"]),
            (cw[:].rearrange("p o k -> p (o k)"), a["cw"]), (cb[:], a["cb"]), (dskip[:], a["dskip"]),
            (aneg[:].rearrange("p o n -> p (o n)"), a["a_log"]),
            (w_tau[:].rearrange("p s k -> p (s k)"), a["w_tau"].partition_broadcast(128)),
            (b_tau[:].rearrange("p s k -> p (s k)"), a["b_tau"].partition_broadcast(128)),
            (alpha[:], a["alpha"].partition_broadcast(128)),
            (outb[:], a["outb"]), (ln_g[:], a["ln_g"].partition_broadcast(128)), (ln_b[:], a["ln_b"].partition_broadcast(128)),
            (rw[:].rearrange("p k e -> p (k e)"), a["rw"]),
        ]
        LOADED = 16 * len(loads)
        banks = [py[0], py[1], py[2], prep[:, 0, :], prep[:, 1, :], pf[0], pf[1], pq]

        def sp_setup(sp):
            for dst, src in loads:
                if len(dst.shape) == 2 and len(src.shape) == 3:
                    src = src.rearrange("p a k -> p (a k)")
                sp.dma_start(dst, src).then_inc(w_in, 16)

        def pool_setup(gp):
            gp.memset(ones[:], 1.0)
            gp.memset(ident[:], 0.0).then_inc(set_pool, 1)
            gp.memset(spare, 0.0)
            gp.iota(spare_i[:], pattern=[[128, SPARES]], base=2 * NTOK, channel_multiplier=1).then_inc(set_pool, 1)
            gp.wait_ge(set_pool, 2)
            gp.tensor_copy(spare[:, :, D:D + 1], spare_i[:].unsqueeze(2))
            gp.affine_select(out=ident[:], in_=ident[:], compare_op=ALU.not_equal, fill=1.0, base=0, pattern=[[-1, 128]], channel_multiplier=1).then_inc(set_pool, 1)

        def dve_setup(v):
            v.memset(xc[:].rearrange("p d o b l -> p (d o b l)"), 0.0)
            v.memset(zero_cols[:], 0.0)
            v.memset(eps[:], EPS)
            v.memset(halfpi[:], math.pi / 2)
            v.memset(mask[:], 1.0).then_inc(set_dve, 1)
            v.wait_ge(set_dve, 1)
            for q in range(4):
                o = v.memset(mask[LT * q:LT * q + 5, :], 0.0)
            o.then_inc(set_dve, 1)
            v.wait_ge(set_dve, 2)
            v.wait_ge(w_in, LOADED)
            v.tensor_scalar(am[:], alpha[:, 0:2], mask[:], None, ALU.mult)
            v.wait_ge(set_pool, 3)
            for k in range(PD // 128):
                v.tensor_scalar(gw[:, k, :], projT[:, k, :], tgam[:, k:k + 1], None, ALU.mult)
                v.tensor_scalar(betas[:, k, :], ones[:], tbet[:, k:k + 1], None, ALU.mult)
            v.tensor_tensor(sel1, ident[0:96, 0:32], ident[0:96, 32:64], ALU.add).then_inc(set_dve, 1)
            v.wait_ge(set_dve, 3)
            v.tensor_tensor(sel1, sel1, ident[0:96, 64:96], ALU.add).then_inc(set_dve, 1)
            v.wait_ge(set_dve, 4)
            v.tensor_copy(sel[:], sel1.unsqueeze(2).to_broadcast([96, 2 * NS, 128])).then_inc(set_dve, 1)
            v.wait_ge(set_act, 1)
            v.tensor_scalar(aneg[:], aneg[:], -1.0, None, ALU.mult).then_inc(set_dve, 1)

        def pe_setup(pe):
            pe.wait_ge(w_in, LOADED)
            pe.wait_ge(set_dve, 5)
            i = 0
            for d in range(2):
                for k in range(2):
                    for h in range(2):
                        for j in range(2):
                            mm = pe.matmul(banks[i][0:KH, 0:DI], bm_in[:, d, j, KH * k:KH * k + KH], inT[:, j, DI * h:DI * h + DI], start=(j == 0), stop=(j == 1))
                        mm.then_inc(set_pe, 1)
                        i += 1
            pe.wait_ge(set_act, 9)
            for i in range(NC):
                for j in range(2):
                    pe.matmul(py[i][:, 0:D], outw[:, j, 128 * i:128 * i + 128], bmoT[:, j, :], start=(j == 0), stop=(j == 1))
            for d in range(2):
                for o in range(2 * NC):
                    for j in range(2):
                        pe.matmul(pf[0][:, 2 * NC * d + o:2 * NC * d + o + 1], inT[:, j, 128 * o:128 * o + 128], bm_b[:, d, j:j + 1], start=(j == 0), stop=(j == 1))
            for k in range(PD // 128):
                pe.matmul(pf[1][:, 0:D], ones[:], gw[:, k, :], start=(k == 0), stop=(k == PD // 128 - 1))
            for k in range(PD // 128):
                pe.matmul(pq[:, 0:D], betas[:, k, :], projT[:, k, :], start=(k == 0), stop=False)
            pe.matmul(pq[:, 0:D], ones[0:1, :], projb, start=False, stop=True).then_inc(set_pe, 1)

        def act_setup(act):
            act.wait_ge(w_in, LOADED)
            act.activation(aneg[:], aneg[:], ACT.Exp).then_inc(set_act, 1)
            i = 0
            for d in range(2):
                for k in range(2):
                    for h in range(2):
                        act.wait_ge(set_pe, i + 1)
                        act.activation(wxz[:, d, k, DI * h:DI * h + DI], banks[i][0:KH, 0:DI], ACT.Copy).then_inc(set_act, 1)
                        i += 1
            act.wait_ge(set_pe, 9)
            for i in range(NC):
                act.activation(w2t[:, i, :], py[i][:, 0:D], ACT.Copy)
            act.activation(bxz[:].rearrange("p d o -> p (d o)"), pf[0][:, 0:4 * NC], ACT.Copy)
            act.activation(proj_sum[:], pf[1][:, 0:D], ACT.Copy)
            act.activation(proj_bias[:], pq[:, 0:D], ACT.Copy).then_inc(set_act, 1)

        def set_up(eng):
            eng.wait_ge(set_dve, 6)
            eng.wait_ge(set_act, 10)
            eng.wait_ge(set_pool, 3)
            eng.wait_ge(w_in, LOADED)

        FRONT = ["load", "front1", "front2", "front3", "xT"]
        DIR = ["xz", "conv", "bc", "split", "dt", "softplus"]
        BACK = ["back1", "back2", "back3", "back4"]

        def plan(c, back, front):
            slots = {w: [] for w in range(U2)}
            for i, s in enumerate(DIR):
                slots[i].append((s, c, 1))
            if back:
                for i, s in enumerate(BACK):
                    slots[6 + i].append((s, c - 1, 0))
            slots[UD - 1].append(("keep", c, 0))
            if front:
                for i, s in enumerate(FRONT):
                    slots[UD + i].append((s, c + 1, 0))
                for i, s in enumerate(DIR):
                    slots[UD + 5 + i].append((s, c + 1, 0))
            for g in range(1, 2 * NG):
                slots[NC * (g - 1) + 1].append(("rep", c, g))
            for w in range(U2):
                yield "unit", c, w
                yield from slots[w]
                if w % UD == UD - 1:
                    yield "gate", c, w // UD
            if front:
                yield "rep", c + 1, 0

        def prologue():
            for s in FRONT:
                yield s, 0, 0
            for s in DIR:
                yield s, 0, 0
            yield "rep", 0, 0

        def run(eng, steps, plan_steps):
            for what, c, k in plan_steps:
                if what in steps:
                    steps[what](eng, c, k)

        def program(eng, steps):
            run(eng, steps, prologue())
            run(eng, steps, plan(0, False, True))
            run(eng, steps, plan(1, True, True))
            with eng.Fori(2, NCH - 1) as c:
                run(eng, steps, plan(c, True, True))
            run(eng, steps, plan(NCH - 1, True, False))
            run(eng, steps, ((s, NCH - 1, 0) for s in BACK))

        @block.sync
        def _(sp):
            sp_setup(sp)
            sp.wait_ge(set_pool, 3)
            for q in range(SPARES):
                sp.dma_start(dram["xs"].rearrange("(r q) p x -> q p r x", q=SPARES)[q], spare[:, q, :].unsqueeze(1).to_broadcast([128, NJ // SPARES, XW])).then_inc(filled, 16)
            program(sp, {
                "load": lambda e, c, k: sp_front(e, c),
                "back4": lambda e, c, k: sp_back(e, c),
            })
            sp.wait_ge(h2_out, 16 * NCH)
            sp.wait_ge(x3_out, 16 * NCH)
            sp.wait_ge(filled, 16 * SPARES)

        @block.gpsimd
        def _(gp):
            pool_setup(gp)
            set_up(gp)
            program(gp, {
                "load": lambda e, c, k: pool_front(e, c),
                "keep": lambda e, c, k: pool_keep(e, c),
                "unit": pool_unit,
            })

        @block.scalar
        def _(act):
            act_setup(act)
            set_up(act)
            program(act, {
                "front1": lambda e, c, k: act_front1(e, c),
                "front2": lambda e, c, k: act_front2(e, c),
                "xT": lambda e, c, k: act_front3(e, c),
                "keep": lambda e, c, k: act_keep(e, c),
                "xz": act_dir1, "conv": act_dir2, "bc": act_dir3, "dt": act_dir4,
                "rep": act_rep, "unit": act_unit,
                "back1": lambda e, c, k: act_back1(e, c),
                "back2": lambda e, c, k: act_back2(e, c),
                "back4": lambda e, c, k: act_back3(e, c),
            })

        @block.vector
        def _(v):
            dve_setup(v)
            set_up(v)

            def unit_v(e, c, w):
                dve_scan(e, c, w)
                if w % UD:
                    dve_hc(e, c, w - 1)
                if w % UD == UD - 1:
                    dve_hc(e, c, w)

            program(v, {
                "front1": lambda e, c, k: dve_front1(e, c),
                "front2": lambda e, c, k: dve_front2(e, c),
                "front3": lambda e, c, k: dve_front3(e, c),
                "conv": dve_dir1, "split": dve_dir2, "dt": dve_dir3a, "softplus": dve_dir3,
                "unit": unit_v, "gate": dve_gate,
                "back1": lambda e, c, k: dve_back1(e, c),
                "back2": lambda e, c, k: dve_back2(e, c),
                "back3": lambda e, c, k: dve_back3(e, c),
                "back4": lambda e, c, k: dve_back4(e, c),
            })

        @block.tensor
        def _(pe):
            pe_setup(pe)
            set_up(pe)

            def unit_pe(e, c, w):
                if w % UD:
                    pe_unit(e, c, w - 1)
                if w % UD == UD - 1:
                    pe_unit(e, c, w)

            program(pe, {
                "load": lambda e, c, k: pe_front(e, c),
                "xT": lambda e, c, k: pe_front2(e, c),
                "xz": pe_dir1, "bc": pe_dir2, "dt": pe_dir3,
                "rep": pe_rep, "unit": unit_pe,
                "back1": lambda e, c, k: pe_back1(e, c),
                "back4": lambda e, c, k: (pe_back2(e, c), pe_back3(e, c)),
            })

def build_experts(nc, a, dram, ident, logits, sem, out):
    with ExitStack() as ctx:
        def sb(name, shape, dt=F32):
            return ctx.enter_context(nc.sbuf_tensor(name, shape, dt))

        def pb(name, shape, dt=F32):
            return ctx.enter_context(nc.psum_tensor(name, shape, dt))

        w13 = sb("w13", [KH, E, 2, 2 * HF])
        wd = sb("wd", [128, E, HF // 128, D])
        xe = sb("xe", [128, NTT, XW])
        dest = sb("dest", [128, NTT], I32)
        tri = sb("tri", [128, 128])
        every = sb("every", [128, 128])
        rev_i = sb("rev_i", [128, E], I32)
        rev = sb("rev", [128, E])
        tile_i = sb("tile_i", [1, NJ], I32)
        tile_f = sb("tile_f", [1, NJ])
        cand = sb("cand", [128, NTT, E])
        pick = [sb(f"pick{k}", [128, NTT, E]) for k in range(2)]
        left = sb("left", [128, NTT, E])
        top = [sb(f"top{k}", [128, NTT]) for k in range(2)]
        best = sb("best", [128, NTT])
        both = sb("both", [128, NTT, E])
        totals = sb("totals", [128, E, NTT])
        cum = sb("cum", [128, E, NTT])
        carry_on = sb("carry_on", [128, E, NTT])
        slotmap = sb("slotmap", [128, NTT, E])
        tiles_i = sb("tiles_i", [128, E], I32)
        tiles_f = sb("tiles_f", [128, E])
        ends = sb("ends", [128, E])
        starts = sb("starts", [128, E])
        one8 = sb("one8", [128, E])
        slot_f = sb("slot_f", [128, NTT])
        slot = [sb(f"slot{k}", [128, NTT], I32) for k in range(2)]
        le = sb("le", [1, NJ, E])
        owner_f = sb("owner_f", [1, NJ])
        owner = sb("owner", [1, NJ], I32)
        wt = [sb(f"wt{k}", [128, NTT]) for k in range(2)]
        xs = sb("xs", [128, 2, XW])
        xsT = sb("xsT", [KH, 2, 2, 128])
        act_g = sb("act_g", [128, HF])
        hid = sb("hid", [128, HF])
        hidT = sb("hidT", [128, 2, HF])
        ys = sb("ys", [128, 2, D])
        yidx = sb("yidx", [128, 2], I32)
        yp = sb("yp", [128, 2, NT, 2, D])
        hres = sb("hres", [128, 2, NT, D])

        gu = pb("gu", [128, 2 * HF])
        hps = pb("hps", [128, 1024])
        xps = pb("xps", [128, 512])
        yps = pb("yps", [128, 512])
        cnt = pb("cnt", [128, 512])

        w_in = sem("expert_weights_loaded")
        xe_in = sem("tokens_loaded")
        mk = sem("masks_made")
        mk_v = sem("masks_made_dve")
        rt_a = sem("routing_exp")
        rt_p = sem("routing_counts")
        scattered = sem("tokens_scattered")
        xs_in = [sem(f"slot_tile_loaded{b}") for b in range(2)]
        xt_ps = sem("slot_tile_transposed")
        xt_sb = sem("slot_tile_ready")
        gu_ok = sem("gate_up_done")
        sg_ok = sem("gate_activated")
        hid_ok = sem("hidden_ready")
        ht_ps = sem("hidden_transposed")
        ht_sb = sem("hidden_turned_ready")
        y_ps = sem("down_done")
        y_sb = sem("rows_ready")
        ix_ok = sem("row_places_ready")
        y_out = [sem(f"rows_scattered{b}") for b in range(2)]
        back_in = [sem(f"pairs_loaded{b}") for b in range(2)]
        mix = sem("mixed")
        out_ok = [sem(f"outputs_stored{b}") for b in range(2)]
        passes = {e: sem(f"expert_passes_{e}") for e in ("SP", "Pool", "DVE")}

        def alone(eng):
            eng.sem_inc(passes[eng.engine.name], 1)

        block = ctx.enter_context(nc.Block())
        KT = HF // 128
        j_all = range(NJ)

        def bc_t(x):
            return x.unsqueeze(2).to_broadcast([128, NTT, E])

        def sp_tile(sp, j, b):
            wait(sp, xt_ps, j - 1)
            alone(sp)
            wait(sp, ix_ok, j - 1)
            alone(sp)
            sp.dma_start(xs[:, b, :], dram["xs"][bass.ds(j, 1)].rearrange("a p k -> p (a k)")).then_inc(xs_in[b], 16)

        def pe_xT(pe, j, b, n):
            pe.wait_ge(xs_in[b], 16 * n)
            wait(pe, xt_sb, j)
            for k in range(2):
                mm = pe.transpose(xps[0:KH, 128 * k:128 * k + 128], xs[:, b, KH * k:KH * k + KH], ident[:])
            mm.then_inc(xt_ps, 1)

        def act_xT(act, j, b):
            act.wait_ge(xt_ps, j + 1)
            wait(act, gu_ok, j - 1)
            act.activation(xsT[:, b].rearrange("p k t -> p (k t)"), xps[0:KH, 0:256], ACT.Copy).then_inc(xt_sb, 1)

        def pe_gu(pe, j, b, e):
            pe.wait_ge(xt_sb, j + 1)
            wait(pe, hid_ok, j)
            for n in range(3):
                for k in range(2):
                    mm = pe.matmul(gu[:, 512 * n:512 * n + 512], xsT[:, b, k, :], w13[:, bass.ds(e, 1), k, 512 * n:512 * n + 512].rearrange("p a n -> p (a n)"), start=(k == 0), stop=(k == 1))
            mm.then_inc(gu_ok, 1)

        def act_gate(act, j):
            act.wait_ge(gu_ok, j + 1)
            wait(act, hid_ok, j)
            act.activation(act_g[:], gu[:, 0:HF], ACT.Silu).then_inc(sg_ok, 1)

        def dve_hid(v, j):
            v.wait_ge(sg_ok, j + 1)
            wait(v, ht_ps, j)
            v.tensor_tensor(hid[:], act_g[:], gu[:, HF:2 * HF], ALU.mult).then_inc(hid_ok, 1)

        def pe_hT(pe, j):
            pe.wait_ge(hid_ok, j + 1)
            wait(pe, ht_sb, j)
            for k in range(KT):
                mm = pe.transpose(hps[:, 128 * k:128 * k + 128], hid[:, 128 * k:128 * k + 128], ident[:])
            mm.then_inc(ht_ps, 1)

        def act_hT(act, j, b):
            act.wait_ge(ht_ps, j + 1)
            wait(act, y_ps, j - 1)
            act.activation(hidT[:, b, :], hps[:, 0:HF], ACT.Copy).then_inc(ht_sb, 1)

        def pe_down(pe, j, b, e):
            pe.wait_ge(ht_sb, j + 1)
            wait(pe, y_sb, j)
            for k in range(KT):
                mm = pe.matmul(yps[:, 0:D], hidT[:, b, 128 * k:128 * k + 128], wd[:, bass.ds(e, 1), k, :].rearrange("p a n -> p (a n)"), start=(k == 0), stop=(k == KT - 1))
            mm.then_inc(y_ps, 1)

        def dve_y(v, j, b, n):
            v.wait_ge(y_ps, j + 1)
            wait(v, y_out[b], 16 * n)
            v.tensor_copy(ys[:, b, :], yps[:, 0:D]).then_inc(y_sb, 1)

        def dve_idx(v, j, b, n):
            v.wait_ge(xs_in[b], 16 * n + 16)
            wait(v, y_out[b], 16 * n)
            v.tensor_copy(yidx[:, b:b + 1], xs[:, b, D:D + 1]).then_inc(ix_ok, 1)

        def pool_y(gp, j, b):
            gp.wait_ge(ix_ok, j + 1)
            gp.wait_ge(y_sb, j + 1)
            alone(gp)
            gp.indirect_dma_start(dram["pairs"], bass.IndirectOffsetOnAxis(ap=yidx[:, b:b + 1], axis=0), ys[:, b, :], None).then_inc(y_out[b], 16)

        def owner_of(pe, j):
            return pe.value_load(owner[0:1, bass.ds(j, 1)], min_val=0, max_val=E - 1)

        def sp_pairs(sp, c, b, n):
            wait(sp, mix, 2 * c - 2)
            alone(sp)
            sp.dma_start(yp[:, b].rearrange("p t k d -> p t (k d)"), rows_of(dram["pairs"], c)).then_inc(back_in[b], 16)
            wait(sp, out_ok[b], 16 * n)
            alone(sp)
            sp.dma_start(hres[:, b].rearrange("p t d -> p (t d)"), dram["h2"][bass.ds(c, 1)].rearrange("a p k -> p (a k)")).then_inc(back_in[b], 16)

        def rows_of(pairs, c):
            return pairs[0:2 * NTOK, :].rearrange("(c t p k) d -> c p t (k d)", c=NCH, t=NT, p=128)[bass.ds(c, 1)].rearrange("a p t q -> p (a t) q")

        def dve_mix(v, c, b, n):
            v.wait_ge(back_in[b], 32 * n + 32)
            for k in range(2):
                if k:
                    v.wait_ge(mix, 2 * c + 1)
                for t in range(NT):
                    o = v.scalar_tensor_tensor(hres[:, b, t, :], yp[:, b, t, k, :], wt[k][:, bass.ds(NT * c + t, 1)], hres[:, b, t, :], ALU.mult, ALU.add)
                o.then_inc(mix, 1)

        def sp_store(sp, c, b):
            sp.wait_ge(mix, 2 * c + 2)
            alone(sp)
            sp.dma_start(out[bass.ds(c, 1)].rearrange("a p k -> p (a k)"), hres[:, b].rearrange("p t d -> p (t d)")).then_inc(out_ok[b], 16)

        rv = Steps(sem("routing_dve"), "max0 eq0 cand0 best0 pick0 left max1 eq1 cand1 best1 pick1 both diff den w0 w1 "
                   "totals cum tiles0 tiles1 tiles2 ends starts excl off map s0 slots0 place0 s1 slots1 place1 ge sum owner")

        def turn(v, op, name):
            op.then_inc(rv.sem, 1)
            v.wait_ge(rv.sem, rv.after(name, 0))

        def dve_route(v):
            def by_expert(x):
                return x[:].unsqueeze(1).to_broadcast([128, NTT, E])

            v.wait_ge(mk, 3)
            v.tensor_copy(rev[:], rev_i[:])
            v.tensor_copy(tile_f[:], tile_i[:])
            v.memset(one8[:], 1.0)
            v.memset(carry_on[:], 1.0)
            v.memset(xe[:, :, D:XW], 0.0).then_inc(mk_v, 1)
            v.wait_ge(mk_v, 1)
            v.memset(carry_on[:, :, 0:1], 0.0)
            v.tensor_copy(xe[:, :, D:D + 1], dest[:].unsqueeze(2)).then_inc(mk_v, 1)
            v.wait_ge(mk_v, 2)
            src = logits
            for k in range(2):
                turn(v, v.tensor_reduce(top[k][:], src[:], AX.X, ALU.max), f"max{k}")
                turn(v, v.tensor_tensor(both[:], src[:], bc_t(top[k][:]), ALU.is_equal), f"eq{k}")
                turn(v, v.tensor_tensor(cand[:], both[:], by_expert(rev), ALU.mult), f"cand{k}")
                turn(v, v.tensor_reduce(best[:], cand[:], AX.X, ALU.max), f"best{k}")
                turn(v, v.tensor_tensor(pick[k][:], cand[:], bc_t(best[:]), ALU.is_equal), f"pick{k}")
                if k == 0:
                    turn(v, v.scalar_tensor_tensor(left[:], pick[0][:], -3.0e38, logits[:], ALU.mult, ALU.add), "left")
                    src = left
            turn(v, v.tensor_tensor(both[:], pick[0][:], pick[1][:], ALU.add), "both")
            turn(v, v.tensor_tensor(wt[1][:], top[1][:], top[0][:], ALU.subtract), "diff")
            v.wait_ge(rt_a, 1)
            turn(v, v.tensor_scalar(slot_f[:], wt[1][:], 1.0, None, ALU.add), "den")
            turn(v, v.reciprocal(wt[0][:], slot_f[:]), "w0")
            turn(v, v.tensor_tensor(wt[1][:], wt[1][:], wt[0][:], ALU.mult), "w1")
            v.wait_ge(rt_p, 1)
            turn(v, v.tensor_copy(totals[:], cnt[:, NTT * E:2 * NTT * E].rearrange("p (t e) -> p e t", e=E)), "totals")
            turn(v, v.tensor_tensor_scan(cum[:].rearrange("p e t -> p (e t)"), carry_on[:].rearrange("p e t -> p (e t)"), totals[:].rearrange("p e t -> p (e t)"), 0.0, ALU.mult, ALU.add), "cum")
            turn(v, v.tensor_scalar(tiles_i[:].unsqueeze(2), cum[:, :, NTT - 1:NTT], 127.0, None, ALU.add), "tiles0")
            turn(v, v.tensor_scalar(tiles_i[:], tiles_i[:], 7, None, ALU.arith_shift_right), "tiles1")
            turn(v, v.tensor_copy(tiles_f[:], tiles_i[:]), "tiles2")
            turn(v, v.tensor_tensor_scan(ends[:], one8[:], tiles_f[:], 0.0, ALU.mult, ALU.add), "ends")
            turn(v, v.tensor_tensor(starts[:], ends[:], tiles_f[:], ALU.subtract), "starts")
            turn(v, v.tensor_tensor(cum[:], cum[:], totals[:], ALU.subtract), "excl")
            turn(v, v.scalar_tensor_tensor(cum[:], starts[:].unsqueeze(2).to_broadcast([128, E, NTT]), 128.0, cum[:], ALU.mult, ALU.add), "off")
            turn(v, v.tensor_tensor(slotmap[:], cnt[:, 0:NTT * E].rearrange("p (t e) -> p t e", e=E), cum[:].rearrange("p e t -> p t e"), ALU.add), "map")
            for k in range(2):
                turn(v, v.tensor_tensor(cand[:], pick[k][:], slotmap[:], ALU.mult), f"s{k}")
                turn(v, v.tensor_reduce(slot_f[:], cand[:], AX.X, ALU.add), f"slots{k}")
                turn(v, v.tensor_copy(slot[k][:], slot_f[:]), f"place{k}")
            turn(v, v.tensor_tensor(le[:], tile_f[:].unsqueeze(2).to_broadcast([1, NJ, E]), ends[0:1, :].unsqueeze(1).to_broadcast([1, NJ, E]), ALU.is_ge), "ge")
            turn(v, v.tensor_reduce(owner_f[:], le[:], AX.X, ALU.add), "sum")
            turn(v, v.tensor_scalar(owner[:], owner_f[:], float(E - 1), None, ALU.min), "owner")
            v.wait_ge(scattered, 16 * NTT)
            v.tensor_scalar(xe[:, :, D:D + 1], xe[:, :, D:D + 1], 1.0, None, ALU.add).then_inc(mk_v, 1)

        LAST = NJ - 1

        @block.sync
        def _(sp):
            for c in range(NCH):
                sp.dma_start(xe[:, NT * c:NT * c + NT, 0:D], dram["x3"][c].rearrange("p (t d) -> p t d", d=D)).then_inc(xe_in, 16)
            for e in range(E):
                sp.dma_start(w13[:, e].rearrange("p k n -> p (k n)"), a["w13"][:, e, :]).then_inc(w_in, 16)
                sp.dma_start(wd[:, e].rearrange("p k n -> p (k n)"), a["wd"][:, e, :]).then_inc(w_in, 16)
            sp.wait_ge(scattered, 16 * 2 * NTT)
            for j in range(2):
                sp_tile(sp, j, j)
            with sp.Fori(1, NJ // 2) as i:
                for b in range(2):
                    sp_tile(sp, 2 * i + b, b)
            sp_tile(sp, LAST, 0)
            for b in range(2):
                sp.wait_ge(y_out[b], 16 * (NJ // 2 + 1 - b))
            for c in range(2):
                sp_pairs(sp, c, c, 0)
            with sp.Fori(1, NCH // 2) as i:
                for b in range(2):
                    sp_store(sp, 2 * i - 2 + b, b)
                    sp_pairs(sp, 2 * i + b, b, i)
            for b in range(2):
                sp_store(sp, NCH - 2 + b, b)
            for b in range(2):
                sp.wait_ge(out_ok[b], 16 * (NCH // 2))

        @block.gpsimd
        def _(gp):
            gp.iota(rev_i[:], pattern=[[-1, E]], base=E, channel_multiplier=0)
            gp.iota(tile_i[:], pattern=[[1, NJ]], base=0, channel_multiplier=0)
            gp.iota(dest[:], pattern=[[256, NTT]], base=0, channel_multiplier=2)
            gp.memset(every[:], 1.0).then_inc(mk, 1)
            gp.wait_ge(mk, 1)
            gp.affine_select(out=tri[:], in_=every[:], compare_op=ALU.is_gt, fill=0.0, base=0, pattern=[[1, 128]], channel_multiplier=-1).then_inc(mk, 1)
            gp.wait_ge(mk, 2)
            gp.sem_inc(mk, 1)
            gp.wait_ge(mk_v, 2)
            gp.wait_ge(xe_in, 16 * NCH)
            for k in range(2):
                gp.wait_ge(rv.sem, rv.after(f"place{k}", 0))
                if k:
                    gp.wait_ge(mk_v, 3)
                for t in range(NTT):
                    gp.indirect_dma_start(dram["xs"].rearrange("j p x -> (j p) x"), bass.IndirectOffsetOnAxis(ap=slot[k][:, t:t + 1], axis=0), xe[:, t, :], None).then_inc(scattered, 16)
            for b in range(2):
                pool_y(gp, b, b)
            with gp.Fori(1, NJ // 2) as i:
                for b in range(2):
                    pool_y(gp, 2 * i + b, b)
            pool_y(gp, LAST, 0)

        @block.scalar
        def _(act):
            act.wait_ge(rv.sem, rv.after("diff", 0))
            act.activation(wt[1][:], wt[1][:], ACT.Exp).then_inc(rt_a, 1)
            act_xT(act, 0, 0)

            def tile(j, b):
                act_gate(act, j)
                act_xT(act, j + 1, 1 - b)
                act_hT(act, j, b)

            for b in range(2):
                tile(b, b)
            with act.Fori(1, NJ // 2) as i:
                for b in range(2):
                    tile(2 * i + b, b)
            act_gate(act, LAST)
            act_hT(act, LAST, 0)

        @block.vector
        def _(v):
            dve_route(v)
            dve_hid(v, 0)
            dve_idx(v, 0, 0, 0)
            dve_hid(v, 1)
            dve_y(v, 0, 0, 0)
            dve_idx(v, 1, 1, 0)
            with v.Fori(1, NJ // 2) as i:
                for b in range(2):
                    dve_hid(v, 2 * i + b)
                    dve_y(v, 2 * i + b - 1, 1 - b, i - 1 + b)
                    dve_idx(v, 2 * i + b, b, i)
            dve_hid(v, LAST)
            dve_y(v, LAST - 1, 1, LAST // 2 - 1)
            dve_idx(v, LAST, 0, LAST // 2)
            dve_y(v, LAST, 0, LAST // 2)
            for b in range(2):
                dve_mix(v, b, b, 0)
            with v.Fori(1, NCH // 2) as i:
                for b in range(2):
                    dve_mix(v, 2 * i + b, b, i)

        @block.tensor
        def _(pe):
            pe.wait_ge(mk, 2)
            pe.wait_ge(rv.sem, rv.after("both", 0))
            pe.matmul(cnt[:, 0:NTT * E], tri[:], both[:].rearrange("p t e -> p (t e)"), start=True, stop=True)
            pe.matmul(cnt[:, NTT * E:2 * NTT * E], every[:], both[:].rearrange("p t e -> p (t e)"), start=True, stop=True).then_inc(rt_p, 1)
            pe.wait_ge(w_in, 16 * 2 * E)
            pe.wait_ge(rv.sem, rv.after("owner", 0))
            pe_xT(pe, 0, 0, 1)
            e0 = owner_of(pe, 0)
            pe_gu(pe, 0, 0, e0)
            pe_xT(pe, 1, 1, 1)
            pe_hT(pe, 0)
            pe_gu(pe, 1, 1, owner_of(pe, 1))
            pe_down(pe, 0, 0, owner_of(pe, 0))
            pe_xT(pe, 2, 0, 2)
            pe_hT(pe, 1)
            with pe.Fori(1, NJ // 2) as i:
                for b in range(2):
                    j = 2 * i + b
                    pe_gu(pe, j, b, owner_of(pe, j))
                    pe_down(pe, j - 1, 1 - b, owner_of(pe, j - 1))
                    pe_xT(pe, j + 1, 1 - b, i + 1 + b)
                    pe_hT(pe, j)
            pe_gu(pe, LAST, 0, owner_of(pe, LAST))
            pe_down(pe, LAST - 1, 1, owner_of(pe, LAST - 1))
            pe_hT(pe, LAST)
            pe_down(pe, LAST, 0, owner_of(pe, LAST))


INPUTS = ["p_tok", "p_T", "ids", "taus", "tok_emb", "seg_emb", "w_tau", "b_tau", "alpha", "projT", "tgam", "tbet", "projb",
          "bm_in", "bm_b", "inT", "outw", "bmoT", "xpw_bc", "xpw_dt", "dtw", "dtb", "cw", "cb", "dskip", "a_log",
          "outb", "ln_g", "ln_b", "rw", "w13", "wd"]


def fusion_block(nc, a, out):
    dram = {
        "h2": nc.dram_tensor("h2_scratch", [NCH, 128, NT * D], F32, kind="Internal").ap(),
        "x3": nc.dram_tensor("x3_scratch", [NCH, 128, NT * D], F32, kind="Internal").ap(),
        "xs": nc.dram_tensor("slot_rows", [NJ, 128, XW], F32, kind="Internal").ap(),
        "pairs": nc.dram_tensor("result_rows", [2 * NTOK + 128 * SPARES, D], F32, kind="Internal").ap(),
    }
    with ExitStack() as ctx:
        def sem(name):
            return ctx.enter_context(nc.semaphore(name))

        ident = ctx.enter_context(nc.sbuf_tensor("ident", [128, 128], F32))
        logits = ctx.enter_context(nc.sbuf_tensor("logits", [128, NTT, E], F32))
        build_mamba(nc, a, dram, ident, logits, sem)
        build_experts(nc, a, dram, ident, logits, sem, out)


def lay_out(f):
    import numpy as np

    def rows(x, p):
        x = x.reshape(-1, p, *x.shape[1:])
        return np.moveaxis(x, 1, 0).reshape(p, -1)

    patches = f["x"].reshape(B, 3, 4, 16, 4, 16).transpose(0, 2, 4, 3, 5, 1).reshape(NCH, 128, PD)

    def texts(x):
        return x.reshape(NCH, 2, 128)

    xpw = f["L0_attn_m_xproj_w"].T
    row = lambda n: f[n].reshape(1, -1)
    column = lambda n, p: rows(f[n].reshape(-1, 1), p)
    a = {
        "p_tok": patches,
        "p_T": patches.reshape(NCH, 128, PD // 128, 128).transpose(0, 3, 2, 1).reshape(NCH, 128, PD),
        "ids": np.concatenate([texts(f["x_txt"]), texts(f["itok_BS_0_3"])], 1).transpose(0, 2, 1),
        "taus": np.concatenate([texts(f["fside_BS_age"]), texts(f["fside_BS_position"])], 1).transpose(0, 2, 1),
        "tok_emb": f["L0_txt_token_emb"], "seg_emb": f["L0_txt_seg_emb"],
        "w_tau": np.concatenate([f["L0_txt_w_age"], f["L0_txt_w0_age"], f["L0_txt_w_abs"], f["L0_txt_w0_abs"]], 1),
        "b_tau": np.concatenate([f["L0_txt_b_age"], f["L0_txt_b0_age"], f["L0_txt_b_abs"], f["L0_txt_b0_abs"]], 1),
        "alpha": np.stack([f["L0_txt_alpha_age"], f["L0_txt_alpha_abs"], f["L0_txt_alpha_seg"]]).reshape(1, 3),
        "projT": rows(f["L0_tok_W_proj"].T, 128), "tgam": column("L0_tok_gamma", 128), "tbet": column("L0_tok_beta", 128),
        "projb": row("L0_tok_b_proj"),
        "bm_in": rows(f["L0_attn_bm_in_w"], KH), "bm_b": column("L0_attn_bm_in_b", KH), "inT": rows(f["L0_attn_m_in_w"].T, KH),
        "outw": rows(f["L0_attn_m_out_w"], KH), "bmoT": rows(f["L0_attn_bm_out_w"].T, KH),
        "xpw_bc": rows(xpw[:, R:], 128).reshape(128, NC, 2 * NS), "xpw_dt": rows(xpw[:, :R], 128).reshape(128, NC, R),
        "dtw": f["L0_attn_m_dt_w"].T, "dtb": column("L0_attn_m_dt_b", 128),
        "cw": rows(f["L0_attn_m_conv_w"], 128), "cb": column("L0_attn_m_conv_b", 128),
        "dskip": column("L0_attn_m_D", 128), "a_log": rows(f["L0_attn_m_A_log"], 128),
        "outb": row("L0_attn_bm_out_b"), "ln_g": row("L0_attn_ln_g"), "ln_b": row("L0_attn_ln_b"),
        "rw": rows(f["L0_ffn_router_w"].T, KH),
        "w13": np.stack([f["L0_ffn_Wg"], f["L0_ffn_Wu"]], 1).reshape(E, 2, HF, 2, KH).transpose(4, 0, 3, 1, 2).reshape(KH, E, 4 * HF),
        "wd": f["L0_ffn_Wd"].reshape(E, D, HF // 128, 128).transpose(3, 0, 2, 1).reshape(128, E, (HF // 128) * D),
    }
    return {n: np.ascontiguousarray(x) for n, x in a.items()}


def kernel(**inputs):
    import numpy as np
    import concourse.bacc as bacc
    from concourse.bass_utils import run_bass_kernel_spmd

    nc = bacc.Bacc("TRN2", target_bir_lowering=False, num_devices=1)
    laid = lay_out({n: np.asarray(x) for n, x in inputs.items()})
    args = {n: nc.dram_tensor(f"in_{n}", laid[n].shape, mybir.dt.from_np(laid[n].dtype), kind="ExternalInput").ap() for n in INPUTS}
    out = nc.dram_tensor("out_tokens", [NCH, 128, NT * D], F32, kind="ExternalOutput").ap()
    fusion_block(nc, args, out)
    r = run_bass_kernel_spmd(nc, [{f"in_{n}": laid[n] for n in INPUTS}], core_ids=[0])
    y = np.asarray(r.results[0]["out_tokens"]).reshape(NCH, 128, NT, D)
    image = y[:, :, 0].reshape(NCH, CB, LI, D)
    text = y[:, :, 1:].transpose(0, 2, 1, 3).reshape(NCH, CB, LT, D)
    return np.concatenate([image, text], 2).reshape(B, L, D)
```

```python
from contextlib import ExitStack
import math

import concourse.bass as bass
from concourse import mybir

F32 = mybir.dt.float32
BF16 = mybir.dt.bfloat16
I32 = mybir.dt.int32
ALU = mybir.AluOpType
ACT = mybir.ActivationFunctionType
AX = mybir.AxisListType

B, L, LI, LT = 64, 48, 16, 32
D, DI, NS, R = 192, 384, 16, 12
KH = D // 2
PD = 768
CB = 8
NCH = B // CB
T = CB * L
NT = T // 128
NC = DI // 128
NG = 4
GN = NS // NG
UD = NG * NC
U2 = 2 * UD
NRING = 4
NDA = 3
AHEAD = 2
KC = 3
EPS = 1e-5
E, HF = 8, 768
NTOK = B * L
NTT = NTOK // 128
NJ = 2 * NTT + E - 1
SPARES = 5
XW = D + 4

TWO_PI = 2 * math.pi
C1 = 6.28125
C2 = 0.0019350051879882812
C3 = TWO_PI - C1 - C2
MAGIC = 12582912.0
PI_IN = 3.1415925


class Steps:

    def __init__(self, sem, names):
        self.sem, self.names = sem, names.split()

    def after(self, name, turn):
        return len(self.names) * turn + self.names.index(name) + 1


def wait(eng, sem, value):
    if isinstance(value, int) and value <= 0:
        return
    eng.wait_ge(sem, value)


def build_mamba(nc, a, dram, ident, logits, sem):
    with ExitStack() as ctx:
        def sb(name, shape, dt=F32):
            return ctx.enter_context(nc.sbuf_tensor(name, shape, dt))

        def pb(name, shape, dt=F32):
            return ctx.enter_context(nc.psum_tensor(name, shape, dt))

        ones = sb("ones", [128, 128])
        sel = sb("sel", [96, 2 * NS], BF16)
        wxz = sb("wxz", [KH, 2, 2, 2 * DI])
        bxz = sb("bxz", [128, 2, 2 * NC])
        gw = sb("gw", [128, PD // 128, D])
        proj_sum = sb("proj_sum", [128, D])
        proj_bias = sb("proj_bias", [128, D])
        w2t = sb("w2t", [128, NC, D])
        xpw_bc = sb("xpw_bc", [128, NC, 96])
        xpw_dt = sb("xpw_dt", [128, NC, R])
        dtw = sb("dtw", [R, DI])
        dtb = sb("dtb", [128, NC])
        cw = sb("cw", [128, NC, KC + 1])
        cb = sb("cb", [128, NC])
        dskip = sb("dskip", [128, NC])
        aneg = sb("aneg", [128, NC, NS])
        w_tau = sb("w_tau", [128, 2, D])
        b_tau = sb("b_tau", [128, 2, D])
        alpha = sb("alpha", [128, 3])
        mask = sb("mask", [128, 1])
        am = sb("am", [128, 2])
        outb = sb("outb", [1, D])
        ln_g = sb("ln_g", [128, D])
        ln_b = sb("ln_b", [128, D])
        rw = sb("rw", [KH, 2, E])
        eps = sb("eps", [128, 1])
        spare_i = sb("spare_i", [128, SPARES], I32)
        halfpi = sb("halfpi", [128, 1])
        ptok = sb("ptok", [128, PD])
        pT = sb("pT", [128, PD // 128, 128])
        ids = sb("ids", [128, 4], I32)
        taus = sb("taus", [128, 4])
        tok_rows = sb("tok_rows", [128, 2, D])
        seg_rows = sb("seg_rows", [128, 2, D])
        theta = sb("theta", [128, 2, 2, D])
        turns = sb("turns", [128, 2, 2, D])
        resid = sb("resid", [128, 2, 2, D])
        img_t = sb("img_t", [128, D])
        pst = sb("pst", [128, 2, 6])
        pmv = sb("pmv", [128, 2])
        pneg = sb("pneg", [128, 1])
        prs = sb("prs", [128, 2])
        hst = sb("hst", [128, NT, 6])
        hmv = sb("hmv", [128, NT, 2])
        hrs = sb("hrs", [128, 2, NT])
        h_new = sb("h_new", [128, NT, D])
        x1_new = sb("x1_new", [128, NT, D])
        xT = sb("xT", [KH, 2, CB, L])
        xc = sb("xc", [128, 2, NC, CB, L + KC])
        u = sb("u", [128, 2, NC, T])
        zs = sb("zs", [128, 2, NC, T])
        dt_ = sb("dt_", [128, 2, NC, T])
        dtu = sb("dtu", [128, 2, NC, T])
        stk = sb("stk", [96, 2, T], BF16)
        mid = sb("mid", [96, T], BF16)
        rr = sb("rr", [96, T])
        dtx = sb("dtx", [R, T])
        ea = sb("ea", [128, NC, T])
        lg1 = sb("lg1", [128, NC, T])
        da = sb("da", [128, NDA, GN, T])
        ring = sb("ring", [128, NRING, GN, T])
        zero_cols = sb("zero_cols", [128, GN * CB])
        brep = sb("brep", [128, 2, GN, T])
        crep = sb("crep", [128, 2, GN, T])
        yg = sb("yg", [128, 2, NC, T])
        hb = sb("hb", [128, NT, D])
        x1 = sb("x1", [128, NT, D])
        h2 = sb("h2", [128, NT, D])
        x3 = sb("x3", [128, NT, D])
        qst = sb("qst", [128, NT, 6])
        qmv = sb("qmv", [128, NT, 2])
        qrs = sb("qrs", [128, 2, NT])
        x3T = sb("x3T", [KH, 2, T])
        spare = yg[:].rearrange("p d o t -> p (d o t)")[:, 0:SPARES * XW].rearrange("p (q x) -> p q x", q=SPARES)
        bm_in = ring[0:KH, 0, :, :].rearrange("p n t -> p (n t)")[:, 0:2 * 2 * D].rearrange("p (d j k) -> p d j k", d=2, j=2)
        bm_b = ring[0:KH, 0, 3, 0:4].rearrange("p (d j) -> p d j", d=2)
        inT = ring[0:KH, 1, :, :].rearrange("p n t -> p (n t)")[:, 0:2 * 2 * DI].rearrange("p (j o) -> p j o", j=2)
        outw = ring[0:KH, 2, :, :].rearrange("p n t -> p (n t)")[:, 0:2 * DI].rearrange("p (j o) -> p j o", j=2)
        bmoT = ring[0:KH, 3, :, :].rearrange("p n t -> p (n t)")[:, 0:2 * D].rearrange("p (j o) -> p j o", j=2)
        projT = brep[:, 0, :, :].rearrange("p n t -> p (n t)")[:, 0:6 * D].rearrange("p (k o) -> p k o", k=6)
        tgam = crep[:, 0, 0, 0:6]
        tbet = crep[:, 0, 0, 8:14]
        betas = crep[:, 1, :, :].rearrange("p n t -> p (n t)")[:, 0:768].rearrange("p (k m) -> p k m", k=6)
        projb = crep[0:1, 0, 1, 0:D]
        sel1 = da[0:96, 0, 0, 0:2 * NS]

        py = [pb(f"py{i}", [128, 512]) for i in range(NC)]
        prep = pb("prep", [128, 2, 512])
        pf = [pb(f"pf{i}", [128, 512]) for i in range(2)]
        pq = pb("pq", [128, 512])

        w_in = sem("weights_loaded")
        set_pool = sem("setup_pool")
        set_dve = sem("setup_dve")
        set_pe = sem("setup_pe")
        set_act = sem("setup_act")
        patch_in = sem("patches_loaded")
        ids_in = sem("ids_loaded")
        rows_in = sem("rows_gathered")
        rep_ps = sem("rep_in_psum")
        rep_sb = sem("rep_in_sbuf")
        da_ok = sem("decay_ready")
        dbu_ok = sem("dbu_ready")
        scan_ok = sem("scan_done")
        hc_ok = sem("hc_ready")
        y_ok = sem("states_summed")
        y_out = sem("y_evacuated")
        yg_ok = sem("y_gated")
        hb_ok = sem("h_kept")
        x1_ok = sem("x1_kept")
        full = [sem(f"front{i}_filled") for i in range(2)]
        free = [sem(f"front{i}_freed") for i in range(2)]
        qfull = sem("back_filled")
        qfree = sem("back_freed")
        passes = {e: sem(f"passes_{e}") for e in ("SP", "Pool", "DVE")}
        h2_out = sem("h2_stored")
        filled = sem("slots_filled")
        x3_out = sem("x3_stored")
        fv = Steps(sem("front_dve"), "pstat paggr pneg theta turn round res1 res2 res3 clamp img txt1 txt2 txt3 hstat haggr x1")
        fa = Steps(sem("front_act"), "lnp rsp sin lin lnh rsh")
        dv = Steps(sem("dir_dve"), "conv0 conv1 conv2 conv3 split2 split3 max w1 r m dt dtu")
        da_s = Steps(sem("dir_act"), "silu x exp ln")
        qv = Steps(sem("back_dve"), "stat aggr norm gain h2 stat3 aggr3 x3")
        qa = Steps(sem("back_act"), "ln rs ln3 rs3")

        FJOBS = [("img", 1), ("xT0", 1), ("xT1", 1)]
        for d in range(2):
            FJOBS += [(f"xz{d}_{o}", 1) for o in range(2 * NC)]
            FJOBS += [(f"bc{d}", 2), (f"dtx{d}", 1)] + [(f"dt{d}_{o}", 1) for o in range(NC)]
        JOB = {}
        nfull, nfree = [0, 0], [0, 0]
        for i, (name, readers) in enumerate(FJOBS):
            b = i % 2
            JOB[name] = (b, nfull[b], nfree[b])
            nfull[b] += 1
            nfree[b] += readers

        def job_start(pe, name, c):
            b, _, fr = JOB[name]
            wait(pe, free[b], nfree[b] * c + fr)
            return pf[b]

        def job_wait(eng, name, c):
            b, fu, _ = JOB[name]
            eng.wait_ge(full[b], nfull[b] * c + fu + 1)
            return pf[b]

        def job_read(eng, name, c):
            b, _, fr = JOB[name]
            eng.wait_ge(free[b], nfree[b] * c + fr + dict(FJOBS)[name])

        def jsem(name, which):
            return (full if which == "full" else free)[JOB[name][0]]

        QJ = 5

        def alone(eng):
            eng.sem_inc(passes[eng.engine.name], 1)

        def sp_front(sp, c):
            if not isinstance(c, int) or c > 0:
                wait(sp, fv.sem, fv.after("txt3", c - 1))
                alone(sp)
                wait(sp, free[0], nfree[0] * (c - 1) + 1)
                alone(sp)
                wait(sp, rows_in, 64 * c)
                alone(sp)
            sp.dma_start(ids[:], a["ids"][bass.ds(c, 1)].rearrange("a p k -> p (a k)")).then_inc(ids_in, 16)
            sp.dma_start(taus[:], a["taus"][bass.ds(c, 1)].rearrange("a p k -> p (a k)")).then_inc(ids_in, 16)
            sp.dma_start(ptok[:], a["p_tok"][bass.ds(c, 1)].rearrange("a p k -> p (a k)")).then_inc(patch_in, 16)
            sp.dma_start(pT[:].rearrange("p k t -> p (k t)"), a["p_T"][bass.ds(c, 1)].rearrange("a p k -> p (a k)")).then_inc(patch_in, 16)

        def pool_front(gp, c):
            gp.wait_ge(ids_in, 32 * c + 32)
            wait(gp, fv.sem, fv.after("txt3", c - 1))
            alone(gp)
            for t in range(2):
                gp.indirect_dma_start(tok_rows[:, t, :], None, a["tok_emb"], bass.IndirectOffsetOnAxis(ap=ids[:, t:t + 1], axis=0)).then_inc(rows_in, 16)
                gp.indirect_dma_start(seg_rows[:, t, :], None, a["seg_emb"], bass.IndirectOffsetOnAxis(ap=ids[:, 2 + t:3 + t], axis=0)).then_inc(rows_in, 16)

        def pool_keep(gp, c):
            gp.wait_ge(fv.sem, fv.after("x1", c))
            wait(gp, qv.sem, qv.after("h2", c - 1))
            gp.tensor_tensor(hb[:], h_new[:], ln_b[:].unsqueeze(1).to_broadcast([128, NT, D]), ALU.add).then_inc(hb_ok, 1)

        def act_keep(act, c):
            act.wait_ge(fv.sem, fv.after("x1", c))
            wait(act, qfree, QJ * (c - 1) + 2)
            act.activation(x1[:], x1_new[:], ACT.Copy).then_inc(x1_ok, 1)

        def pe_front(pe, c):
            pe.wait_ge(patch_in, 32 * c + 32)
            p = job_start(pe, "img", c)
            for k in range(PD // 128):
                mm = pe.matmul(p[:, 0:D], pT[:, k, :], gw[:, k, :], start=(k == 0), stop=(k == PD // 128 - 1))
            mm.then_inc(jsem("img", "full"), 1)

        def dve_front1(v, c):
            v.wait_ge(patch_in, 32 * c + 32)
            wait(v, fv.sem, fv.after("paggr", c - 1))
            for i in range(2):
                o = v.bn_stats(pst[:, i, :], ptok[:, 384 * i:384 * i + 384])
            o.then_inc(fv.sem, 1)
            v.wait_ge(fv.sem, fv.after("pstat", c))
            wait(v, fa.sem, fa.after("lnp", c - 1))
            alone(v)
            v.bn_aggr(pmv[:], pst[:].rearrange("p a k -> p (a k)")).then_inc(fv.sem, 1)
            v.wait_ge(fv.sem, fv.after("paggr", c))
            v.tensor_scalar(pneg[:], pmv[:, 0:1], -1.0, None, ALU.mult).then_inc(fv.sem, 1)
            v.wait_ge(ids_in, 32 * c + 32)
            wait(v, fa.sem, fa.after("lin", c - 1))
            for s in range(2):
                for t in range(2):
                    o = v.scalar_tensor_tensor(theta[:, s, t, :], w_tau[:, s, :], taus[:, 2 * s + t:2 * s + t + 1], b_tau[:, s, :], ALU.mult, ALU.add)
            o.then_inc(fv.sem, 1)
            v.wait_ge(fv.sem, fv.after("theta", c))
            for s in range(2):
                o = v.tensor_scalar(turns[:, s], theta[:, s], 1.0 / TWO_PI, 0.25 if s == 0 else 0.0, ALU.mult, ALU.add)
            o.then_inc(fv.sem, 1)
            v.wait_ge(fv.sem, fv.after("turn", c))
            v.tensor_scalar(turns[:], turns[:], MAGIC, -MAGIC, ALU.add, ALU.add).then_inc(fv.sem, 1)

        def dve_front1b(v, c):
            v.wait_ge(fv.sem, fv.after("round", c))
            wait(v, fv.sem, fv.after("txt2", c - 1))
            v.scalar_tensor_tensor(fl(resid), fl(turns), -C1, fl(theta), ALU.mult, ALU.add).then_inc(fv.sem, 1)
            v.wait_ge(fv.sem, fv.after("res1", c))
            v.scalar_tensor_tensor(fl(resid), fl(turns), -C2, fl(resid), ALU.mult, ALU.add).then_inc(fv.sem, 1)
            v.wait_ge(fv.sem, fv.after("res2", c))
            v.scalar_tensor_tensor(fl(resid), fl(turns), -C3, fl(resid), ALU.mult, ALU.add).then_inc(fv.sem, 1)
            v.wait_ge(fv.sem, fv.after("res3", c))
            for s in range(2):
                sh = math.pi / 2 if s == 0 else 0.0
                o = v.tensor_scalar(resid[:, s], resid[:, s], PI_IN - sh, -PI_IN - sh, ALU.min, ALU.max)
            o.then_inc(fv.sem, 1)

        def fl(t):
            return t[:].rearrange("p a b c -> p (a b c)")

        def act_front1(act, c):
            act.wait_ge(fv.sem, fv.after("paggr", c))
            wait(act, fv.sem, fv.after("img", c - 1))
            act.activation(prs[:, 0:1], pmv[:, 1:2], ACT.Ln, bias=eps[:]).then_inc(fa.sem, 1)
            act.wait_ge(fa.sem, fa.after("lnp", c))
            act.activation(prs[:, 1:2], prs[:, 0:1], ACT.Exp, scale=-0.5).then_inc(fa.sem, 1)
            act.preload_act_table_set("silu_and_others")
            act.wait_ge(fv.sem, fv.after("clamp", c))
            for s in range(2):
                o = act.activation(resid[:, s, :, 0:D - 1], resid[:, s, :, 0:D - 1], ACT.Sin, bias=halfpi[:] if s == 0 else 0.0)
            o.then_inc(fa.sem, 1)
            act.preload_act_table_set("natural_log_exp_and_others")
            act.activation(resid[:, :, :, D - 1:D], theta[:, :, :, D - 1:D], ACT.Copy).then_inc(fa.sem, 1)

        def dve_front2(v, c):
            job_wait(v, "img", c)
            wait(v, fv.sem, fv.after("img", c - 1))
            v.wait_ge(fv.sem, fv.after("pneg", c))
            v.scalar_tensor_tensor(img_t[:], proj_sum[:], pneg[:], pf[JOB["img"][0]][:, 0:D], ALU.mult, ALU.add).then_inc(jsem("img", "free"), 1)
            job_read(v, "img", c)
            v.wait_ge(fa.sem, fa.after("rsp", c))
            wait(v, fv.sem, fv.after("x1", c - 1))
            wait(v, hb_ok, c)
            v.scalar_tensor_tensor(h_new[:, 0, :], img_t[:], prs[:, 1:2], proj_bias[:], ALU.mult, ALU.add).then_inc(fv.sem, 1)
            v.wait_ge(fa.sem, fa.after("lin", c))
            v.wait_ge(rows_in, 64 * c + 64)
            for t in range(2):
                o = v.scalar_tensor_tensor(h_new[:, 1 + t, :], resid[:, 0, t, :], am[:, 0:1], tok_rows[:, t, :], ALU.mult, ALU.add)
            o.then_inc(fv.sem, 1)
            v.wait_ge(fv.sem, fv.after("txt1", c))
            for t in range(2):
                o = v.scalar_tensor_tensor(h_new[:, 1 + t, :], resid[:, 1, t, :], am[:, 1:2], h_new[:, 1 + t, :], ALU.mult, ALU.add)
            o.then_inc(fv.sem, 1)
            v.wait_ge(fv.sem, fv.after("txt2", c))
            for t in range(2):
                o = v.scalar_tensor_tensor(h_new[:, 1 + t, :], seg_rows[:, t, :], alpha[:, 2:3], h_new[:, 1 + t, :], ALU.mult, ALU.add)
            o.then_inc(fv.sem, 1)
            v.wait_ge(fv.sem, fv.after("txt3", c))
            for t in range(NT):
                o = v.bn_stats(hst[:, t, :], h_new[:, t, :])
            o.then_inc(fv.sem, 1)
            v.wait_ge(fv.sem, fv.after("hstat", c))
            wait(v, fa.sem, fa.after("lnh", c - 1))
            wait(v, fv.sem, fv.after("x1", c - 1))
            alone(v)
            for t in range(NT):
                o = v.bn_aggr(hmv[:, t, :], hst[:, t, :])
            o.then_inc(fv.sem, 1)

        def act_front2(act, c):
            act.wait_ge(fv.sem, fv.after("haggr", c))
            act.activation(hrs[:, 0, :], hmv[:, :, 1], ACT.Ln, bias=eps[:]).then_inc(fa.sem, 1)
            act.wait_ge(fa.sem, fa.after("lnh", c))
            act.activation(hrs[:, 1, :], hrs[:, 0, :], ACT.Exp, scale=-0.5).then_inc(fa.sem, 1)

        def dve_front3(v, c):
            v.wait_ge(fa.sem, fa.after("rsh", c))
            v.wait_ge(fv.sem, fv.after("haggr", c))
            wait(v, x1_ok, c)
            if not isinstance(c, int) or c > 0:
                wait(v, full[JOB["xT1"][0]], nfull[JOB["xT1"][0]] * (c - 1) + JOB["xT1"][1] + 1)
            for t in range(NT):
                o = v.tensor_scalar(x1_new[:, t, :], h_new[:, t, :], hmv[:, t, 0:1], hrs[:, 1, t:t + 1], ALU.subtract, ALU.mult)
            o.then_inc(fv.sem, 1)

        def pe_front2(pe, c):
            pe.wait_ge(fv.sem, fv.after("x1", c))
            for k in range(2):
                p = job_start(pe, f"xT{k}", c)
                for t in range(NT):
                    mm = pe.transpose(p[0:KH, 128 * t:128 * t + 128], x1_new[:, t, k * KH:(k + 1) * KH], ident[:])
                mm.then_inc(jsem(f"xT{k}", "full"), 1)

        def act_front3(act, c):
            if not isinstance(c, int) or c > 0:
                wait(act, full[JOB[f"xz1_{2 * NC - 1}"][0]], nfull[JOB[f"xz1_{2 * NC - 1}"][0]] * (c - 1) + JOB[f"xz1_{2 * NC - 1}"][1] + 1)
                wait(act, full[JOB[f"xz1_{2 * NC - 2}"][0]], nfull[JOB[f"xz1_{2 * NC - 2}"][0]] * (c - 1) + JOB[f"xz1_{2 * NC - 2}"][1] + 1)
            for k in range(2):
                p = job_wait(act, f"xT{k}", c)
                act.activation(xT[:, k, :, 0:LI], p[0:KH, 0:128].rearrange("p (b l) -> p b l", b=CB), ACT.Copy)
                o = act.activation(xT[:, k, :, LI:L], p[0:KH, 128:T].rearrange("p (b l) -> p b l", b=CB), ACT.Copy)
                o.then_inc(jsem(f"xT{k}", "free"), 1)

        def pe_xz(pe, c, d, pair):
            if pair == 0:
                job_read(pe, "xT1", c)
            for o in (2 * pair, 2 * pair + 1):
                p = job_start(pe, f"xz{d}_{o}", c)
                for k in range(2):
                    mm = pe.matmul(p[:, 0:T], wxz[:, d, k, 128 * o:128 * o + 128], xT[:, k].rearrange("p b l -> p (b l)"), start=(k == 0), stop=(k == 1))
                mm.then_inc(jsem(f"xz{d}_{o}", "full"), 1)

        def act_xz(act, c, d, pair):
            e = 2 * c + d
            if pair == 0:
                wait(act, dv.sem, dv.after("conv3", e - 2))
            if pair == 1:
                wait(act, yg_ok, e - 1)
            for o in (2 * pair, 2 * pair + 1):
                p = job_wait(act, f"xz{d}_{o}", c)
                if o < NC:
                    base = KC if d == 0 else 0
                    out = xc[:, d, o, :, base:base + L]
                    op = act.activation(out, p[:, 0:T].rearrange("p (b l) -> p b l", b=CB), ACT.Identity, bias=bxz[:, d, o:o + 1])
                else:
                    op = act.activation(zs[:, d, o - NC, :], p[:, 0:T], ACT.Identity, bias=bxz[:, d, o:o + 1])
                op.then_inc(jsem(f"xz{d}_{o}", "free"), 1)

        def dve_dir1(v, c, d):
            e = 2 * c + d
            job_read(v, f"xz{d}_{NC - 1}", c)
            job_read(v, f"xz{d}_{NC - 2}", c)
            wait(v, yg_ok, e - 1)
            wait(v, dv.sem, dv.after("dtu", e - 2))
            for k in range(KC + 1):
                if k:
                    v.wait_ge(dv.sem, dv.after(f"conv{k - 1}", e))
                for o in range(NC):
                    at = k if d == 0 else KC - k
                    x = xc[:, d, o, :, at:at + L]
                    uo = u[:, d, o, :].rearrange("p (b l) -> p b l", b=CB)
                    if k == 0:
                        op = v.tensor_scalar(uo, x, cw[:, o, 0:1], cb[:, o:o + 1], ALU.mult, ALU.add)
                    else:
                        op = v.scalar_tensor_tensor(uo, x, cw[:, o, k:k + 1], uo, ALU.mult, ALU.add)
                op.then_inc(dv.sem, 1)

        def act_dir2(act, c, d):
            e = 2 * c + d
            act.preload_act_table_set("silu_and_others")
            act.wait_ge(dv.sem, dv.after("conv3", e))
            job_read(act, f"xz{d}_{2 * NC - 1}", c)
            act.activation(u[:, d], u[:, d], ACT.Silu)
            act.activation(zs[:, d], zs[:, d], ACT.Silu).then_inc(da_s.sem, 1)
            act.preload_act_table_set("natural_log_exp_and_others")

        def pe_dir2(pe, c, d):
            e = 2 * c + d
            pe.wait_ge(da_s.sem, da_s.after("silu", e))
            p = job_start(pe, f"bc{d}", c)
            for i in range(NC):
                mm = pe.matmul(p[0:96, 0:T], xpw_bc[:, i, :], u[:, d, i, :], start=(i == 0), stop=(i == NC - 1))
            mm.then_inc(jsem(f"bc{d}", "full"), 1)
            p = job_start(pe, f"dtx{d}", c)
            for i in range(NC):
                mm = pe.matmul(p[0:R, 0:T], xpw_dt[:, i, :], u[:, d, i, :], start=(i == 0), stop=(i == NC - 1))
            mm.then_inc(jsem(f"dtx{d}", "full"), 1)

        def act_dir3(act, c, d):
            e = 2 * c + d
            p = job_wait(act, f"bc{d}", c)
            wait(act, rep_ps, 4 * NG * (e - 1))
            act.activation(stk[:, d, :], p[0:96, 0:T], ACT.Copy).then_inc(jsem(f"bc{d}", "free"), 1)
            p = job_wait(act, f"dtx{d}", c)
            act.activation(dtx[:], p[0:R, 0:T], ACT.Copy).then_inc(jsem(f"dtx{d}", "free"), 1)

        def dve_dir2(v, c, d):
            e = 2 * c + d
            p = job_wait(v, f"bc{d}", c)
            b, _, fr = JOB[f"bc{d}"]
            v.wait_ge(free[b], nfree[b] * c + fr + 1)
            wait(v, dv.sem, dv.after("split3", e - 1))
            v.tensor_tensor(rr[:], p[0:96, 0:T], stk[:, d, :], ALU.subtract).then_inc(jsem(f"bc{d}", "free"), 1)
            job_read(v, f"bc{d}", c)
            v.tensor_copy(mid[64:96, :], rr[64:96, :])
            v.tensor_copy(stk[32:64, d, :], rr[32:64, :]).then_inc(dv.sem, 1)
            v.wait_ge(dv.sem, dv.after("split2", e))
            v.tensor_tensor(stk[64:96, d, :], rr[64:96, :], mid[64:96, :], ALU.subtract).then_inc(dv.sem, 1)

        def pe_dt(pe, c, d, tiles):
            job_read(pe, f"dtx{d}", c)
            for o in tiles:
                p = job_start(pe, f"dt{d}_{o}", c)
                pe.matmul(p[:, 0:T], dtw[:, 128 * o:128 * o + 128], dtx[:], start=True, stop=True).then_inc(jsem(f"dt{d}_{o}", "full"), 1)

        def act_dt(act, c, d, tiles):
            wait(act, dbu_ok, UD * (2 * c + d - 1))
            for o in tiles:
                p = job_wait(act, f"dt{d}_{o}", c)
                act.activation(dtu[:, d, o, :], p[:, 0:T], ACT.Identity, bias=dtb[:, o:o + 1]).then_inc(jsem(f"dt{d}_{o}", "free"), 1)

        def act_soft(act, c, d):
            e = 2 * c + d
            wait(act, dv.sem, dv.after("r", e - 1))
            job_read(act, f"dt{d}_{NC - 2}", c)
            job_read(act, f"dt{d}_{NC - 1}", c)
            act.activation(ea[:], dtu[:, d], ACT.Abs).then_inc(da_s.sem, 1)
            act.wait_ge(da_s.sem, da_s.after("x", e))
            act.activation(ea[:], ea[:], ACT.Exp, scale=-1.0).then_inc(da_s.sem, 1)
            act.wait_ge(da_s.sem, da_s.after("exp", e))
            wait(act, dv.sem, dv.after("m", e - 1))
            act.activation(lg1[:], ea[:], ACT.Ln, bias=1.0).then_inc(da_s.sem, 1)

        def dve_soft(v, c, d):
            e = 2 * c + d
            wait(v, da_ok, UD * (e - 1))
            v.wait_ge(da_s.sem, da_s.after("exp", e))
            v.tensor_scalar(dt_[:, d], dtu[:, d], 0.0, None, ALU.max).then_inc(dv.sem, 1)
            v.wait_ge(dv.sem, dv.after("max", e))
            v.tensor_scalar(dtu[:, d], ea[:], 1.0, -1.0, ALU.add, ALU.add).then_inc(dv.sem, 1)
            v.wait_ge(dv.sem, dv.after("w1", e))
            v.wait_ge(da_s.sem, da_s.after("ln", e))
            v.tensor_tensor(ea[:], ea[:], dtu[:, d], ALU.subtract).then_inc(dv.sem, 1)
            v.tensor_tensor(dt_[:, d], dt_[:, d], lg1[:], ALU.add).then_inc(dv.sem, 1)
            v.wait_ge(dv.sem, dv.after("m", e))
            v.tensor_tensor(dt_[:, d], dt_[:, d], ea[:], ALU.add).then_inc(dv.sem, 1)
            v.wait_ge(dv.sem, dv.after("dt", e))
            v.tensor_tensor(dtu[:, d], dt_[:, d], u[:, d], ALU.mult).then_inc(dv.sem, 1)

        def pe_rep(pe, c, g, piece):
            d, ng = g // NG, g % NG
            q = 4 * (2 * NG * c + g) + piece
            pe.wait_ge(dv.sem, dv.after("split3", 2 * c + d))
            wait(pe, rep_sb, q)
            for i in range(2):
                j = piece // 2 * NS + ng * GN + 2 * (piece % 2) + i
                mm = pe.matmul(prep[:, i, 0:T], sel[:, j:j + 1].to_broadcast([96, 128]), stk[:, d, :], start=True, stop=True)
            mm.then_inc(rep_ps, 1)

        def act_rep(act, c, g, piece):
            G = 2 * NG * c + g
            if piece % 2 == 0:
                wait(act, dbu_ok if piece == 0 else hc_ok, NC * (G - 1))
            act.wait_ge(rep_ps, 4 * G + piece + 1)
            at = 2 * (piece % 2)
            dst = (brep if piece < 2 else crep)[:, g % 2, at:at + 2, :]
            act.activation(dst, prep[:, :, 0:T], ACT.Copy).then_inc(rep_sb, 1)

        def unit(w):
            d, r = divmod(w, UD)
            ng, o = divmod(r, NC)
            return d, ng, o, d * NG + ng

        def act_unit(act, c, w):
            d, ng, o, g = unit(w)
            U = U2 * c + w
            act.wait_ge(dv.sem, dv.after("dt", 2 * c + d))
            wait(act, scan_ok, U + 1 - NDA)
            lo = 1 if d == 0 else 0
            if w % UD < NDA:
                start = da[:, w % NDA].rearrange("p n (b l) -> p (n b) l", b=CB)[:, :, (L - 1) * d:(L - 1) * d + 1]
                act.activation(start, zero_cols[:].unsqueeze(2), ACT.Copy)
            src = dt_[:, d, o, :].rearrange("p (b l) -> p b l", b=CB)[:, :, lo:lo + L - 1]
            for i in range(GN):
                n = ng * GN + i
                dst = da[:, w % NDA, i, :].rearrange("p (b l) -> p b l", b=CB)[:, :, lo:lo + L - 1]
                op = act.activation(dst, src, ACT.Exp, scale=aneg[:, o, n:n + 1])
            op.then_inc(da_ok, 1)

        def pool_unit(gp, c, w):
            d, ng, o, g = unit(w)
            U, G = U2 * c + w, 2 * NG * c + g
            gp.wait_ge(dv.sem, dv.after("dtu", 2 * c + d))
            gp.wait_ge(rep_sb, 4 * G + 2)
            wait(gp, y_ok, U + 1 - NRING)
            gp.tensor_tensor(ring[:, w % NRING], dtu[:, d, o, :].unsqueeze(1).to_broadcast([128, GN, T]), brep[:, g % 2], ALU.mult).then_inc(dbu_ok, 1)

        def dve_scan(v, c, w):
            d, ng, o, g = unit(w)
            U = U2 * c + w
            v.wait_ge(da_ok, U + 1)
            v.wait_ge(dbu_ok, U + 1)
            x0 = da[:, w % NDA].rearrange("p n t -> p (n t)")
            h = ring[:, w % NRING].rearrange("p n t -> p (n t)")
            if d == 1:
                x0, h = x0[:, ::-1], h[:, ::-1]
            v.tensor_tensor_scan(h, x0, h, 0.0, ALU.mult, ALU.add).then_inc(scan_ok, 1)

        def dve_hc(v, c, w):
            d, ng, o, g = unit(w)
            U, G = U2 * c + w, 2 * NG * c + g
            v.wait_ge(scan_ok, U + 1)
            v.wait_ge(rep_sb, 4 * G + 4)
            v.tensor_tensor(ring[:, w % NRING], ring[:, w % NRING], crep[:, g % 2], ALU.mult).then_inc(hc_ok, 1)

        def pe_unit(pe, c, w):
            d, ng, o, g = unit(w)
            U = U2 * c + w
            pe.wait_ge(hc_ok, U + 1)
            if ng == 0:
                wait(pe, y_out, NC * (2 * c + d - 1) + o + 1)
            for i in range(GN):
                mm = pe.matmul(py[o][:, 0:T], ident[:], ring[:, w % NRING, i, :], start=(ng == 0 and i == 0), stop=(ng == NG - 1 and i == GN - 1))
            mm.then_inc(y_ok, 1)

        def dve_gate(v, c, d):
            e = 2 * c + d
            for o in range(NC):
                v.wait_ge(y_ok, U2 * c + UD * d + UD - NC + o + 1)
                v.scalar_tensor_tensor(u[:, d, o, :], u[:, d, o, :], dskip[:, o:o + 1], py[o][:, 0:T], ALU.mult, ALU.add).then_inc(y_out, 1)
            v.wait_ge(y_out, NC * (e + 1))
            wait(v, qfull, QJ * (c - 1) + 2)
            v.wait_ge(filled, 16 * SPARES)
            for lo, hi in ((0, LI), (LI, L)):
                yv, zv = (x[:, d].rearrange("p o (b l) -> p o b l", b=CB)[:, :, :, lo:hi] for x in (u, zs))
                ov = yg[:, d, :, CB * lo:CB * hi].rearrange("p o (b l) -> p o b l", b=CB)
                op = v.tensor_tensor(ov, yv, zv, ALU.mult)
            op.then_inc(yg_ok, 1)

        def pe_out(pe, c, tiles):
            pe.wait_ge(yg_ok, 2 * c + 2)
            wait(pe, qfree, QJ * c + tiles[0] // 2)
            for t in tiles:
                at = D * (t % 2)
                for i in range(2 * NC):
                    pe.matmul(pq[:, at:at + D], yg[:, i // NC, i % NC, 128 * t:128 * t + 128], w2t[:, i % NC, :], start=(i == 0), stop=False)
                mm = pe.matmul(pq[:, at:at + D], ones[0:1, :], outb[:], start=False, stop=True)
            mm.then_inc(qfull, 1)

        def dve_out(v, c, tiles):
            if tiles[0] == 0:
                v.wait_ge(x1_ok, c + 1)
                wait(v, h2_out, 16 * c)
            v.wait_ge(qfull, QJ * c + tiles[0] // 2 + 1)
            n = len(tiles)
            v.tensor_tensor(h2[:, tiles[0]:tiles[0] + n, :], pq[:, 0:n * D].rearrange("p (t k) -> p t k", k=D), x1[:, tiles[0]:tiles[0] + n, :], ALU.add).then_inc(qfree, 1)

        def dve_stat(v, c):
            v.wait_ge(qfree, QJ * c + 2)
            for t in range(NT):
                o = v.bn_stats(qst[:, t, :], h2[:, t, :])
            o.then_inc(qv.sem, 1)
            v.wait_ge(qv.sem, qv.after("stat", c))
            alone(v)
            for t in range(NT):
                o = v.bn_aggr(qmv[:, t, :], qst[:, t, :])
            o.then_inc(qv.sem, 1)

        def act_back1(act, c):
            act.wait_ge(qv.sem, qv.after("aggr", c))
            act.activation(qrs[:, 0, :], qmv[:, :, 1], ACT.Ln, bias=eps[:]).then_inc(qa.sem, 1)
            act.wait_ge(qa.sem, qa.after("ln", c))
            act.activation(qrs[:, 1, :], qrs[:, 0, :], ACT.Exp, scale=-0.5).then_inc(qa.sem, 1)

        def dve_back2(v, c):
            v.wait_ge(qa.sem, qa.after("rs", c))
            for t in range(NT):
                o = v.tensor_scalar(h2[:, t, :], h2[:, t, :], qmv[:, t, 0:1], qrs[:, 1, t:t + 1], ALU.subtract, ALU.mult)
            o.then_inc(qv.sem, 1)
            v.wait_ge(qv.sem, qv.after("norm", c))
            v.tensor_tensor(h2[:], h2[:], ln_g[:].unsqueeze(1).to_broadcast([128, NT, D]), ALU.mult).then_inc(qv.sem, 1)
            v.wait_ge(qv.sem, qv.after("gain", c))
            v.wait_ge(hb_ok, c + 1)
            v.tensor_tensor(h2[:], h2[:], hb[:], ALU.add).then_inc(qv.sem, 1)
            v.wait_ge(qv.sem, qv.after("h2", c))
            for t in range(NT):
                o = v.bn_stats(qst[:, t, :], h2[:, t, :])
            o.then_inc(qv.sem, 1)
            v.wait_ge(qv.sem, qv.after("stat3", c))
            alone(v)
            for t in range(NT):
                o = v.bn_aggr(qmv[:, t, :], qst[:, t, :])
            o.then_inc(qv.sem, 1)

        def act_back2(act, c):
            act.wait_ge(qv.sem, qv.after("aggr3", c))
            act.activation(qrs[:, 0, :], qmv[:, :, 1], ACT.Ln, bias=eps[:]).then_inc(qa.sem, 1)
            act.wait_ge(qa.sem, qa.after("ln3", c))
            act.activation(qrs[:, 1, :], qrs[:, 0, :], ACT.Exp, scale=-0.5).then_inc(qa.sem, 1)

        def dve_back3(v, c):
            v.wait_ge(qa.sem, qa.after("rs3", c))
            wait(v, x3_out, 16 * c)
            wait(v, qfull, QJ * (c - 1) + 4)
            for t in range(NT):
                o = v.tensor_scalar(x3[:, t, :], h2[:, t, :], qmv[:, t, 0:1], qrs[:, 1, t:t + 1], ALU.subtract, ALU.mult)
            o.then_inc(qv.sem, 1)

        def sp_back(sp, c, what):
            sp.wait_ge(qv.sem, qv.after(what, c))
            alone(sp)
            src, done = (h2, h2_out) if what == "h2" else (x3, x3_out)
            sp.dma_start(dram[what][bass.ds(c, 1)].rearrange("a p k -> p (a k)"), src[:].rearrange("p t k -> p (t k)")).then_inc(done, 16)

        def pe_x3T(pe, c, k):
            pe.wait_ge(qv.sem, qv.after("x3", c))
            wait(pe, qfree, QJ * c + 2 + k)
            for t in range(NT):
                mm = pe.transpose(pq[0:KH, 128 * t:128 * t + 128], x3[:, t, k * KH:(k + 1) * KH], ident[:])
            mm.then_inc(qfull, 1)

        def act_x3T(act, c, k):
            act.wait_ge(qfull, QJ * c + 3 + k)
            if k == 0:
                wait(act, qfull, QJ * c)
            act.activation(x3T[:, k, :], pq[0:KH, 0:T], ACT.Copy).then_inc(qfree, 1)

        def pe_router(pe, c):
            wait(pe, qfree, QJ * c + 4)
            for t in range(NT):
                for k in range(2):
                    mm = pe.matmul(pq[:, E * t:E * t + E], x3T[:, k, 128 * t:128 * t + 128], rw[:, k, :], start=(k == 0), stop=(k == 1))
            mm.then_inc(qfull, 1)

        def dve_router(v, c):
            v.wait_ge(qfull, QJ * c + QJ)
            v.tensor_copy(logits[:, bass.ds(NT * c, NT), :].rearrange("p t e -> p (t e)"), pq[:, 0:NT * E]).then_inc(qfree, 1)

        block = ctx.enter_context(nc.Block())
        loads = [
            (bm_in.rearrange("p d j k -> p (d j k)"), a["bm_in"]), (bm_b.rearrange("p d j -> p (d j)"), a["bm_b"]),
            (inT.rearrange("p j o -> p (j o)"), a["inT"]), (outw.rearrange("p j o -> p (j o)"), a["outw"]),
            (bmoT.rearrange("p j o -> p (j o)"), a["bmoT"]), (projT.rearrange("p k o -> p (k o)"), a["projT"]),
            (tgam, a["tgam"]), (tbet, a["tbet"]), (projb, a["projb"]),
            (xpw_bc[:, :, 0:2 * NS], a["xpw_bc"]), (xpw_bc[:, :, 2 * NS:4 * NS], a["xpw_bc"]), (xpw_bc[:, :, 4 * NS:6 * NS], a["xpw_bc"]),
            (xpw_dt[:], a["xpw_dt"]), (dtw[:], a["dtw"]), (dtb[:], a["dtb"]),
            (cw[:].rearrange("p o k -> p (o k)"), a["cw"]), (cb[:], a["cb"]), (dskip[:], a["dskip"]),
            (aneg[:].rearrange("p o n -> p (o n)"), a["a_log"]),
            (w_tau[:].rearrange("p s k -> p (s k)"), a["w_tau"].partition_broadcast(128)),
            (b_tau[:].rearrange("p s k -> p (s k)"), a["b_tau"].partition_broadcast(128)),
            (alpha[:], a["alpha"].partition_broadcast(128)),
            (outb[:], a["outb"]), (ln_g[:], a["ln_g"].partition_broadcast(128)), (ln_b[:], a["ln_b"].partition_broadcast(128)),
            (rw[:].rearrange("p k e -> p (k e)"), a["rw"]),
        ]
        LOADED = 16 * len(loads)
        banks = [py[0], py[1], py[2], prep[:, 0, :], prep[:, 1, :], pf[0], pf[1], pq]

        def sp_setup(sp):
            for dst, src in loads:
                if len(dst.shape) == 2 and len(src.shape) == 3:
                    src = src.rearrange("p a k -> p (a k)")
                sp.dma_start(dst, src).then_inc(w_in, 16)

        def pool_setup(gp):
            gp.memset(ones[:], 1.0)
            gp.memset(ident[:], 0.0).then_inc(set_pool, 1)
            gp.memset(spare, 0.0)
            gp.iota(spare_i[:], pattern=[[128, SPARES]], base=2 * NTOK, channel_multiplier=1).then_inc(set_pool, 1)
            gp.wait_ge(set_pool, 2)
            gp.tensor_copy(spare[:, :, D:D + 1], spare_i[:].unsqueeze(2))
            gp.affine_select(out=ident[:], in_=ident[:], compare_op=ALU.not_equal, fill=1.0, base=0, pattern=[[-1, 128]], channel_multiplier=1).then_inc(set_pool, 1)

        def dve_setup(v):
            v.memset(xc[:].rearrange("p d o b l -> p (d o b l)"), 0.0)
            v.memset(zero_cols[:], 0.0)
            v.memset(eps[:], EPS)
            v.memset(halfpi[:], math.pi / 2)
            v.memset(mask[:], 1.0).then_inc(set_dve, 1)
            v.wait_ge(set_dve, 1)
            for q in range(4):
                o = v.memset(mask[LT * q:LT * q + 5, :], 0.0)
            o.then_inc(set_dve, 1)
            v.wait_ge(set_dve, 2)
            v.wait_ge(w_in, LOADED)
            v.tensor_scalar(am[:], alpha[:, 0:2], mask[:], None, ALU.mult)
            v.wait_ge(set_pool, 3)
            for k in range(PD // 128):
                v.tensor_scalar(gw[:, k, :], projT[:, k, :], tgam[:, k:k + 1], None, ALU.mult)
                v.tensor_scalar(betas[:, k, :], ones[:], tbet[:, k:k + 1], None, ALU.mult)
            v.tensor_tensor(sel1, ident[0:96, 0:32], ident[0:96, 32:64], ALU.add).then_inc(set_dve, 1)
            v.wait_ge(set_dve, 3)
            v.tensor_tensor(sel1, sel1, ident[0:96, 64:96], ALU.add).then_inc(set_dve, 1)
            v.wait_ge(set_dve, 4)
            v.tensor_copy(sel[:], sel1).then_inc(set_dve, 1)
            v.wait_ge(set_act, 1)
            v.tensor_scalar(aneg[:], aneg[:], -1.0, None, ALU.mult).then_inc(set_dve, 1)

        def pe_setup(pe):
            pe.wait_ge(w_in, LOADED)
            pe.wait_ge(set_dve, 5)
            i = 0
            for d in range(2):
                for k in range(2):
                    for h in range(2):
                        for j in range(2):
                            mm = pe.matmul(banks[i][0:KH, 0:DI], bm_in[:, d, j, KH * k:KH * k + KH], inT[:, j, DI * h:DI * h + DI], start=(j == 0), stop=(j == 1))
                        mm.then_inc(set_pe, 1)
                        i += 1
            pe.wait_ge(set_act, 9)
            for i in range(NC):
                for j in range(2):
                    pe.matmul(py[i][:, 0:D], outw[:, j, 128 * i:128 * i + 128], bmoT[:, j, :], start=(j == 0), stop=(j == 1))
            for d in range(2):
                for o in range(2 * NC):
                    for j in range(2):
                        pe.matmul(pf[0][:, 2 * NC * d + o:2 * NC * d + o + 1], inT[:, j, 128 * o:128 * o + 128], bm_b[:, d, j:j + 1], start=(j == 0), stop=(j == 1))
            for k in range(PD // 128):
                pe.matmul(pf[1][:, 0:D], ones[:], gw[:, k, :], start=(k == 0), stop=(k == PD // 128 - 1))
            for k in range(PD // 128):
                pe.matmul(pq[:, 0:D], betas[:, k, :], projT[:, k, :], start=(k == 0), stop=False)
            pe.matmul(pq[:, 0:D], ones[0:1, :], projb, start=False, stop=True).then_inc(set_pe, 1)

        def act_setup(act):
            act.wait_ge(w_in, LOADED)
            act.preload_act_table_set("natural_log_exp_and_others")
            act.activation(aneg[:], aneg[:], ACT.Exp).then_inc(set_act, 1)
            i = 0
            for d in range(2):
                for k in range(2):
                    for h in range(2):
                        act.wait_ge(set_pe, i + 1)
                        act.activation(wxz[:, d, k, DI * h:DI * h + DI], banks[i][0:KH, 0:DI], ACT.Copy).then_inc(set_act, 1)
                        i += 1
            act.wait_ge(set_pe, 9)
            for i in range(NC):
                act.activation(w2t[:, i, :], py[i][:, 0:D], ACT.Copy)
            act.activation(bxz[:].rearrange("p d o -> p (d o)"), pf[0][:, 0:4 * NC], ACT.Copy)
            act.activation(proj_sum[:], pf[1][:, 0:D], ACT.Copy)
            act.activation(proj_bias[:], pq[:, 0:D], ACT.Copy).then_inc(set_act, 1)

        def set_up(eng):
            eng.wait_ge(set_dve, 6)
            eng.wait_ge(set_act, 10)
            eng.wait_ge(set_pool, 3)
            eng.wait_ge(w_in, LOADED)

        FRONT = {0: ["load"], 1: ["rows"], 4: ["phase"], 5: ["reduce"], 6: ["sin"], 8: ["img"], 9: ["embed"],
                 10: ["embed_rs"], 11: ["x1", "xT"], 12: ["xT_out"]}
        DIR = {0: ["xz0"], 1: ["xz0_out", "xz1"], 2: ["xz1_out", "xz2", "conv"], 3: ["xz2_out", "silu"], 4: ["bc"],
               5: ["bc_out"], 6: ["split", "dt01"], 7: ["dt01_out", "dt2"], 8: ["dt2_out", "softplus"], 9: ["steps"]}
        BACK = {2: ["out01"], 3: ["out01_add", "out2"], 4: ["out2_add"], 5: ["rs"], 6: ["h2"], 7: ["rs3"], 8: ["x3"],
                9: ["x3T0"], 10: ["x3T0_out", "x3T1"], 11: ["x3T1_out", "router"], 12: ["logits"]}
        GATE = 2 + UD - 1
        REP = -4

        def plan(c, first, last):
            slots = [[] for _ in range(U2)]

            def put(stage, at, chunk, k):
                for w, names in stage.items():
                    slots[at + w] += [(s, chunk, k) for s in names]

            for of_next in (False, True):
                for g in range(2 * NG):
                    for piece in range(4):
                        w = NC * g + REP + piece
                        if w >= 0 and not of_next:
                            slots[w].append(("rep", c, (g, piece)))
                        elif w < 0 and of_next and not last:
                            slots[w].append(("rep", c + 1, (g, piece)))
            put(DIR, 0, c, 1)
            if not first:
                slots[GATE - UD].append(("gate", c - 1, 1))
                put(BACK, 0, c - 1, 0)
            slots[8].append(("keep", c, 0))
            slots[GATE].append(("gate", c, 0))
            if not last:
                put(FRONT, 0, c + 1, 0)
                put(DIR, UD, c + 1, 0)
            for w in range(U2):
                if w + AHEAD < U2:
                    yield "ahead", c, w + AHEAD
                elif not last:
                    yield "ahead", c + 1, w + AHEAD - U2
                yield "scan", c, w
                if w:
                    yield "product", c, w - 1
                elif not first:
                    yield "product", c - 1, U2 - 1
                yield from slots[w]
                if w:
                    yield "sum", c, w - 1
                elif not first:
                    yield "sum", c - 1, U2 - 1

        def in_order(stage, c, k):
            return [(s, c, k) for w in sorted(stage) for s in stage[w]]

        def prologue():
            yield from in_order(FRONT, 0, 0)
            yield from in_order(DIR, 0, 0)
            for g in range(2 * NG):
                for piece in range(4):
                    if NC * g + REP + piece < 0:
                        yield "rep", 0, (g, piece)
            for w in range(AHEAD):
                yield "ahead", 0, w

        def epilogue():
            c = NCH - 1
            yield "product", c, U2 - 1
            yield "sum", c, U2 - 1
            yield "gate", c, 1
            yield from in_order(BACK, c, 0)

        def run(eng, steps, plan_steps):
            for what, c, k in plan_steps:
                if what in steps:
                    steps[what](eng, c, k)

        def program(eng, steps):
            run(eng, steps, prologue())
            run(eng, steps, plan(0, True, False))
            run(eng, steps, plan(1, False, False))
            with eng.Fori(2, NCH - 1) as c:
                run(eng, steps, plan(c, False, False))
            run(eng, steps, plan(NCH - 1, False, True))
            run(eng, steps, epilogue())

        @block.sync
        def _(sp):
            sp_setup(sp)
            sp.wait_ge(set_pool, 3)
            for q in range(SPARES):
                sp.dma_start(dram["xs"].rearrange("(r q) p x -> q p r x", q=SPARES)[q], spare[:, q, :].unsqueeze(1).to_broadcast([128, NJ // SPARES, XW])).then_inc(filled, 16)
            program(sp, {
                "load": lambda e, c, k: sp_front(e, c),
                "h2": lambda e, c, k: sp_back(e, c, "h2"),
                "x3": lambda e, c, k: sp_back(e, c, "x3"),
            })
            sp.wait_ge(h2_out, 16 * NCH)
            sp.wait_ge(x3_out, 16 * NCH)
            sp.wait_ge(filled, 16 * SPARES)

        @block.gpsimd
        def _(gp):
            pool_setup(gp)
            set_up(gp)
            program(gp, {
                "rows": lambda e, c, k: pool_front(e, c),
                "keep": lambda e, c, k: pool_keep(e, c),
                "ahead": pool_unit,
            })

        @block.scalar
        def _(act):
            act_setup(act)
            set_up(act)
            program(act, {
                "sin": lambda e, c, k: act_front1(e, c),
                "embed_rs": lambda e, c, k: act_front2(e, c),
                "xT_out": lambda e, c, k: act_front3(e, c),
                "keep": lambda e, c, k: act_keep(e, c),
                "xz0_out": lambda e, c, d: act_xz(e, c, d, 0),
                "xz1_out": lambda e, c, d: act_xz(e, c, d, 1),
                "xz2_out": lambda e, c, d: act_xz(e, c, d, 2),
                "silu": act_dir2, "bc_out": act_dir3,
                "dt01_out": lambda e, c, d: act_dt(e, c, d, (0, 1)),
                "dt2_out": lambda e, c, d: act_dt(e, c, d, (2,)),
                "softplus": act_soft,
                "rep": lambda e, c, k: act_rep(e, c, *k),
                "ahead": act_unit,
                "rs": lambda e, c, k: act_back1(e, c),
                "rs3": lambda e, c, k: act_back2(e, c),
                "x3T0_out": lambda e, c, k: act_x3T(e, c, 0),
                "x3T1_out": lambda e, c, k: act_x3T(e, c, 1),
            })

        @block.vector
        def _(v):
            dve_setup(v)
            set_up(v)
            program(v, {
                "phase": lambda e, c, k: dve_front1(e, c),
                "reduce": lambda e, c, k: dve_front1b(e, c),
                "embed": lambda e, c, k: dve_front2(e, c),
                "x1": lambda e, c, k: dve_front3(e, c),
                "conv": dve_dir1, "split": dve_dir2, "steps": dve_soft,
                "scan": dve_scan, "product": dve_hc, "gate": dve_gate,
                "out01_add": lambda e, c, k: dve_out(e, c, (0, 1)),
                "out2_add": lambda e, c, k: (dve_out(e, c, (2,)), dve_stat(e, c)),
                "h2": lambda e, c, k: dve_back2(e, c),
                "x3": lambda e, c, k: dve_back3(e, c),
                "logits": lambda e, c, k: dve_router(e, c),
            })

        @block.tensor
        def _(pe):
            pe_setup(pe)
            set_up(pe)
            program(pe, {
                "img": lambda e, c, k: pe_front(e, c),
                "xT": lambda e, c, k: pe_front2(e, c),
                "xz0": lambda e, c, d: pe_xz(e, c, d, 0),
                "xz1": lambda e, c, d: pe_xz(e, c, d, 1),
                "xz2": lambda e, c, d: pe_xz(e, c, d, 2),
                "bc": pe_dir2,
                "dt01": lambda e, c, d: pe_dt(e, c, d, (0, 1)),
                "dt2": lambda e, c, d: pe_dt(e, c, d, (2,)),
                "rep": lambda e, c, k: pe_rep(e, c, *k),
                "sum": pe_unit,
                "out01": lambda e, c, k: pe_out(e, c, (0, 1)),
                "out2": lambda e, c, k: pe_out(e, c, (2,)),
                "x3T0": lambda e, c, k: pe_x3T(e, c, 0),
                "x3T1": lambda e, c, k: pe_x3T(e, c, 1),
                "router": lambda e, c, k: pe_router(e, c),
            })


def build_experts(nc, a, dram, ident, logits, sem, out):
    with ExitStack() as ctx:
        def sb(name, shape, dt=F32):
            return ctx.enter_context(nc.sbuf_tensor(name, shape, dt))

        def pb(name, shape, dt=F32):
            return ctx.enter_context(nc.psum_tensor(name, shape, dt))

        w13 = sb("w13", [KH, E, 2, 2 * HF])
        wd = sb("wd", [128, E, HF // 128, D])
        xe = sb("xe", [128, NTT, XW])
        dest = sb("dest", [128, NTT], I32)
        tri = sb("tri", [128, 128])
        every = sb("every", [128, 128])
        rev_i = sb("rev_i", [128, E], I32)
        rev = sb("rev", [128, E])
        tile_i = sb("tile_i", [1, NJ], I32)
        tile_f = sb("tile_f", [1, NJ])
        cand = sb("cand", [128, NTT, E])
        pick = [sb(f"pick{k}", [128, NTT, E]) for k in range(2)]
        left = sb("left", [128, NTT, E])
        top = [sb(f"top{k}", [128, NTT]) for k in range(2)]
        best = sb("best", [128, NTT])
        both = sb("both", [128, NTT, E])
        totals = sb("totals", [128, E, NTT])
        cum = sb("cum", [128, E, NTT])
        carry_on = sb("carry_on", [128, E, NTT])
        slotmap = sb("slotmap", [128, NTT, E])
        tiles_i = sb("tiles_i", [128, E], I32)
        tiles_f = sb("tiles_f", [128, E])
        ends = sb("ends", [128, E])
        starts = sb("starts", [128, E])
        one8 = sb("one8", [128, E])
        slot_f = sb("slot_f", [128, NTT])
        slot = [sb(f"slot{k}", [128, NTT], I32) for k in range(2)]
        le = sb("le", [1, NJ, E])
        owner_f = sb("owner_f", [1, NJ])
        owner = sb("owner", [1, NJ], I32)
        wt = [sb(f"wt{k}", [128, NTT]) for k in range(2)]
        xs = sb("xs", [128, 2, XW])
        xsT = sb("xsT", [KH, 2, 2, 128])
        act_g = sb("act_g", [128, HF])
        hid = sb("hid", [128, HF])
        hidT = sb("hidT", [128, 2, HF])
        ys = sb("ys", [128, 2, D])
        yidx = sb("yidx", [128, 2], I32)
        yp = sb("yp", [128, 2, NT, 2, D])
        hres = sb("hres", [128, 2, NT, D])

        gu = pb("gu", [128, 2 * HF])
        hps = pb("hps", [128, 1024])
        xps = pb("xps", [128, 512])
        yps = pb("yps", [128, 512])
        cnt = pb("cnt", [128, 512])

        w_in = sem("expert_weights_loaded")
        xe_in = sem("tokens_loaded")
        mk = sem("masks_made")
        mk_v = sem("masks_made_dve")
        rt_a = sem("routing_exp")
        rt_p = sem("routing_counts")
        scattered = sem("tokens_scattered")
        xs_in = [sem(f"slot_tile_loaded{b}") for b in range(2)]
        xt_ps = sem("slot_tile_transposed")
        xt_sb = sem("slot_tile_ready")
        gu_ok = sem("gate_up_done")
        sg_ok = sem("gate_activated")
        hid_ok = sem("hidden_ready")
        ht_ps = sem("hidden_transposed")
        ht_sb = sem("hidden_turned_ready")
        y_ps = sem("down_done")
        y_sb = sem("rows_ready")
        ix_ok = sem("row_places_ready")
        y_out = [sem(f"rows_scattered{b}") for b in range(2)]
        back_in = [sem(f"pairs_loaded{b}") for b in range(2)]
        mix = sem("mixed")
        out_ok = [sem(f"outputs_stored{b}") for b in range(2)]
        passes = {e: sem(f"expert_passes_{e}") for e in ("SP", "Pool", "DVE")}

        def alone(eng):
            eng.sem_inc(passes[eng.engine.name], 1)

        block = ctx.enter_context(nc.Block())
        KT = HF // 128
        j_all = range(NJ)

        def bc_t(x):
            return x.unsqueeze(2).to_broadcast([128, NTT, E])

        def sp_tile(sp, j, b):
            wait(sp, xt_ps, j - 1)
            alone(sp)
            wait(sp, ix_ok, j - 1)
            alone(sp)
            sp.dma_start(xs[:, b, :], dram["xs"][bass.ds(j, 1)].rearrange("a p k -> p (a k)")).then_inc(xs_in[b], 16)

        def pe_xT(pe, j, b, n):
            pe.wait_ge(xs_in[b], 16 * n)
            wait(pe, xt_sb, j)
            for k in range(2):
                mm = pe.transpose(xps[0:KH, 128 * k:128 * k + 128], xs[:, b, KH * k:KH * k + KH], ident[:])
            mm.then_inc(xt_ps, 1)

        def act_xT(act, j, b):
            act.wait_ge(xt_ps, j + 1)
            wait(act, gu_ok, j - 1)
            act.activation(xsT[:, b].rearrange("p k t -> p (k t)"), xps[0:KH, 0:256], ACT.Copy).then_inc(xt_sb, 1)

        def pe_gu(pe, j, b, e):
            pe.wait_ge(xt_sb, j + 1)
            wait(pe, hid_ok, j)
            for n in range(3):
                for k in range(2):
                    mm = pe.matmul(gu[:, 512 * n:512 * n + 512], xsT[:, b, k, :], w13[:, bass.ds(e, 1), k, 512 * n:512 * n + 512].rearrange("p a n -> p (a n)"), start=(k == 0), stop=(k == 1))
            mm.then_inc(gu_ok, 1)

        def act_gate(act, j):
            act.wait_ge(gu_ok, j + 1)
            wait(act, hid_ok, j)
            act.activation(act_g[:], gu[:, 0:HF], ACT.Silu).then_inc(sg_ok, 1)

        def dve_hid(v, j):
            v.wait_ge(sg_ok, j + 1)
            wait(v, ht_ps, j)
            v.tensor_tensor(hid[:], act_g[:], gu[:, HF:2 * HF], ALU.mult).then_inc(hid_ok, 1)

        def pe_hT(pe, j):
            pe.wait_ge(hid_ok, j + 1)
            wait(pe, ht_sb, j)
            for k in range(KT):
                mm = pe.transpose(hps[:, 128 * k:128 * k + 128], hid[:, 128 * k:128 * k + 128], ident[:])
            mm.then_inc(ht_ps, 1)

        def act_hT(act, j, b):
            act.wait_ge(ht_ps, j + 1)
            wait(act, y_ps, j - 1)
            act.activation(hidT[:, b, :], hps[:, 0:HF], ACT.Copy).then_inc(ht_sb, 1)

        def pe_down(pe, j, b, e):
            pe.wait_ge(ht_sb, j + 1)
            wait(pe, y_sb, j)
            for k in range(KT):
                mm = pe.matmul(yps[:, 0:D], hidT[:, b, 128 * k:128 * k + 128], wd[:, bass.ds(e, 1), k, :].rearrange("p a n -> p (a n)"), start=(k == 0), stop=(k == KT - 1))
            mm.then_inc(y_ps, 1)

        def dve_y(v, j, b, n):
            v.wait_ge(y_ps, j + 1)
            wait(v, y_out[b], 16 * n)
            v.tensor_copy(ys[:, b, :], yps[:, 0:D]).then_inc(y_sb, 1)

        def dve_idx(v, j, b, n):
            v.wait_ge(xs_in[b], 16 * n + 16)
            wait(v, y_out[b], 16 * n)
            v.tensor_copy(yidx[:, b:b + 1], xs[:, b, D:D + 1]).then_inc(ix_ok, 1)

        def pool_y(gp, j, b):
            gp.wait_ge(ix_ok, j + 1)
            gp.wait_ge(y_sb, j + 1)
            alone(gp)
            gp.indirect_dma_start(dram["pairs"], bass.IndirectOffsetOnAxis(ap=yidx[:, b:b + 1], axis=0), ys[:, b, :], None).then_inc(y_out[b], 16)

        def owner_of(pe, j):
            return pe.value_load(owner[0:1, bass.ds(j, 1)], min_val=0, max_val=E - 1)

        def sp_pairs(sp, c, b, n):
            wait(sp, mix, 2 * c - 2)
            alone(sp)
            sp.dma_start(yp[:, b].rearrange("p t k d -> p t (k d)"), rows_of(dram["pairs"], c)).then_inc(back_in[b], 16)
            wait(sp, out_ok[b], 16 * n)
            alone(sp)
            sp.dma_start(hres[:, b].rearrange("p t d -> p (t d)"), dram["h2"][bass.ds(c, 1)].rearrange("a p k -> p (a k)")).then_inc(back_in[b], 16)

        def rows_of(pairs, c):
            return pairs[0:2 * NTOK, :].rearrange("(c t p k) d -> c p t (k d)", c=NCH, t=NT, p=128)[bass.ds(c, 1)].rearrange("a p t q -> p (a t) q")

        def dve_mix(v, c, b, n):
            v.wait_ge(back_in[b], 32 * n + 32)
            for k in range(2):
                if k:
                    v.wait_ge(mix, 2 * c + 1)
                for t in range(NT):
                    o = v.scalar_tensor_tensor(hres[:, b, t, :], yp[:, b, t, k, :], wt[k][:, bass.ds(NT * c + t, 1)], hres[:, b, t, :], ALU.mult, ALU.add)
                o.then_inc(mix, 1)

        def sp_store(sp, c, b):
            sp.wait_ge(mix, 2 * c + 2)
            alone(sp)
            sp.dma_start(out[bass.ds(c, 1)].rearrange("a p k -> p (a k)"), hres[:, b].rearrange("p t d -> p (t d)")).then_inc(out_ok[b], 16)

        rv = Steps(sem("routing_dve"), "max0 eq0 cand0 best0 pick0 left max1 eq1 cand1 best1 pick1 both diff den w0 w1 "
                   "totals cum tiles0 tiles1 tiles2 ends starts excl off map s0 slots0 place0 s1 slots1 place1 ge sum owner")

        def turn(v, op, name):
            op.then_inc(rv.sem, 1)
            v.wait_ge(rv.sem, rv.after(name, 0))

        def dve_route(v):
            def by_expert(x):
                return x[:].unsqueeze(1).to_broadcast([128, NTT, E])

            v.wait_ge(mk, 3)
            v.tensor_copy(rev[:], rev_i[:])
            v.tensor_copy(tile_f[:], tile_i[:])
            v.memset(one8[:], 1.0)
            v.memset(carry_on[:], 1.0)
            v.memset(xe[:, :, D:XW], 0.0).then_inc(mk_v, 1)
            v.wait_ge(mk_v, 1)
            v.memset(carry_on[:, :, 0:1], 0.0)
            v.tensor_copy(xe[:, :, D:D + 1], dest[:].unsqueeze(2)).then_inc(mk_v, 1)
            v.wait_ge(mk_v, 2)
            src = logits
            for k in range(2):
                turn(v, v.tensor_reduce(top[k][:], src[:], AX.X, ALU.max), f"max{k}")
                turn(v, v.tensor_tensor(both[:], src[:], bc_t(top[k][:]), ALU.is_equal), f"eq{k}")
                turn(v, v.tensor_tensor(cand[:], both[:], by_expert(rev), ALU.mult), f"cand{k}")
                turn(v, v.tensor_reduce(best[:], cand[:], AX.X, ALU.max), f"best{k}")
                turn(v, v.tensor_tensor(pick[k][:], cand[:], bc_t(best[:]), ALU.is_equal), f"pick{k}")
                if k == 0:
                    turn(v, v.scalar_tensor_tensor(left[:], pick[0][:], -3.0e38, logits[:], ALU.mult, ALU.add), "left")
                    src = left
            turn(v, v.tensor_tensor(both[:], pick[0][:], pick[1][:], ALU.add), "both")
            turn(v, v.tensor_tensor(wt[1][:], top[1][:], top[0][:], ALU.subtract), "diff")
            v.wait_ge(rt_a, 1)
            turn(v, v.tensor_scalar(slot_f[:], wt[1][:], 1.0, None, ALU.add), "den")
            turn(v, v.reciprocal(wt[0][:], slot_f[:]), "w0")
            turn(v, v.tensor_tensor(wt[1][:], wt[1][:], wt[0][:], ALU.mult), "w1")
            v.wait_ge(rt_p, 1)
            turn(v, v.tensor_copy(totals[:], cnt[:, NTT * E:2 * NTT * E].rearrange("p (t e) -> p e t", e=E)), "totals")
            turn(v, v.tensor_tensor_scan(cum[:].rearrange("p e t -> p (e t)"), carry_on[:].rearrange("p e t -> p (e t)"), totals[:].rearrange("p e t -> p (e t)"), 0.0, ALU.mult, ALU.add), "cum")
            turn(v, v.tensor_scalar(tiles_i[:].unsqueeze(2), cum[:, :, NTT - 1:NTT], 127.0, None, ALU.add), "tiles0")
            turn(v, v.tensor_scalar(tiles_i[:], tiles_i[:], 7, None, ALU.arith_shift_right), "tiles1")
            turn(v, v.tensor_copy(tiles_f[:], tiles_i[:]), "tiles2")
            turn(v, v.tensor_tensor_scan(ends[:], one8[:], tiles_f[:], 0.0, ALU.mult, ALU.add), "ends")
            turn(v, v.tensor_tensor(starts[:], ends[:], tiles_f[:], ALU.subtract), "starts")
            turn(v, v.tensor_tensor(cum[:], cum[:], totals[:], ALU.subtract), "excl")
            turn(v, v.scalar_tensor_tensor(cum[:], starts[:].unsqueeze(2).to_broadcast([128, E, NTT]), 128.0, cum[:], ALU.mult, ALU.add), "off")
            turn(v, v.tensor_tensor(slotmap[:], cnt[:, 0:NTT * E].rearrange("p (t e) -> p t e", e=E), cum[:].rearrange("p e t -> p t e"), ALU.add), "map")
            for k in range(2):
                turn(v, v.tensor_tensor(cand[:], pick[k][:], slotmap[:], ALU.mult), f"s{k}")
                turn(v, v.tensor_reduce(slot_f[:], cand[:], AX.X, ALU.add), f"slots{k}")
                turn(v, v.tensor_copy(slot[k][:], slot_f[:]), f"place{k}")
            turn(v, v.tensor_tensor(le[:], tile_f[:].unsqueeze(2).to_broadcast([1, NJ, E]), ends[0:1, :].unsqueeze(1).to_broadcast([1, NJ, E]), ALU.is_ge), "ge")
            turn(v, v.tensor_reduce(owner_f[:], le[:], AX.X, ALU.add), "sum")
            turn(v, v.tensor_scalar(owner[:], owner_f[:], float(E - 1), None, ALU.min), "owner")
            v.wait_ge(scattered, 16 * NTT)
            v.tensor_scalar(xe[:, :, D:D + 1], xe[:, :, D:D + 1], 1.0, None, ALU.add).then_inc(mk_v, 1)

        LAST = NJ - 1

        @block.sync
        def _(sp):
            for c in range(NCH):
                sp.dma_start(xe[:, NT * c:NT * c + NT, 0:D], dram["x3"][c].rearrange("p (t d) -> p t d", d=D)).then_inc(xe_in, 16)
            for e in range(E):
                sp.dma_start(w13[:, e].rearrange("p k n -> p (k n)"), a["w13"][:, e, :]).then_inc(w_in, 16)
                sp.dma_start(wd[:, e].rearrange("p k n -> p (k n)"), a["wd"][:, e, :]).then_inc(w_in, 16)
            sp.wait_ge(scattered, 16 * 2 * NTT)
            for j in range(2):
                sp_tile(sp, j, j)
            with sp.Fori(1, NJ // 2) as i:
                for b in range(2):
                    sp_tile(sp, 2 * i + b, b)
            sp_tile(sp, LAST, 0)
            for b in range(2):
                sp.wait_ge(y_out[b], 16 * (NJ // 2 + 1 - b))
            for c in range(2):
                sp_pairs(sp, c, c, 0)
            with sp.Fori(1, NCH // 2) as i:
                for b in range(2):
                    sp_store(sp, 2 * i - 2 + b, b)
                    sp_pairs(sp, 2 * i + b, b, i)
            for b in range(2):
                sp_store(sp, NCH - 2 + b, b)
            for b in range(2):
                sp.wait_ge(out_ok[b], 16 * (NCH // 2))

        @block.gpsimd
        def _(gp):
            gp.iota(rev_i[:], pattern=[[-1, E]], base=E, channel_multiplier=0)
            gp.iota(tile_i[:], pattern=[[1, NJ]], base=0, channel_multiplier=0)
            gp.iota(dest[:], pattern=[[256, NTT]], base=0, channel_multiplier=2)
            gp.memset(every[:], 1.0).then_inc(mk, 1)
            gp.wait_ge(mk, 1)
            gp.affine_select(out=tri[:], in_=every[:], compare_op=ALU.is_gt, fill=0.0, base=0, pattern=[[1, 128]], channel_multiplier=-1).then_inc(mk, 1)
            gp.wait_ge(mk, 2)
            gp.sem_inc(mk, 1)
            gp.wait_ge(mk_v, 2)
            gp.wait_ge(xe_in, 16 * NCH)
            for k in range(2):
                gp.wait_ge(rv.sem, rv.after(f"place{k}", 0))
                if k:
                    gp.wait_ge(mk_v, 3)
                for t in range(NTT):
                    gp.indirect_dma_start(dram["xs"].rearrange("j p x -> (j p) x"), bass.IndirectOffsetOnAxis(ap=slot[k][:, t:t + 1], axis=0), xe[:, t, :], None).then_inc(scattered, 16)
            for b in range(2):
                pool_y(gp, b, b)
            with gp.Fori(1, NJ // 2) as i:
                for b in range(2):
                    pool_y(gp, 2 * i + b, b)
            pool_y(gp, LAST, 0)

        @block.scalar
        def _(act):
            act.wait_ge(rv.sem, rv.after("diff", 0))
            act.activation(wt[1][:], wt[1][:], ACT.Exp).then_inc(rt_a, 1)
            act_xT(act, 0, 0)

            def tile(j, b):
                act_gate(act, j)
                act_xT(act, j + 1, 1 - b)
                act_hT(act, j, b)

            for b in range(2):
                tile(b, b)
            with act.Fori(1, NJ // 2) as i:
                for b in range(2):
                    tile(2 * i + b, b)
            act_gate(act, LAST)
            act_hT(act, LAST, 0)

        @block.vector
        def _(v):
            dve_route(v)
            dve_hid(v, 0)
            dve_idx(v, 0, 0, 0)
            dve_hid(v, 1)
            dve_y(v, 0, 0, 0)
            dve_idx(v, 1, 1, 0)
            with v.Fori(1, NJ // 2) as i:
                for b in range(2):
                    dve_hid(v, 2 * i + b)
                    dve_y(v, 2 * i + b - 1, 1 - b, i - 1 + b)
                    dve_idx(v, 2 * i + b, b, i)
            dve_hid(v, LAST)
            dve_y(v, LAST - 1, 1, LAST // 2 - 1)
            dve_idx(v, LAST, 0, LAST // 2)
            dve_y(v, LAST, 0, LAST // 2)
            for b in range(2):
                dve_mix(v, b, b, 0)
            with v.Fori(1, NCH // 2) as i:
                for b in range(2):
                    dve_mix(v, 2 * i + b, b, i)

        @block.tensor
        def _(pe):
            pe.wait_ge(mk, 2)
            pe.wait_ge(rv.sem, rv.after("both", 0))
            pe.matmul(cnt[:, 0:NTT * E], tri[:], both[:].rearrange("p t e -> p (t e)"), start=True, stop=True)
            pe.matmul(cnt[:, NTT * E:2 * NTT * E], every[:], both[:].rearrange("p t e -> p (t e)"), start=True, stop=True).then_inc(rt_p, 1)
            pe.wait_ge(w_in, 16 * 2 * E)
            pe.wait_ge(rv.sem, rv.after("owner", 0))
            pe_xT(pe, 0, 0, 1)
            e0 = owner_of(pe, 0)
            pe_gu(pe, 0, 0, e0)
            pe_xT(pe, 1, 1, 1)
            pe_hT(pe, 0)
            pe_gu(pe, 1, 1, owner_of(pe, 1))
            pe_down(pe, 0, 0, owner_of(pe, 0))
            pe_xT(pe, 2, 0, 2)
            pe_hT(pe, 1)
            with pe.Fori(1, NJ // 2) as i:
                for b in range(2):
                    j = 2 * i + b
                    pe_gu(pe, j, b, owner_of(pe, j))
                    pe_down(pe, j - 1, 1 - b, owner_of(pe, j - 1))
                    pe_xT(pe, j + 1, 1 - b, i + 1 + b)
                    pe_hT(pe, j)
            pe_gu(pe, LAST, 0, owner_of(pe, LAST))
            pe_down(pe, LAST - 1, 1, owner_of(pe, LAST - 1))
            pe_hT(pe, LAST)
            pe_down(pe, LAST, 0, owner_of(pe, LAST))


INPUTS = ["p_tok", "p_T", "ids", "taus", "tok_emb", "seg_emb", "w_tau", "b_tau", "alpha", "projT", "tgam", "tbet", "projb",
          "bm_in", "bm_b", "inT", "outw", "bmoT", "xpw_bc", "xpw_dt", "dtw", "dtb", "cw", "cb", "dskip", "a_log",
          "outb", "ln_g", "ln_b", "rw", "w13", "wd"]


def fusion_block(nc, a, out):
    dram = {
        "h2": nc.dram_tensor("h2_scratch", [NCH, 128, NT * D], F32, kind="Internal").ap(),
        "x3": nc.dram_tensor("x3_scratch", [NCH, 128, NT * D], F32, kind="Internal").ap(),
        "xs": nc.dram_tensor("slot_rows", [NJ, 128, XW], F32, kind="Internal").ap(),
        "pairs": nc.dram_tensor("result_rows", [2 * NTOK + 128 * SPARES, D], F32, kind="Internal").ap(),
    }
    with ExitStack() as ctx:
        def sem(name):
            return ctx.enter_context(nc.semaphore(name))

        ident = ctx.enter_context(nc.sbuf_tensor("ident", [128, 128], F32))
        logits = ctx.enter_context(nc.sbuf_tensor("logits", [128, NTT, E], F32))
        build_mamba(nc, a, dram, ident, logits, sem)
        build_experts(nc, a, dram, ident, logits, sem, out)


def lay_out(f):
    import numpy as np

    def rows(x, p):
        x = x.reshape(-1, p, *x.shape[1:])
        return np.moveaxis(x, 1, 0).reshape(p, -1)

    patches = f["x"].reshape(B, 3, 4, 16, 4, 16).transpose(0, 2, 4, 3, 5, 1).reshape(NCH, 128, PD)

    def texts(x):
        return x.reshape(NCH, 2, 128)

    xpw = f["L0_attn_m_xproj_w"].T
    row = lambda n: f[n].reshape(1, -1)
    column = lambda n, p: rows(f[n].reshape(-1, 1), p)
    a = {
        "p_tok": patches,
        "p_T": patches.reshape(NCH, 128, PD // 128, 128).transpose(0, 3, 2, 1).reshape(NCH, 128, PD),
        "ids": np.concatenate([texts(f["x_txt"]), texts(f["itok_BS_0_3"])], 1).transpose(0, 2, 1),
        "taus": np.concatenate([texts(f["fside_BS_age"]), texts(f["fside_BS_position"])], 1).transpose(0, 2, 1),
        "tok_emb": f["L0_txt_token_emb"], "seg_emb": f["L0_txt_seg_emb"],
        "w_tau": np.concatenate([f["L0_txt_w_age"], f["L0_txt_w0_age"], f["L0_txt_w_abs"], f["L0_txt_w0_abs"]], 1),
        "b_tau": np.concatenate([f["L0_txt_b_age"], f["L0_txt_b0_age"], f["L0_txt_b_abs"], f["L0_txt_b0_abs"]], 1),
        "alpha": np.stack([f["L0_txt_alpha_age"], f["L0_txt_alpha_abs"], f["L0_txt_alpha_seg"]]).reshape(1, 3),
        "projT": rows(f["L0_tok_W_proj"].T, 128), "tgam": column("L0_tok_gamma", 128), "tbet": column("L0_tok_beta", 128),
        "projb": row("L0_tok_b_proj"),
        "bm_in": rows(f["L0_attn_bm_in_w"], KH), "bm_b": column("L0_attn_bm_in_b", KH), "inT": rows(f["L0_attn_m_in_w"].T, KH),
        "outw": rows(f["L0_attn_m_out_w"], KH), "bmoT": rows(f["L0_attn_bm_out_w"].T, KH),
        "xpw_bc": rows(xpw[:, R:], 128).reshape(128, NC, 2 * NS), "xpw_dt": rows(xpw[:, :R], 128).reshape(128, NC, R),
        "dtw": f["L0_attn_m_dt_w"].T, "dtb": column("L0_attn_m_dt_b", 128),
        "cw": rows(f["L0_attn_m_conv_w"], 128), "cb": column("L0_attn_m_conv_b", 128),
        "dskip": column("L0_attn_m_D", 128), "a_log": rows(f["L0_attn_m_A_log"], 128),
        "outb": row("L0_attn_bm_out_b"), "ln_g": row("L0_attn_ln_g"), "ln_b": row("L0_attn_ln_b"),
        "rw": rows(f["L0_ffn_router_w"].T, KH),
        "w13": np.stack([f["L0_ffn_Wg"], f["L0_ffn_Wu"]], 1).reshape(E, 2, HF, 2, KH).transpose(4, 0, 3, 1, 2).reshape(KH, E, 4 * HF),
        "wd": f["L0_ffn_Wd"].reshape(E, D, HF // 128, 128).transpose(3, 0, 2, 1).reshape(128, E, (HF // 128) * D),
    }
    return {n: np.ascontiguousarray(x) for n, x in a.items()}


def kernel(**inputs):
    import numpy as np
    import concourse.bacc as bacc
    from concourse.bass_utils import run_bass_kernel_spmd

    nc = bacc.Bacc("TRN2", target_bir_lowering=False, num_devices=1)
    laid = lay_out({n: np.asarray(x) for n, x in inputs.items()})
    args = {n: nc.dram_tensor(f"in_{n}", laid[n].shape, mybir.dt.from_np(laid[n].dtype), kind="ExternalInput").ap() for n in INPUTS}
    out = nc.dram_tensor("out_tokens", [NCH, 128, NT * D], F32, kind="ExternalOutput").ap()
    fusion_block(nc, args, out)
    r = run_bass_kernel_spmd(nc, [{f"in_{n}": laid[n] for n in INPUTS}], core_ids=[0])
    y = np.asarray(r.results[0]["out_tokens"]).reshape(NCH, 128, NT, D)
    image = y[:, :, 0].reshape(NCH, CB, LI, D)
    text = y[:, :, 1:].transpose(0, 2, 1, 3).reshape(NCH, CB, LT, D)
    return np.concatenate([image, text], 2).reshape(B, L, D)
```

```python
from contextlib import ExitStack
import math

import concourse.bass as bass
from concourse import mybir

F32 = mybir.dt.float32
BF16 = mybir.dt.bfloat16
I32 = mybir.dt.int32
ALU = mybir.AluOpType
ACT = mybir.ActivationFunctionType
AX = mybir.AxisListType

B, L, LI, LT = 64, 48, 16, 32
D, DI, NS, R = 192, 384, 16, 12
KH = D // 2
PD = 768
CB = 8
NCH = B // CB
T = CB * L
NT = T // 128
NC = DI // 128
NG = 4
GN = NS // NG
UD = NG * NC
U2 = 2 * UD
NRING = 6
NDA = 3
AHEAD = 2
KC = 3
EPS = 1e-5
E, HF = 8, 768
NTOK = B * L
NTT = NTOK // 128
NJ = 2 * NTT + E - 1
XW = D + 4

TWO_PI = 2 * math.pi
C1 = 6.28125
C2 = 0.0019350051879882812
C3 = TWO_PI - C1 - C2
MAGIC = 12582912.0
PI_IN = 3.1415925


class Steps:

    def __init__(self, sem, names):
        self.sem, self.names = sem, names.split()

    def after(self, name, turn):
        return len(self.names) * turn + self.names.index(name) + 1


def wait(eng, sem, value):
    if isinstance(value, int) and value <= 0:
        return
    eng.wait_ge(sem, value)


def build_mamba(nc, a, dram, ident, logits, sem):
    with ExitStack() as ctx:
        def sb(name, shape, dt=F32):
            return ctx.enter_context(nc.sbuf_tensor(name, shape, dt))

        def pb(name, shape, dt=F32):
            return ctx.enter_context(nc.psum_tensor(name, shape, dt))

        ones = sb("ones", [128, 128])
        sel = sb("sel", [96, 2 * NS], BF16)
        wxz = sb("wxz", [KH + 1, 2, 2, 2 * DI])
        gw = sb("gw", [128, PD // 128, D])
        proj_sum = sb("proj_sum", [128, D])
        proj_bias = sb("proj_bias", [128, D])
        w2t = sb("w2t", [128, NC, D])
        xpw = sb("xpw", [128, NC, 96 + R])
        dtw = sb("dtw", [96 + R, DI])
        dtb = sb("dtb", [128, NC])
        cw = sb("cw", [128, NC, KC + 1])
        cb = sb("cb", [128, NC])
        dskip = sb("dskip", [128, NC])
        skip_diag = sb("skip_diag", [128, NC, 128])
        aneg = sb("aneg", [128, NC, NS])
        w_tau = sb("w_tau", [128, 2, D])
        b_tau = sb("b_tau", [128, 2, D])
        alpha = sb("alpha", [128, 3])
        mask = sb("mask", [128, 1])
        am = sb("am", [128, 2])
        outb = dtw[0:1, 0:D]
        ln_g = sb("ln_g", [128, D])
        ln_b = sb("ln_b", [128, D])
        rw = sb("rw", [KH, 2, E])
        eps = sb("eps", [128, 1])
        spare_i = sb("spare_i", [128, 1], I32)
        halfpi = sb("halfpi", [128, 1])
        ptok = sb("ptok", [128, PD])
        pT = sb("pT", [128, PD // 128, 128])
        ids = sb("ids", [128, 4], I32)
        taus = sb("taus", [128, 4])
        tok_rows = sb("tok_rows", [128, 2, D])
        seg_rows = sb("seg_rows", [128, 2, D])
        theta = sb("theta", [128, 2, 2, D])
        turns = sb("turns", [128, 2, 2, D])
        resid = sb("resid", [128, 2, 2, D])
        img_t = sb("img_t", [128, D])
        pst = sb("pst", [128, 2, 6])
        pmv = sb("pmv", [128, 2])
        pneg = sb("pneg", [128, 1])
        prs = sb("prs", [128, 2])
        hst = sb("hst", [128, NT, 6])
        hmv = sb("hmv", [128, NT, 2])
        hrs = sb("hrs", [128, 2, NT])
        h_new = sb("h_new", [128, NT, D])
        x1_new = sb("x1_new", [128, NT, D])
        xT = sb("xT", [KH + 1, 2, CB, L])
        xc = sb("xc", [128, NC, CB, KC + L + KC])
        u = sb("u", [128, 2, NC, T])
        zs = sb("zs", [128, 2, NC, T])
        dt_ = sb("dt_", [128, 2, NC, T])
        dtu = sb("dtu", [128, 2, NC, T])
        stk = sb("stk", [96, 2, T], BF16)
        mid = sb("mid", [96, T], BF16)
        rr = sb("rr", [96, T])
        dtx = sb("dtx", [96 + R, T])
        ea = sb("ea", [128, NC, T])
        da = sb("da", [128, NDA, GN, T])
        ring = sb("ring", [128, NRING, GN, T])
        zero_cols = sb("zero_cols", [128, GN * CB])
        brep = sb("brep", [128, 2, GN, T])
        crep = sb("crep", [128, 2, GN, T])
        yg = sb("yg", [128, 2, NC, T])
        hb = sb("hb", [128, NT, D])
        hb_next = sb("hb_next", [128, NT, D])
        x1 = sb("x1", [128, NT, D])
        h2 = sb("h2", [128, NT, D])
        x3 = sb("x3", [128, NT, D])
        qst = sb("qst", [128, NT, 6])
        qmv = sb("qmv", [128, NT, 2])
        qrs = sb("qrs", [128, 2, NT])
        x3T = turns[0:KH].rearrange("p s t k -> p (s t k)").rearrange("p (k t) -> p k t", k=2)
        spare = yg[:].rearrange("p d o t -> p (d o t)")[:, 0:XW]
        bm_in = ring[0:KH, 0, :, :].rearrange("p n t -> p (n t)")[:, 0:2 * 2 * (D + 1)].rearrange("p (d j k) -> p d j k", d=2, j=2)
        inT = ring[0:KH, 1, :, :].rearrange("p n t -> p (n t)")[:, 0:2 * 2 * DI].rearrange("p (j o) -> p j o", j=2)
        outw = ring[0:KH, 2, :, :].rearrange("p n t -> p (n t)")[:, 0:2 * DI].rearrange("p (j o) -> p j o", j=2)
        bmoT = ring[0:KH, 3, :, :].rearrange("p n t -> p (n t)")[:, 0:2 * D].rearrange("p (j o) -> p j o", j=2)
        projT = brep[:, 0, :, :].rearrange("p n t -> p (n t)")[:, 0:6 * D].rearrange("p (k o) -> p k o", k=6)
        tgam = crep[:, 0, 0, 0:6]
        tbet = crep[:, 0, 0, 8:14]
        betas = crep[:, 1, :, :].rearrange("p n t -> p (n t)")[:, 0:768].rearrange("p (k m) -> p k m", k=6)
        projb = crep[0:1, 0, 1, 0:D]
        sel1 = da[0:96, 0, 0, 0:2 * NS]

        py = [pb(f"py{i}", [128, 512]) for i in range(NC)]
        prep = pb("prep", [128, 2, 512])
        pf = [pb(f"pf{i}", [128, 512]) for i in range(2)]
        pq = pb("pq", [128, 512])

        fold_in = sem("folded_weights_loaded")
        w_in = sem("weights_loaded")
        set_pool = sem("setup_pool")
        set_dve = sem("setup_dve")
        set_pe = sem("setup_pe")
        set_act = sem("setup_act")
        patch_in = sem("patches_loaded")
        ids_in = sem("ids_loaded")
        rows_in = sem("rows_gathered")
        rep_ps = sem("rep_in_psum")
        rep_sb = sem("rep_in_sbuf")
        da_ok = sem("decay_ready")
        dtu_ok = sem("step_times_input")
        dbu_ok = sem("dbu_ready")
        scan_ok = sem("scan_done")
        hc_ok = sem("hc_ready")
        y_ok = sem("states_summed")
        gated = sem("y_gated")
        hb_next_ok = sem("h_taken")
        hb_ok = sem("h_kept")
        x1_ok = sem("x1_kept")
        full = [sem(f"front{i}_filled") for i in range(2)]
        free = [sem(f"front{i}_freed") for i in range(2)]
        qfull = sem("back_filled")
        qfree = sem("back_freed")
        img_ps = sem("image_projected")
        img_sb = sem("image_evacuated")
        passes = {e: sem(f"passes_{e}") for e in ("SP", "Pool", "DVE")}
        h2_out = sem("h2_stored")
        filled = sem("slots_filled")
        x3_out = sem("x3_stored")
        fv = Steps(sem("front_dve"), "pstat paggr pneg res1 res2 res3 clamp img txt1 txt2 txt3 hstat haggr x1")
        fp = Steps(sem("front_pool"), "scaled theta turn round")
        fa = Steps(sem("front_act"), "lnp rsp sin lin lnh rsh")
        dv = Steps(sem("dir_dve"), "conv0a conv1a conv2a conv0b conv1b conv2b split2 split3 m w1 r dt")
        ds = Steps(sem("dir_act"), "silu x0 exp0 x1 exp1 ln")
        qv = Steps(sem("back_dve"), "stat aggr stat3 aggr3")
        qp = Steps(sem("back_pool"), "norm gain h2 x3")
        qa = Steps(sem("back_act"), "ln rs ln3 rs3")

        FJOBS = [("xT0", 1), ("xT1", 1)]
        for d in range(2):
            x, z = ([(f"xz{d}_{NC * i + o}", 1) for o in range(NC)] for i in range(2))
            rest = [(f"bc{d}", 2)] + [(f"dt{d}_{o}", 1) for o in range(NC)]
            FJOBS += x + rest + z if d == 0 else x + z[:2] + rest + z[2:]
        JOB = {}
        nfull, nfree = [0, 0], [0, 0]
        for i, (name, readers) in enumerate(FJOBS):
            b = i % 2
            JOB[name] = (b, nfull[b], nfree[b])
            nfull[b] += 1
            nfree[b] += readers

        def job_start(pe, name, c):
            b, _, fr = JOB[name]
            wait(pe, free[b], nfree[b] * c + fr)
            return pf[b]

        def job_wait(eng, name, c):
            b, fu, _ = JOB[name]
            eng.wait_ge(full[b], nfull[b] * c + fu + 1)
            return pf[b]

        def job_read(eng, name, c):
            b, _, fr = JOB[name]
            eng.wait_ge(free[b], nfree[b] * c + fr + dict(FJOBS)[name])

        def jsem(name, which):
            return (full if which == "full" else free)[JOB[name][0]]

        QJ = 5

        def alone(eng):
            eng.sem_inc(passes[eng.engine.name], 1)

        def sp_load(sp, c):
            if not isinstance(c, int) or c > 0:
                wait(sp, fp.sem, fp.after("theta", c - 1))
                alone(sp)
                wait(sp, fv.sem, fv.after("pstat", c - 1))
                alone(sp)
                wait(sp, img_ps, c)
                alone(sp)
                wait(sp, rows_in, 64 * c)
                alone(sp)
            sp.dma_start(ids[:], a["ids"][bass.ds(c, 1)].rearrange("a p k -> p (a k)")).then_inc(ids_in, 16)
            sp.dma_start(taus[:], a["taus"][bass.ds(c, 1)].rearrange("a p k -> p (a k)")).then_inc(ids_in, 16)
            sp.dma_start(ptok[:], a["p_tok"][bass.ds(c, 1)].rearrange("a p k -> p (a k)")).then_inc(patch_in, 16)
            sp.dma_start(pT[:].rearrange("p k t -> p (k t)"), a["p_T"][bass.ds(c, 1)].rearrange("a p k -> p (a k)")).then_inc(patch_in, 16)

        def pool_rows(gp, c):
            gp.wait_ge(ids_in, 32 * c + 32)
            wait(gp, fv.sem, fv.after("txt3", c - 1))
            alone(gp)
            for t in range(2):
                gp.indirect_dma_start(tok_rows[:, t, :], None, a["tok_emb"], bass.IndirectOffsetOnAxis(ap=ids[:, t:t + 1], axis=0)).then_inc(rows_in, 16)
                gp.indirect_dma_start(seg_rows[:, t, :], None, a["seg_emb"], bass.IndirectOffsetOnAxis(ap=ids[:, 2 + t:3 + t], axis=0)).then_inc(rows_in, 16)

        def pool_keep(gp, c):
            gp.wait_ge(fv.sem, fv.after("x1", c))
            wait(gp, hb_ok, c)
            gp.tensor_tensor(hb_next[:], h_new[:], ln_b[:].unsqueeze(1).to_broadcast([128, NT, D]), ALU.add).then_inc(hb_next_ok, 1)

        def pool_kept(gp, c):
            gp.wait_ge(hb_next_ok, c + 1)
            wait(gp, qp.sem, qp.after("h2", c - 1))
            alone(gp)
            gp.tensor_copy(hb[:], hb_next[:]).then_inc(hb_ok, 1)

        def act_keep(act, c):
            act.wait_ge(fv.sem, fv.after("x1", c))
            wait(act, qfree, QJ * (c - 1) + 2)
            act.activation(x1[:], x1_new[:], ACT.Copy).then_inc(x1_ok, 1)

        def pe_img(pe, c):
            pe.wait_ge(patch_in, 32 * c + 32)
            wait(pe, qfree, QJ * (c - 2) + 2)
            for k in range(PD // 128):
                mm = pe.matmul(pq[:, 0:D], pT[:, k, :], gw[:, k, :], start=(k == 0), stop=(k == PD // 128 - 1))
            mm.then_inc(img_ps, 1)

        def dve_patch_stats(v, c):
            v.wait_ge(patch_in, 32 * c + 32)
            wait(v, fv.sem, fv.after("paggr", c - 1))
            for i in range(2):
                o = v.bn_stats(pst[:, i, :], ptok[:, 384 * i:384 * i + 384])
            o.then_inc(fv.sem, 1)
            v.wait_ge(fv.sem, fv.after("pstat", c))
            wait(v, fa.sem, fa.after("lnp", c - 1))
            alone(v)
            v.bn_aggr(pmv[:], pst[:].rearrange("p a k -> p (a k)")).then_inc(fv.sem, 1)
            v.wait_ge(fv.sem, fv.after("paggr", c))
            v.tensor_scalar(pneg[:], pmv[:, 0:1], -1.0, None, ALU.mult).then_inc(fv.sem, 1)

        def pool_phase(gp, c):
            gp.wait_ge(ids_in, 32 * c + 32)
            wait(gp, fa.sem, fa.after("lin", c - 1))
            alone(gp)
            wait(gp, fv.sem, fv.after("res3", c - 1))
            alone(gp)
            for s in range(2):
                for t in range(2):
                    o = gp.tensor_scalar(theta[:, s, t, :], w_tau[:, s, :], taus[:, 2 * s + t:2 * s + t + 1], None, ALU.mult)
            o.then_inc(fp.sem, 1)
            gp.wait_ge(fp.sem, fp.after("scaled", c))
            for s in range(2):
                o = gp.tensor_tensor(theta[:, s], theta[:, s], b_tau[:, s, :].unsqueeze(1).to_broadcast([128, 2, D]), ALU.add)
            o.then_inc(fp.sem, 1)

        def whole_turns(eng, c):
            eng.wait_ge(fp.sem, fp.after("theta", c))
            wait(eng, qfull, QJ * (c - 2))
            alone(eng)
            for s in range(2):
                o = eng.tensor_scalar(turns[:, s], theta[:, s], 1.0 / TWO_PI, 0.25 if s == 0 else 0.0, ALU.mult, ALU.add)
            o.then_inc(fp.sem, 1)
            eng.wait_ge(fp.sem, fp.after("turn", c))
            alone(eng)
            eng.tensor_scalar(turns[:], turns[:], MAGIC, -MAGIC, ALU.add, ALU.add).then_inc(fp.sem, 1)

        def dve_reduce(v, c):
            v.wait_ge(fp.sem, fp.after("round", c))
            wait(v, fv.sem, fv.after("txt2", c - 1))
            v.scalar_tensor_tensor(fl(resid), fl(turns), -C1, fl(theta), ALU.mult, ALU.add).then_inc(fv.sem, 1)
            v.wait_ge(fv.sem, fv.after("res1", c))
            v.scalar_tensor_tensor(fl(resid), fl(turns), -C2, fl(resid), ALU.mult, ALU.add).then_inc(fv.sem, 1)
            v.wait_ge(fv.sem, fv.after("res2", c))
            v.scalar_tensor_tensor(fl(resid), fl(turns), -C3, fl(resid), ALU.mult, ALU.add).then_inc(fv.sem, 1)
            v.wait_ge(fv.sem, fv.after("res3", c))
            for s in range(2):
                sh = math.pi / 2 if s == 0 else 0.0
                o = v.tensor_scalar(resid[:, s], resid[:, s], PI_IN - sh, -PI_IN - sh, ALU.min, ALU.max)
            o.then_inc(fv.sem, 1)

        def fl(t):
            return t[:].rearrange("p a b c -> p (a b c)")

        def act_sin(act, c):
            act.wait_ge(fv.sem, fv.after("paggr", c))
            wait(act, fv.sem, fv.after("img", c - 1))
            act.activation(prs[:, 0:1], pmv[:, 1:2], ACT.Ln, bias=eps[:]).then_inc(fa.sem, 1)
            act.wait_ge(fa.sem, fa.after("lnp", c))
            act.activation(prs[:, 1:2], prs[:, 0:1], ACT.Exp, scale=-0.5).then_inc(fa.sem, 1)
            act.preload_act_table_set("silu_and_others")
            act.wait_ge(fv.sem, fv.after("clamp", c))
            for s in range(2):
                o = act.activation(resid[:, s, :, 0:D - 1], resid[:, s, :, 0:D - 1], ACT.Sin, bias=halfpi[:] if s == 0 else 0.0)
            o.then_inc(fa.sem, 1)
            act.preload_act_table_set("natural_log_exp_and_others")
            act.activation(resid[:, :, :, D - 1:D], theta[:, :, :, D - 1:D], ACT.Copy).then_inc(fa.sem, 1)

        def dve_embed(v, c):
            v.wait_ge(img_ps, c + 1)
            wait(v, fv.sem, fv.after("img", c - 1))
            v.wait_ge(fv.sem, fv.after("pneg", c))
            v.scalar_tensor_tensor(img_t[:], proj_sum[:], pneg[:], pq[:, 0:D], ALU.mult, ALU.add).then_inc(img_sb, 1)
            v.wait_ge(img_sb, c + 1)
            v.wait_ge(fa.sem, fa.after("rsp", c))
            wait(v, fv.sem, fv.after("x1", c - 1))
            wait(v, hb_next_ok, c)
            v.scalar_tensor_tensor(h_new[:, 0, :], img_t[:], prs[:, 1:2], proj_bias[:], ALU.mult, ALU.add).then_inc(fv.sem, 1)
            v.wait_ge(fa.sem, fa.after("lin", c))
            v.wait_ge(rows_in, 64 * c + 64)
            for t in range(2):
                o = v.scalar_tensor_tensor(h_new[:, 1 + t, :], resid[:, 0, t, :], am[:, 0:1], tok_rows[:, t, :], ALU.mult, ALU.add)
            o.then_inc(fv.sem, 1)
            v.wait_ge(fv.sem, fv.after("txt1", c))
            for t in range(2):
                o = v.scalar_tensor_tensor(h_new[:, 1 + t, :], resid[:, 1, t, :], am[:, 1:2], h_new[:, 1 + t, :], ALU.mult, ALU.add)
            o.then_inc(fv.sem, 1)
            v.wait_ge(fv.sem, fv.after("txt2", c))
            for t in range(2):
                o = v.scalar_tensor_tensor(h_new[:, 1 + t, :], seg_rows[:, t, :], alpha[:, 2:3], h_new[:, 1 + t, :], ALU.mult, ALU.add)
            o.then_inc(fv.sem, 1)
            v.wait_ge(fv.sem, fv.after("txt3", c))
            for t in range(NT):
                o = v.bn_stats(hst[:, t, :], h_new[:, t, :])
            o.then_inc(fv.sem, 1)
            v.wait_ge(fv.sem, fv.after("hstat", c))
            wait(v, fa.sem, fa.after("lnh", c - 1))
            wait(v, fv.sem, fv.after("x1", c - 1))
            alone(v)
            for t in range(NT):
                o = v.bn_aggr(hmv[:, t, :], hst[:, t, :])
            o.then_inc(fv.sem, 1)

        def act_embed_rs(act, c):
            act.wait_ge(fv.sem, fv.after("haggr", c))
            act.activation(hrs[:, 0, :], hmv[:, :, 1], ACT.Ln, bias=eps[:]).then_inc(fa.sem, 1)
            act.wait_ge(fa.sem, fa.after("lnh", c))
            act.activation(hrs[:, 1, :], hrs[:, 0, :], ACT.Exp, scale=-0.5).then_inc(fa.sem, 1)

        def dve_x1(v, c):
            v.wait_ge(fa.sem, fa.after("rsh", c))
            v.wait_ge(fv.sem, fv.after("haggr", c))
            wait(v, x1_ok, c)
            if not isinstance(c, int) or c > 0:
                wait(v, full[JOB["xT1"][0]], nfull[JOB["xT1"][0]] * (c - 1) + JOB["xT1"][1] + 1)
            for t in range(NT):
                o = v.tensor_scalar(x1_new[:, t, :], h_new[:, t, :], hmv[:, t, 0:1], hrs[:, 1, t:t + 1], ALU.subtract, ALU.mult)
            o.then_inc(fv.sem, 1)

        def pe_xT(pe, c):
            pe.wait_ge(fv.sem, fv.after("x1", c))
            for k in range(2):
                p = job_start(pe, f"xT{k}", c)
                for t in range(NT):
                    mm = pe.transpose(p[0:KH, 128 * t:128 * t + 128], x1_new[:, t, k * KH:(k + 1) * KH], ident[:])
                mm.then_inc(jsem(f"xT{k}", "full"), 1)

        def act_xT(act, c):
            if not isinstance(c, int) or c > 0:
                wait(act, full[JOB[f"xz1_{2 * NC - 1}"][0]], nfull[JOB[f"xz1_{2 * NC - 1}"][0]] * (c - 1) + JOB[f"xz1_{2 * NC - 1}"][1] + 1)
                wait(act, full[JOB[f"xz1_{2 * NC - 2}"][0]], nfull[JOB[f"xz1_{2 * NC - 2}"][0]] * (c - 1) + JOB[f"xz1_{2 * NC - 2}"][1] + 1)
            for k in range(2):
                p = job_wait(act, f"xT{k}", c)
                act.activation(xT[0:KH, k, :, 0:LI], p[0:KH, 0:128].rearrange("p (b l) -> p b l", b=CB), ACT.Copy)
                o = act.activation(xT[0:KH, k, :, LI:L], p[0:KH, 128:T].rearrange("p (b l) -> p b l", b=CB), ACT.Copy)
                o.then_inc(jsem(f"xT{k}", "free"), 1)

        def pe_xz(pe, c, d, tiles):
            if tiles[0] == 0:
                job_read(pe, "xT1", c)
            for o in tiles:
                p = job_start(pe, f"xz{d}_{o}", c)
                for k in range(2):
                    rows = KH + k
                    mm = pe.matmul(p[:, 0:T], wxz[0:rows, d, k, 128 * o:128 * o + 128], xT[0:rows, k].rearrange("p b l -> p (b l)"), start=(k == 0), stop=(k == 1))
                mm.then_inc(jsem(f"xz{d}_{o}", "full"), 1)

        def act_xz(act, c, d, tiles):
            e = 2 * c + d
            if tiles[0] == 0:
                wait(act, dv.sem, dv.after("dt", e - 1))
            if tiles[0] >= NC:
                wait(act, gated, NC * (e - 2) + tiles[-1] - NC + 1)
            for o in tiles:
                p = job_wait(act, f"xz{d}_{o}", c)
                if o < NC:
                    out = xc[:, o, :, KC:KC + L]
                    act.activation(out, p[:, 0:T].rearrange("p (b l) -> p b l", b=CB), ACT.Copy)
                    op = act.activation(ea[:, o, :], p[:, 0:T], ACT.Identity, scale=cw[:, o, KC:KC + 1], bias=cb[:, o:o + 1])
                else:
                    op = act.activation(zs[:, d, o - NC, :], p[:, 0:T], ACT.Copy)
                op.then_inc(jsem(f"xz{d}_{o}", "free"), 1)

        def dve_conv(v, c, d, tiles):
            e = 2 * c + d
            half = "a" if tiles[0] == 0 else "b"
            for o in tiles:
                job_read(v, f"xz{d}_{o}", c)
            for k in range(KC):
                if k:
                    v.wait_ge(dv.sem, dv.after(f"conv{k - 1}{half}", e))
                for o in tiles:
                    at = k if d == 0 else 2 * KC - k
                    x = xc[:, o, :, at:at + L]
                    acc = ea[:, o, :].rearrange("p (b l) -> p b l", b=CB)
                    op = v.scalar_tensor_tensor(acc, x, cw[:, o, k:k + 1], acc, ALU.mult, ALU.add)
                op.then_inc(dv.sem, 1)

        def act_silu(act, c, d):
            e = 2 * c + d
            act.preload_act_table_set("silu_and_others")
            if not isinstance(e, int) or e > 0:
                before = (c, 0) if d == 1 else (c - 1, 1)
                job_read(act, f"xz{before[1]}_{2 * NC - 1}", before[0])
                job_read(act, f"xz{before[1]}_{2 * NC - 2}", before[0])
                op = act.activation(zs[:, 1 - d], zs[:, 1 - d], ACT.Silu)
            if not isinstance(c, int) or c < NCH:
                act.wait_ge(dv.sem, dv.after("conv2b", e))
                wait(act, y_ok, UD * (e - 1))
                op = act.activation(u[:, d], ea[:], ACT.Silu)
            op.then_inc(ds.sem, 1)
            act.preload_act_table_set("natural_log_exp_and_others")

        def pe_bc(pe, c, d):
            e = 2 * c + d
            pe.wait_ge(ds.sem, ds.after("silu", e))
            p = job_start(pe, f"bc{d}", c)
            for i in range(NC):
                mm = pe.matmul(p[0:96 + R, 0:T], xpw[:, i, :], u[:, d, i, :], start=(i == 0), stop=(i == NC - 1))
            mm.then_inc(jsem(f"bc{d}", "full"), 1)

        def act_bc(act, c, d):
            e = 2 * c + d
            p = job_wait(act, f"bc{d}", c)
            wait(act, rep_ps, 4 * NG * (e - 1))
            act.activation(stk[:, d, :], p[0:96, 0:T], ACT.Copy)
            act.activation(dtx[96:96 + R, :], p[96:96 + R, 0:T], ACT.Copy).then_inc(jsem(f"bc{d}", "free"), 1)

        def dve_split(v, c, d):
            e = 2 * c + d
            p = job_wait(v, f"bc{d}", c)
            b, _, fr = JOB[f"bc{d}"]
            v.wait_ge(free[b], nfree[b] * c + fr + 1)
            wait(v, dv.sem, dv.after("split3", e - 1))
            v.tensor_tensor(rr[:], p[0:96, 0:T], stk[:, d, :], ALU.subtract).then_inc(jsem(f"bc{d}", "free"), 1)
            job_read(v, f"bc{d}", c)
            v.tensor_copy(mid[64:96, :], rr[64:96, :])
            v.tensor_copy(stk[32:64, d, :], rr[32:64, :]).then_inc(dv.sem, 1)
            v.wait_ge(dv.sem, dv.after("split2", e))
            v.tensor_tensor(stk[64:96, d, :], rr[64:96, :], mid[64:96, :], ALU.subtract).then_inc(dv.sem, 1)

        def pe_dt(pe, c, d, tiles):
            job_read(pe, f"bc{d}", c)
            for o in tiles:
                p = job_start(pe, f"dt{d}_{o}", c)
                pe.matmul(p[:, 0:T], dtw[96:96 + R, 128 * o:128 * o + 128], dtx[96:96 + R, :], start=True, stop=True).then_inc(jsem(f"dt{d}_{o}", "full"), 1)

        def act_dt(act, c, d, tiles):
            e = 2 * c + d
            if tiles[0] == 0:
                wait(act, dbu_ok, UD * (e - 1))
                act.wait_ge(ds.sem, ds.after("silu", e))
            for o in tiles:
                p = job_wait(act, f"dt{d}_{o}", c)
                act.activation(dtu[:, d, o, :], p[:, 0:T], ACT.Identity, bias=dtb[:, o:o + 1]).then_inc(jsem(f"dt{d}_{o}", "free"), 1)
            for o in tiles:
                job_read(act, f"dt{d}_{o}", c)
            part = slice(tiles[0], tiles[-1] + 1)
            step = min(tiles[0], 1)
            act.activation(ea[:, part], dtu[:, d, part], ACT.Abs).then_inc(ds.sem, 1)
            act.wait_ge(ds.sem, ds.after(f"x{step}", e))
            act.activation(ea[:, part], ea[:, part], ACT.Exp, scale=-1.0).then_inc(ds.sem, 1)

        def act_log(act, c, d):
            e = 2 * c + d
            act.wait_ge(ds.sem, ds.after("exp1", e))
            act.activation(dt_[:, d], ea[:], ACT.Ln, bias=1.0).then_inc(ds.sem, 1)

        def dve_steps(v, c, d):
            e = 2 * c + d
            v.wait_ge(ds.sem, ds.after("ln", e))
            v.scalar_tensor_tensor(dt_[:, d], dtu[:, d], 0.0, dt_[:, d], ALU.max, ALU.add).then_inc(dv.sem, 1)
            v.wait_ge(dv.sem, dv.after("m", e))
            v.tensor_scalar(dtu[:, d], ea[:], 1.0, -1.0, ALU.add, ALU.add).then_inc(dv.sem, 1)
            v.wait_ge(dv.sem, dv.after("w1", e))
            v.tensor_tensor(ea[:], ea[:], dtu[:, d], ALU.subtract).then_inc(dv.sem, 1)
            v.wait_ge(dv.sem, dv.after("r", e))
            v.tensor_tensor(dt_[:, d], dt_[:, d], ea[:], ALU.add).then_inc(dv.sem, 1)

        def pe_rep(pe, c, g, piece):
            d, ng = g // NG, g % NG
            q = 4 * (2 * NG * c + g) + piece
            pe.wait_ge(dv.sem, dv.after("split3", 2 * c + d))
            wait(pe, rep_sb, q)
            for i in range(2):
                j = piece // 2 * NS + ng * GN + 2 * (piece % 2) + i
                mm = pe.matmul(prep[:, i, 0:T], sel[:, j:j + 1].to_broadcast([96, 128]), stk[:, d, :], start=True, stop=True)
            mm.then_inc(rep_ps, 1)

        def act_rep(act, c, g, piece):
            G = 2 * NG * c + g
            if piece % 2 == 0:
                wait(act, dbu_ok if piece == 0 else hc_ok, NC * (G - 1))
            act.wait_ge(rep_ps, 4 * G + piece + 1)
            at = 2 * (piece % 2)
            dst = (brep if piece < 2 else crep)[:, g % 2, at:at + 2, :]
            act.activation(dst, prep[:, :, 0:T], ACT.Copy).then_inc(rep_sb, 1)

        def unit(w):
            d, r = divmod(w, UD)
            ng, o = divmod(r, NC)
            return d, ng, o, d * NG + ng

        def act_decay(act, c, w):
            d, ng, o, g = unit(w)
            U = U2 * c + w
            act.wait_ge(dv.sem, dv.after("dt", 2 * c + d))
            wait(act, scan_ok, U + 1 - NDA)
            lo = 1 if d == 0 else 0
            if w % UD < NDA:
                start = da[:, w % NDA].rearrange("p n (b l) -> p (n b) l", b=CB)[:, :, (L - 1) * d:(L - 1) * d + 1]
                act.activation(start, zero_cols[:].unsqueeze(2), ACT.Copy)
            src = dt_[:, d, o, :].rearrange("p (b l) -> p b l", b=CB)[:, :, lo:lo + L - 1]
            for i in range(GN):
                n = ng * GN + i
                dst = da[:, w % NDA, i, :].rearrange("p (b l) -> p b l", b=CB)[:, :, lo:lo + L - 1]
                op = act.activation(dst, src, ACT.Exp, scale=aneg[:, o, n:n + 1])
            op.then_inc(da_ok, 1)

        def pool_input(gp, c, w):
            d, ng, o, g = unit(w)
            U, G = U2 * c + w, 2 * NG * c + g
            gp.wait_ge(dv.sem, dv.after("dt", 2 * c + d))
            if ng == 0:
                gp.tensor_tensor(dtu[:, d, o, :], dt_[:, d, o, :], u[:, d, o, :], ALU.mult).then_inc(dtu_ok, 1)
                gp.wait_ge(dtu_ok, NC * (2 * c + d) + o + 1)
            gp.wait_ge(rep_sb, 4 * G + 2)
            wait(gp, y_ok, U + 1 - NRING)
            gp.tensor_tensor(ring[:, w % NRING], dtu[:, d, o, :].unsqueeze(1).to_broadcast([128, GN, T]), brep[:, g % 2], ALU.mult).then_inc(dbu_ok, 1)

        def dve_scan(v, c, w):
            d, ng, o, g = unit(w)
            U = U2 * c + w
            v.wait_ge(da_ok, U + 1)
            v.wait_ge(dbu_ok, U + 1)
            x0 = da[:, w % NDA].rearrange("p n t -> p (n t)")
            h = ring[:, w % NRING].rearrange("p n t -> p (n t)")
            if d == 1:
                x0, h = x0[:, ::-1], h[:, ::-1]
            v.tensor_tensor_scan(h, x0, h, 0.0, ALU.mult, ALU.add).then_inc(scan_ok, 1)

        def dve_product(v, c, w):
            d, ng, o, g = unit(w)
            U, G = U2 * c + w, 2 * NG * c + g
            v.wait_ge(scan_ok, U + 1)
            v.wait_ge(rep_sb, 4 * G + 4)
            v.tensor_tensor(ring[:, w % NRING], ring[:, w % NRING], crep[:, g % 2], ALU.mult).then_inc(hc_ok, 1)

        def pe_sum(pe, c, w):
            d, ng, o, g = unit(w)
            U = U2 * c + w
            pe.wait_ge(hc_ok, U + 1)
            if ng == 0:
                wait(pe, gated, NC * (2 * c + d - 1) + o + 1)
            for i in range(GN):
                mm = pe.matmul(py[o][:, 0:T], ident[:], ring[:, w % NRING, i, :], start=(ng == 0 and i == 0), stop=False)
            if ng == NG - 1:
                mm = pe.matmul(py[o][:, 0:T], skip_diag[:, o, :], u[:, d, o, :], start=False, stop=True)
            mm.then_inc(y_ok, 1)

        def dve_gate(v, c, d, o):
            e = 2 * c + d
            v.wait_ge(ds.sem, ds.after("silu", e + 1))
            wait(v, qfull, QJ * (c - 1) + 2)
            v.wait_ge(filled, 32)
            v.wait_ge(y_ok, U2 * c + UD * d + UD - NC + o + 1)
            for lo, hi in ((0, LI), (LI, L)):
                yv, zv = (x.rearrange("p (b l) -> p b l", b=CB)[:, :, lo:hi] for x in (py[o][:, 0:T], zs[:, d, o, :]))
                ov = yg[:, d, o, CB * lo:CB * hi].rearrange("p (b l) -> p b l", b=CB)
                op = v.tensor_tensor(ov, yv, zv, ALU.mult)
            op.then_inc(gated, 1)

        def pe_out(pe, c, tiles):
            pe.wait_ge(gated, NC * (2 * c + 2))
            wait(pe, qfree, QJ * c + tiles[0] // 2)
            for t in tiles:
                at = D * (t % 2)
                for i in range(2 * NC):
                    pe.matmul(pq[:, at:at + D], yg[:, i // NC, i % NC, 128 * t:128 * t + 128], w2t[:, i % NC, :], start=(i == 0), stop=False)
                mm = pe.matmul(pq[:, at:at + D], ones[0:1, :], outb[:], start=False, stop=True)
            mm.then_inc(qfull, 1)

        def dve_out(v, c, tiles):
            if tiles[0] == 0:
                v.wait_ge(x1_ok, c + 1)
                wait(v, h2_out, 16 * c)
            v.wait_ge(qfull, QJ * c + tiles[0] // 2 + 1)
            n = len(tiles)
            v.tensor_tensor(h2[:, tiles[0]:tiles[0] + n, :], pq[:, 0:n * D].rearrange("p (t k) -> p t k", k=D), x1[:, tiles[0]:tiles[0] + n, :], ALU.add).then_inc(qfree, 1)

        def dve_stat(v, c):
            v.wait_ge(qfree, QJ * c + 2)
            for t in range(NT):
                o = v.bn_stats(qst[:, t, :], h2[:, t, :])
            o.then_inc(qv.sem, 1)
            v.wait_ge(qv.sem, qv.after("stat", c))
            alone(v)
            for t in range(NT):
                o = v.bn_aggr(qmv[:, t, :], qst[:, t, :])
            o.then_inc(qv.sem, 1)

        def act_rs(act, c):
            act.wait_ge(qv.sem, qv.after("aggr", c))
            act.activation(qrs[:, 0, :], qmv[:, :, 1], ACT.Ln, bias=eps[:]).then_inc(qa.sem, 1)
            act.wait_ge(qa.sem, qa.after("ln", c))
            act.activation(qrs[:, 1, :], qrs[:, 0, :], ACT.Exp, scale=-0.5).then_inc(qa.sem, 1)

        def norm_h2(eng, c):
            eng.wait_ge(qa.sem, qa.after("rs", c))
            alone(eng)
            for t in range(NT):
                o = eng.tensor_scalar(h2[:, t, :], h2[:, t, :], qmv[:, t, 0:1], qrs[:, 1, t:t + 1], ALU.subtract, ALU.mult)
            o.then_inc(qp.sem, 1)
            eng.wait_ge(qp.sem, qp.after("norm", c))
            eng.tensor_tensor(h2[:], h2[:], ln_g[:].unsqueeze(1).to_broadcast([128, NT, D]), ALU.mult).then_inc(qp.sem, 1)
            eng.wait_ge(qp.sem, qp.after("gain", c))
            eng.wait_ge(hb_ok, c + 1)
            eng.tensor_tensor(h2[:], h2[:], hb[:], ALU.add).then_inc(qp.sem, 1)

        def dve_stat3(v, c):
            v.wait_ge(qp.sem, qp.after("h2", c))
            for t in range(NT):
                o = v.bn_stats(qst[:, t, :], h2[:, t, :])
            o.then_inc(qv.sem, 1)
            v.wait_ge(qv.sem, qv.after("stat3", c))
            alone(v)
            for t in range(NT):
                o = v.bn_aggr(qmv[:, t, :], qst[:, t, :])
            o.then_inc(qv.sem, 1)

        def act_rs3(act, c):
            act.wait_ge(qv.sem, qv.after("aggr3", c))
            act.activation(qrs[:, 0, :], qmv[:, :, 1], ACT.Ln, bias=eps[:]).then_inc(qa.sem, 1)
            act.wait_ge(qa.sem, qa.after("ln3", c))
            act.activation(qrs[:, 1, :], qrs[:, 0, :], ACT.Exp, scale=-0.5).then_inc(qa.sem, 1)

        def norm_x3(eng, c):
            eng.wait_ge(qa.sem, qa.after("rs3", c))
            wait(eng, x3_out, 16 * c)
            wait(eng, qfull, QJ * (c - 1) + 4)
            alone(eng)
            for t in range(NT):
                o = eng.tensor_scalar(x3[:, t, :], h2[:, t, :], qmv[:, t, 0:1], qrs[:, 1, t:t + 1], ALU.subtract, ALU.mult)
            o.then_inc(qp.sem, 1)

        def sp_store(sp, c, what):
            if what == "h2":
                sp.wait_ge(qp.sem, qp.after("h2", c))
            else:
                sp.wait_ge(qp.sem, qp.after("x3", c))
            alone(sp)
            rows, src, done = (out_rows(c), h2, h2_out) if what == "h2" else (dram["x3"][:, bass.ds(c, 1), :].rearrange("p a k -> p (a k)"), x3, x3_out)
            sp.dma_start(rows, src[:].rearrange("p t k -> p (t k)")).then_inc(done, 16)

        def out_rows(c):
            return dram["out"][0:NTOK, :].rearrange("(c p t) d -> c p (t d)", c=NCH, t=NT)[bass.ds(c, 1)].rearrange("a p k -> p (a k)")

        def pe_x3T(pe, c, k):
            pe.wait_ge(qp.sem, qp.after("x3", c))
            wait(pe, qfree, QJ * c + 2 + k)
            if k == 0:
                pe.wait_ge(img_sb, min(c + 3, NCH) if isinstance(c, int) else c + 3)
            for t in range(NT):
                mm = pe.transpose(pq[0:KH, 128 * t:128 * t + 128], x3[:, t, k * KH:(k + 1) * KH], ident[:])
            mm.then_inc(qfull, 1)

        def act_x3T(act, c, k):
            act.wait_ge(qfull, QJ * c + 3 + k)
            if k == 0:
                act.wait_ge(fv.sem, fv.after("clamp", min(c + 2, NCH - 1) if isinstance(c, int) else c + 2))
            act.activation(x3T[:, k, :], pq[0:KH, 0:T], ACT.Copy).then_inc(qfree, 1)

        def pe_router(pe, c):
            wait(pe, qfree, QJ * c + 4)
            for t in range(NT):
                for k in range(2):
                    mm = pe.matmul(pq[:, E * t:E * t + E], x3T[:, k, 128 * t:128 * t + 128], rw[:, k, :], start=(k == 0), stop=(k == 1))
            mm.then_inc(qfull, 1)

        def dve_router(v, c):
            v.wait_ge(qfull, QJ * c + QJ)
            v.tensor_copy(logits[:, bass.ds(NT * c, NT), :].rearrange("p t e -> p (t e)"), pq[:, 0:NT * E]).then_inc(qfree, 1)

        block = ctx.enter_context(nc.Block())
        loads = [
            (bm_in.rearrange("p d j k -> p (d j k)"), a["bm_in"]), (inT.rearrange("p j o -> p (j o)"), a["inT"]), (outw.rearrange("p j o -> p (j o)"), a["outw"]),
            (bmoT.rearrange("p j o -> p (j o)"), a["bmoT"]), (projT.rearrange("p k o -> p (k o)"), a["projT"]),
            (tgam, a["tgam"]), (tbet, a["tbet"]), (projb, a["projb"]),
            (xpw[:, :, 0 * NS:2 * NS], a["xpw_bc"]), (xpw[:, :, 2 * NS:4 * NS], a["xpw_bc"]), (xpw[:, :, 4 * NS:6 * NS], a["xpw_bc"]),
            (xpw[:, :, 96:96 + R], a["xpw_dt"]), (dtw[96:96 + R, :], a["dtw"]), (dtb[:], a["dtb"]),
            (cw[:].rearrange("p o k -> p (o k)"), a["cw"]), (cb[:], a["cb"]), (dskip[:], a["dskip"]),
            (aneg[:].rearrange("p o n -> p (o n)"), a["a_log"]),
            (w_tau[:].rearrange("p s k -> p (s k)"), a["w_tau"].partition_broadcast(128)),
            (b_tau[:].rearrange("p s k -> p (s k)"), a["b_tau"].partition_broadcast(128)),
            (alpha[:], a["alpha"].partition_broadcast(128)),
            (outb[:], a["outb"]), (ln_g[:], a["ln_g"].partition_broadcast(128)), (ln_b[:], a["ln_b"].partition_broadcast(128)),
            (rw[:].rearrange("p k e -> p (k e)"), a["rw"]),
        ]
        FOLDED = 2
        LOADED = 16 * (len(loads) - FOLDED)
        banks = [py[0], py[1], py[2], prep[:, 0, :], prep[:, 1, :], pf[0], pf[1], pq]

        def sp_setup(sp):
            for i, (dst, src) in enumerate(loads):
                if len(dst.shape) == 2 and len(src.shape) == 3:
                    src = src.rearrange("p a k -> p (a k)")
                sp.dma_start(dst, src).then_inc(w_in if i >= FOLDED else fold_in, 16)
                if i == FOLDED - 1:
                    sp_load(sp, 0)

        def pool_setup(gp):
            gp.memset(ones[:], 1.0)
            gp.memset(ident[:], 0.0).then_inc(set_pool, 1)
            gp.memset(spare, 0.0)
            gp.iota(spare_i[:], pattern=[[0, 1]], base=NTOK, channel_multiplier=1).then_inc(set_pool, 1)
            gp.wait_ge(set_pool, 2)
            gp.tensor_copy(spare[:, D:D + 1], spare_i[:])
            gp.affine_select(out=ident[:], in_=ident[:], compare_op=ALU.not_equal, fill=1.0, base=0, pattern=[[-1, 128]], channel_multiplier=1).then_inc(set_pool, 1)

        def dve_setup(v):
            v.memset(xc[:].rearrange("p o b l -> p (o b l)"), 0.0)
            v.memset(zero_cols[:], 0.0)
            v.memset(xT[KH:KH + 1].rearrange("p k b l -> p (k b l)"), 1.0)
            v.memset(eps[:], EPS)
            v.memset(halfpi[:], math.pi / 2)
            v.memset(mask[:], 1.0).then_inc(set_dve, 1)
            v.wait_ge(set_dve, 1)
            for q in range(4):
                o = v.memset(mask[LT * q:LT * q + 5, :], 0.0)
            o.then_inc(set_dve, 1)
            v.wait_ge(set_dve, 2)
            v.wait_ge(w_in, LOADED)
            v.tensor_scalar(am[:], alpha[:, 0:2], mask[:], None, ALU.mult)
            v.wait_ge(set_pool, 3)
            for o in range(NC):
                v.tensor_scalar(skip_diag[:, o, :], ident[:], dskip[:, o:o + 1], None, ALU.mult)
            for k in range(PD // 128):
                v.tensor_scalar(gw[:, k, :], projT[:, k, :], tgam[:, k:k + 1], None, ALU.mult)
                v.tensor_scalar(betas[:, k, :], ones[:], tbet[:, k:k + 1], None, ALU.mult)
            v.tensor_tensor(sel1, ident[0:96, 0:32], ident[0:96, 32:64], ALU.add).then_inc(set_dve, 1)
            v.wait_ge(set_dve, 3)
            v.tensor_tensor(sel1, sel1, ident[0:96, 64:96], ALU.add).then_inc(set_dve, 1)
            v.wait_ge(set_dve, 4)
            v.tensor_copy(sel[:], sel1).then_inc(set_dve, 1)
            v.wait_ge(set_act, 9)
            v.tensor_scalar(aneg[:], aneg[:], -1.0, None, ALU.mult).then_inc(set_dve, 1)

        def pe_setup(pe):
            pe.wait_ge(fold_in, 16 * FOLDED)
            i = 0
            for d in range(2):
                for k in range(2):
                    for h in range(2):
                        for j in range(2):
                            mm = pe.matmul(banks[i][0:KH + k, 0:DI], bm_in[:, d, j, KH * k:KH * (k + 1) + k], inT[:, j, DI * h:DI * h + DI], start=(j == 0), stop=(j == 1))
                        mm.then_inc(set_pe, 1)
                        i += 1
            pe.wait_ge(w_in, LOADED)
            pe.wait_ge(set_dve, 5)
            pe.wait_ge(set_act, 8)
            for k in range(PD // 128):
                pe.matmul(pf[1][:, 0:D], ones[:], gw[:, k, :], start=(k == 0), stop=(k == PD // 128 - 1))
            for k in range(PD // 128):
                pe.matmul(pf[0][:, 0:D], betas[:, k, :], projT[:, k, :], start=(k == 0), stop=False)
            pe.matmul(pf[0][:, 0:D], ones[0:1, :], projb, start=False, stop=True).then_inc(set_pe, 1)
            pe_img(pe, 0)
            for i in range(NC):
                for j in range(2):
                    mm = pe.matmul(py[i][:, 0:D], outw[:, j, 128 * i:128 * i + 128], bmoT[:, j, :], start=(j == 0), stop=(j == 1))
            mm.then_inc(set_pe, 1)

        def act_setup(act):
            act.preload_act_table_set("natural_log_exp_and_others")
            i = 0
            for d in range(2):
                for k in range(2):
                    for h in range(2):
                        act.wait_ge(set_pe, i + 1)
                        act.activation(wxz[0:KH + k, d, k, DI * h:DI * h + DI], banks[i][0:KH + k, 0:DI], ACT.Copy).then_inc(set_act, 1)
                        i += 1
            act.wait_ge(w_in, LOADED)
            act.activation(aneg[:], aneg[:], ACT.Exp).then_inc(set_act, 1)
            act.wait_ge(set_pe, 9)
            act.activation(proj_sum[:], pf[1][:, 0:D], ACT.Copy)
            act.activation(proj_bias[:], pf[0][:, 0:D], ACT.Copy).then_inc(set_act, 1)

        def act_w2t(act):
            act.wait_ge(set_pe, 10)
            for i in range(NC):
                op = act.activation(w2t[:, i, :], py[i][:, 0:D], ACT.Copy)
            op.then_inc(set_act, 1)

        def set_up(eng):
            eng.wait_ge(set_dve, 6)
            eng.wait_ge(set_act, 11)
            eng.wait_ge(set_pool, 3)
            eng.wait_ge(w_in, LOADED)

        FRONT = {0: ["load", "rows"], 1: ["phase"], 3: ["reduce"], 5: ["sin"], 6: ["img"],
                 7: ["embed", "embed_rs"], 8: ["x1"], 9: ["xT"], 10: ["xT_out"]}
        DIR0 = {-2: ["x01"], -1: ["x01_out", "x2"], 0: ["x2_out", "conv01"], 1: ["conv2", "silu", "bc"],
                2: ["bc_out"], 4: ["split", "dt0"], 5: ["dt12", "dt0_out"], 7: ["dt12_out", "softplus"],
                8: ["z01"], 9: ["steps", "z01_out", "z2"], 10: ["z2_out"]}
        DIR1 = {-2: ["x01"], -1: ["x01_out", "x2"], 0: ["x2_out", "conv01"],
                1: ["z01", "conv2", "silu", "z01_out"], 2: ["bc", "bc_out"], 4: ["split"], 5: ["dt0"],
                7: ["dt0_out", "dt12"], 8: ["dt12_out", "softplus", "z2"], 9: ["z2_out", "steps"]}
        BACK = {3: ["out01"], 4: ["out01_add"], 5: ["out2"], 6: ["out2_add"], 7: ["rs"], 8: ["h2"],
                10: ["stat3", "rs3"], 11: ["x3"], 15: ["x3T0"], 17: ["x3T0_out", "x3T1"], 19: ["x3T1_out"],
                20: ["router"], 23: ["logits"]}
        KEEP = 6
        KEPT = 12
        GATE = UD
        REP = -5

        def plan(c, first, last):
            slots = [[] for _ in range(U2)]

            def put(stage, at, chunk, k):
                for w, names in stage.items():
                    if 0 <= at + w < U2:
                        slots[at + w] += [(s, chunk, k) for s in names]

            for of_next in (False, True):
                for g in range(2 * NG):
                    for piece in range(4):
                        w = NC * g + REP + piece
                        if w >= 0 and not of_next:
                            slots[w].append(("rep", c, (g, piece)))
                        elif w < 0 and of_next and not last:
                            slots[w].append(("rep", c + 1, (g, piece)))
            for o in range(NC):
                if not first:
                    slots[GATE - UD + o].append(("gate", c - 1, (1, o)))
                slots[GATE + o].append(("gate", c, (0, o)))
            put(DIR1, 0, c, 1)
            if not first:
                put(BACK, 0, c - 1, 0)
            slots[KEEP].append(("keep", c, 0))
            slots[KEPT].append(("kept", c, 0))
            if last:
                slots[UD + 2].append(("silu", c + 1, 0))
            else:
                put(FRONT, 0, c + 1, 0)
                put(DIR0, UD, c + 1, 0)
                put(DIR1, U2, c + 1, 1)
            for w in range(U2):
                if w + AHEAD < U2:
                    yield "ahead", c, w + AHEAD
                elif not last:
                    yield "ahead", c + 1, w + AHEAD - U2
                yield "scan", c, w
                at = (c, w - 1) if w else (c - 1, U2 - 1)
                if w or not first:
                    yield "product", *at
                summed = (c, w - 2) if w > 1 else (c - 1, U2 + w - 2)
                parts = {"rep": [s for s in slots[w] if s[0] == "rep"], "steps": [s for s in slots[w] if s[0] != "rep"],
                         "sum": [("sum", *summed)] if w > 1 or not first else []}
                yield from parts["rep"]
                yield from parts["sum"]
                yield from parts["steps"]

        def in_order(stage, c, k):
            return [(s, c, k) for w in sorted(stage) for s in stage[w]]

        EARLY = {w: FRONT[w] for w in FRONT if w < 6}

        def early():
            for step in in_order(EARLY, 0, 0):
                if step[0] not in ("load", "rows"):
                    yield step

        def prologue():
            yield from (step for step in in_order({w: FRONT[w] for w in FRONT if w not in EARLY}, 0, 0) if step[0] != "img")
            gates = ("z01", "z01_out", "z2", "z2_out")
            direction = list(in_order(DIR0, 0, 0))
            yield from [step for step in direction if step[0] not in gates]
            for g in range(2 * NG):
                for piece in range(4):
                    if NC * g + REP + piece < 0:
                        yield "rep", 0, (g, piece)
            for w in range(AHEAD):
                yield "ahead", 0, w
            yield from [step for step in direction if step[0] in gates]
            yield from in_order({w: DIR1[w] for w in DIR1 if w < 0}, 0, 1)

        def epilogue():
            c = NCH - 1
            yield "product", c, U2 - 1
            yield "sum", c, U2 - 2
            yield "sum", c, U2 - 1
            for o in range(NC):
                yield "gate", c, (1, o)
            yield from in_order(BACK, c, 0)

        def at_start(c):
            return isinstance(c, int) and c == 0

        def at_end(c):
            return isinstance(c, int) and c == NCH - 1

        def run(eng, steps, plan_steps):
            for what, c, k in plan_steps:
                if what in steps:
                    steps[what](eng, c, k)

        def program(eng, steps):
            run(eng, steps, early())
            if "folded" in steps:
                steps["folded"](eng)
            set_up(eng)
            run(eng, steps, prologue())
            run(eng, steps, plan(0, True, False))
            run(eng, steps, plan(1, False, False))
            with eng.Fori(2, NCH - 1) as c:
                run(eng, steps, plan(c, False, False))
            run(eng, steps, plan(NCH - 1, False, True))
            run(eng, steps, epilogue())

        @block.sync
        def _(sp):
            sp_setup(sp)
            sp.wait_ge(set_pool, 3)
            sp.dma_start(dram["xs"].rearrange("j p x -> p j x"), spare.unsqueeze(1).to_broadcast([128, NJ, XW])).then_inc(filled, 16)
            sp.dma_start(dram["out"][NTOK:NTOK + 128, :], spare[:, 0:D]).then_inc(filled, 16)
            program(sp, {
                "load": lambda e, c, k: sp_load(e, c),
                "h2": lambda e, c, k: sp_store(e, c, "h2"),
                "x3": lambda e, c, k: sp_store(e, c, "x3"),
            })
            sp.wait_ge(h2_out, 16 * NCH)
            sp.wait_ge(x3_out, 16 * NCH)
            sp.wait_ge(filled, 32)

        @block.gpsimd
        def _(gp):
            pool_setup(gp)
            pool_rows(gp, 0)
            gp.wait_ge(w_in, LOADED)
            program(gp, {
                "rows": lambda e, c, k: pool_rows(e, c),
                "phase": lambda e, c, k: (pool_phase(e, c), None if at_start(c) else whole_turns(e, c)),
                "keep": lambda e, c, k: pool_keep(e, c),
                "kept": lambda e, c, k: pool_kept(e, c),
                "h2": lambda e, c, k: None if at_end(c) else norm_h2(e, c),
                "x3": lambda e, c, k: None if at_end(c) else norm_x3(e, c),
                "ahead": pool_input,
            })

        @block.scalar
        def _(act):
            act_setup(act)
            program(act, {
                "folded": act_w2t,
                "sin": lambda e, c, k: act_sin(e, c),
                "embed_rs": lambda e, c, k: act_embed_rs(e, c),
                "xT_out": lambda e, c, k: act_xT(e, c),
                "keep": lambda e, c, k: act_keep(e, c),
                "x01_out": lambda e, c, d: act_xz(e, c, d, (0, 1)),
                "x2_out": lambda e, c, d: act_xz(e, c, d, (2,)),
                "z01_out": lambda e, c, d: act_xz(e, c, d, (3, 4)),
                "z2_out": lambda e, c, d: act_xz(e, c, d, (5,)),
                "silu": act_silu, "bc_out": act_bc,
                "dt0_out": lambda e, c, d: act_dt(e, c, d, (0,)),
                "dt12_out": lambda e, c, d: act_dt(e, c, d, (1, 2)),
                "softplus": act_log,
                "rep": lambda e, c, k: act_rep(e, c, *k),
                "ahead": act_decay,
                "rs": lambda e, c, k: act_rs(e, c),
                "rs3": lambda e, c, k: act_rs3(e, c),
                "x3T0_out": lambda e, c, k: act_x3T(e, c, 0),
                "x3T1_out": lambda e, c, k: act_x3T(e, c, 1),
            })

        @block.vector
        def _(v):
            dve_setup(v)
            program(v, {
                "phase": lambda e, c, k: (dve_patch_stats(e, c), whole_turns(e, c) if at_start(c) else None),
                "reduce": lambda e, c, k: dve_reduce(e, c),
                "embed": lambda e, c, k: dve_embed(e, c),
                "x1": lambda e, c, k: dve_x1(e, c),
                "conv01": lambda e, c, d: dve_conv(e, c, d, (0, 1)),
                "conv2": lambda e, c, d: dve_conv(e, c, d, (2,)),
                "split": dve_split, "steps": dve_steps,
                "scan": dve_scan, "product": dve_product, "gate": lambda e, c, k: dve_gate(e, c, *k),
                "out01_add": lambda e, c, k: dve_out(e, c, (0, 1)),
                "out2_add": lambda e, c, k: (dve_out(e, c, (2,)), dve_stat(e, c)),
                "h2": lambda e, c, k: norm_h2(e, c) if at_end(c) else None,
                "stat3": lambda e, c, k: dve_stat3(e, c),
                "x3": lambda e, c, k: norm_x3(e, c) if at_end(c) else None,
                "logits": lambda e, c, k: dve_router(e, c),
            })

        @block.tensor
        def _(pe):
            pe_setup(pe)
            program(pe, {
                "img": lambda e, c, k: pe_img(e, c),
                "xT": lambda e, c, k: pe_xT(e, c),
                "x01": lambda e, c, d: pe_xz(e, c, d, (0, 1)),
                "x2": lambda e, c, d: pe_xz(e, c, d, (2,)),
                "z01": lambda e, c, d: pe_xz(e, c, d, (3, 4)),
                "z2": lambda e, c, d: pe_xz(e, c, d, (5,)),
                "bc": pe_bc,
                "dt0": lambda e, c, d: pe_dt(e, c, d, (0,)),
                "dt12": lambda e, c, d: pe_dt(e, c, d, (1, 2)),
                "rep": lambda e, c, k: pe_rep(e, c, *k),
                "sum": pe_sum,
                "out01": lambda e, c, k: pe_out(e, c, (0, 1)),
                "out2": lambda e, c, k: pe_out(e, c, (2,)),
                "x3T0": lambda e, c, k: pe_x3T(e, c, 0),
                "x3T1": lambda e, c, k: pe_x3T(e, c, 1),
                "router": lambda e, c, k: pe_router(e, c),
            })


def build_experts(nc, a, dram, ident, logits, sem):
    with ExitStack() as ctx:
        def sb(name, shape, dt=F32):
            return ctx.enter_context(nc.sbuf_tensor(name, shape, dt))

        def pb(name, shape, dt=F32):
            return ctx.enter_context(nc.psum_tensor(name, shape, dt))

        w13 = sb("w13", [KH, E, 2, 2 * HF])
        wd = sb("wd", [128, E, HF // 128, D])
        xe = sb("xe", [128, NTT, XW])
        dest = sb("dest", [128, NTT], I32)
        tri = sb("tri", [128, 128])
        every = sb("every", [128, 128])
        rev_i = sb("rev_i", [128, E], I32)
        rev = sb("rev", [128, E])
        tile_i = sb("tile_i", [1, NJ], I32)
        tile_f = sb("tile_f", [1, NJ])
        cand = sb("cand", [128, NTT, E])
        pick = [sb(f"pick{k}", [128, NTT, E]) for k in range(2)]
        left = sb("left", [128, NTT, E])
        top = [sb(f"top{k}", [128, NTT]) for k in range(2)]
        best = sb("best", [128, NTT])
        both = sb("both", [128, NTT, E])
        totals = sb("totals", [128, E, NTT])
        cum = sb("cum", [128, E, NTT])
        carry_on = sb("carry_on", [128, E, NTT])
        slotmap = sb("slotmap", [128, NTT, E])
        tiles_i = sb("tiles_i", [128, E], I32)
        tiles_f = sb("tiles_f", [128, E])
        ends = sb("ends", [128, E])
        starts = sb("starts", [128, E])
        one8 = sb("one8", [128, E])
        slot_f = sb("slot_f", [128, NTT])
        slot = [sb(f"slot{k}", [128, NTT], I32) for k in range(2)]
        le = sb("le", [1, NJ, E])
        owner_f = sb("owner_f", [1, NJ])
        owner = sb("owner", [1, NJ], I32)
        wt = [sb(f"wt{k}", [128, NTT]) for k in range(2)]
        xs = sb("xs", [128, 2, XW])
        xsT = sb("xsT", [KH, 2, 2, 128])
        act_g = sb("act_g", [128, HF])
        hid = sb("hid", [128, HF])
        hidT = sb("hidT", [128, 2, HF])
        ys = sb("ys", [128, 2, D])
        yidx = sb("yidx", [128, 2], I32)
        yweight = sb("yweight", [128, 2])
        xe2 = sb("xe2", [128, NTT, XW])

        gu = pb("gu", [128, 2 * HF])
        hps = pb("hps", [128, 1024])
        xps = pb("xps", [128, 512])
        yps = pb("yps", [128, 512])
        cnt = pb("cnt", [128, 512])

        w_in = sem("expert_weights_loaded")
        xe_in = [sem(f"tokens_loaded{k}") for k in range(2)]
        mk = sem("masks_made")
        mk_v = sem("masks_made_dve")
        rt_a = sem("routing_exp")
        rt_p = sem("routing_counts")
        scattered = sem("tokens_scattered")
        xs_in = [sem(f"slot_tile_loaded{b}") for b in range(2)]
        xt_ps = sem("slot_tile_transposed")
        xt_sb = sem("slot_tile_ready")
        gu_ok = sem("gate_up_done")
        sg_ok = sem("gate_activated")
        hid_ok = sem("hidden_ready")
        ht_ps = sem("hidden_transposed")
        ht_sb = sem("hidden_turned_ready")
        y_ps = sem("down_done")
        y_sb = sem("rows_ready")
        ix_ok = sem("row_places_ready")
        y_out = [sem(f"rows_scattered{b}") for b in range(2)]
        passes = {e: sem(f"expert_passes_{e}") for e in ("SP", "Pool")}

        def alone(eng):
            eng.sem_inc(passes[eng.engine.name], 1)

        block = ctx.enter_context(nc.Block())
        KT = HF // 128
        j_all = range(NJ)

        def bc_t(x):
            return x.unsqueeze(2).to_broadcast([128, NTT, E])

        def sp_tile(sp, j, b):
            wait(sp, xt_ps, j - 1)
            alone(sp)
            wait(sp, ix_ok, j - 1)
            alone(sp)
            sp.dma_start(xs[:, b, :], dram["xs"][bass.ds(j, 1)].rearrange("a p k -> p (a k)")).then_inc(xs_in[b], 16)

        def pe_xT(pe, j, b, n):
            pe.wait_ge(xs_in[b], 16 * n)
            wait(pe, xt_sb, j)
            for k in range(2):
                mm = pe.transpose(xps[0:KH, 128 * k:128 * k + 128], xs[:, b, KH * k:KH * k + KH], ident[:])
            mm.then_inc(xt_ps, 1)

        def act_xT(act, j, b):
            act.wait_ge(xt_ps, j + 1)
            wait(act, gu_ok, j - 1)
            act.activation(xsT[:, b].rearrange("p k t -> p (k t)"), xps[0:KH, 0:256], ACT.Copy).then_inc(xt_sb, 1)

        def pe_gu(pe, j, b, e):
            pe.wait_ge(xt_sb, j + 1)
            wait(pe, hid_ok, j)
            for n in range(3):
                for k in range(2):
                    mm = pe.matmul(gu[:, 512 * n:512 * n + 512], xsT[:, b, k, :], w13[:, bass.ds(e, 1), k, 512 * n:512 * n + 512].rearrange("p a n -> p (a n)"), start=(k == 0), stop=(k == 1))
            mm.then_inc(gu_ok, 1)

        def act_gate(act, j):
            act.wait_ge(gu_ok, j + 1)
            wait(act, hid_ok, j)
            act.activation(act_g[:], gu[:, 0:HF], ACT.Silu).then_inc(sg_ok, 1)

        def dve_hid(v, j):
            v.wait_ge(sg_ok, j + 1)
            wait(v, ht_ps, j)
            v.tensor_tensor(hid[:], act_g[:], gu[:, HF:2 * HF], ALU.mult).then_inc(hid_ok, 1)

        def pe_hT(pe, j):
            pe.wait_ge(hid_ok, j + 1)
            wait(pe, ht_sb, j)
            for k in range(KT):
                mm = pe.transpose(hps[:, 128 * k:128 * k + 128], hid[:, 128 * k:128 * k + 128], ident[:])
            mm.then_inc(ht_ps, 1)

        def act_hT(act, j, b):
            act.wait_ge(ht_ps, j + 1)
            wait(act, y_ps, j - 1)
            act.activation(hidT[:, b, :], hps[:, 0:HF], ACT.Copy).then_inc(ht_sb, 1)

        def pe_down(pe, j, b, e):
            pe.wait_ge(ht_sb, j + 1)
            wait(pe, y_sb, j)
            for k in range(KT):
                mm = pe.matmul(yps[:, 0:D], hidT[:, b, 128 * k:128 * k + 128], wd[:, bass.ds(e, 1), k, :].rearrange("p a n -> p (a n)"), start=(k == 0), stop=(k == KT - 1))
            mm.then_inc(y_ps, 1)

        def dve_y(v, j, b, n):
            v.wait_ge(y_ps, j + 1)
            wait(v, y_out[b], 16 * n)
            v.wait_ge(ix_ok, j + 1)
            v.tensor_scalar(ys[:, b, :], yps[:, 0:D], yweight[:, b:b + 1], None, ALU.mult).then_inc(y_sb, 1)

        def dve_idx(v, j, b, n):
            v.wait_ge(xs_in[b], 16 * n + 16)
            wait(v, y_out[b], 16 * n)
            v.tensor_copy(yweight[:, b:b + 1], xs[:, b, D + 1:D + 2])
            v.tensor_copy(yidx[:, b:b + 1], xs[:, b, D:D + 1]).then_inc(ix_ok, 1)

        def pool_y(gp, j, b, n):
            gp.wait_ge(y_sb, j + 1)
            alone(gp)
            wait(gp, y_out[1 - b], 16 * (n + b))
            if not isinstance(n, int):
                alone(gp)
            gp.indirect_dma_start(dram["out"], bass.IndirectOffsetOnAxis(ap=yidx[:, b:b + 1], axis=0), ys[:, b, :], None, compute_op=ALU.add).then_inc(y_out[b], 16)

        def owner_of(pe, j):
            return pe.value_load(owner[0:1, bass.ds(j, 1)], min_val=0, max_val=E - 1)

        rv = Steps(sem("routing_dve"), "max0 eq0 cand0 best0 pick0 left max1 eq1 cand1 best1 pick1 both diff den w0 w1 row0 "
                   "totals cum tiles0 tiles1 tiles2 ends starts excl off map s0 slots0 place0 s1 slots1 place1 ge sum owner")

        def turn(v, op, name):
            op.then_inc(rv.sem, 1)
            v.wait_ge(rv.sem, rv.after(name, 0))

        def dve_route(v):
            def by_expert(x):
                return x[:].unsqueeze(1).to_broadcast([128, NTT, E])

            v.wait_ge(mk, 2)
            v.tensor_copy(rev[:], rev_i[:])
            v.tensor_copy(tile_f[:], tile_i[:])
            v.memset(one8[:], 1.0)
            v.memset(carry_on[:], 1.0)
            v.memset(xe2[:, :, D:XW], 0.0)
            v.memset(xe[:, :, D:XW], 0.0).then_inc(mk_v, 1)
            v.wait_ge(mk_v, 1)
            v.memset(carry_on[:, :, 0:1], 0.0)
            v.tensor_copy(xe2[:, :, D:D + 1], dest[:].unsqueeze(2))
            v.tensor_copy(xe[:, :, D:D + 1], dest[:].unsqueeze(2)).then_inc(mk_v, 1)
            v.wait_ge(mk_v, 2)
            src = logits
            for k in range(2):
                turn(v, v.tensor_reduce(top[k][:], src[:], AX.X, ALU.max), f"max{k}")
                turn(v, v.tensor_tensor(both[:], src[:], bc_t(top[k][:]), ALU.is_equal), f"eq{k}")
                turn(v, v.tensor_tensor(cand[:], both[:], by_expert(rev), ALU.mult), f"cand{k}")
                turn(v, v.tensor_reduce(best[:], cand[:], AX.X, ALU.max), f"best{k}")
                turn(v, v.tensor_tensor(pick[k][:], cand[:], bc_t(best[:]), ALU.is_equal), f"pick{k}")
                if k == 0:
                    turn(v, v.scalar_tensor_tensor(left[:], pick[0][:], -3.0e38, logits[:], ALU.mult, ALU.add), "left")
                    src = left
            turn(v, v.tensor_tensor(both[:], pick[0][:], pick[1][:], ALU.add), "both")
            turn(v, v.tensor_tensor(wt[1][:], top[1][:], top[0][:], ALU.subtract), "diff")
            v.wait_ge(rt_a, 1)
            turn(v, v.tensor_scalar(slot_f[:], wt[1][:], 1.0, None, ALU.add), "den")
            turn(v, v.reciprocal(wt[0][:], slot_f[:]), "w0")
            turn(v, v.tensor_tensor(xe2[:, :, D + 1:D + 2], wt[1][:].unsqueeze(2), wt[0][:].unsqueeze(2), ALU.mult), "w1")
            turn(v, v.tensor_copy(xe[:, :, D + 1:D + 2], wt[0][:].unsqueeze(2)), "row0")
            v.wait_ge(rt_p, 1)
            turn(v, v.tensor_copy(totals[:], cnt[:, NTT * E:2 * NTT * E].rearrange("p (t e) -> p e t", e=E)), "totals")
            turn(v, v.tensor_tensor_scan(cum[:].rearrange("p e t -> p (e t)"), carry_on[:].rearrange("p e t -> p (e t)"), totals[:].rearrange("p e t -> p (e t)"), 0.0, ALU.mult, ALU.add), "cum")
            turn(v, v.tensor_scalar(tiles_i[:].unsqueeze(2), cum[:, :, NTT - 1:NTT], 127.0, None, ALU.add), "tiles0")
            turn(v, v.tensor_scalar(tiles_i[:], tiles_i[:], 7, None, ALU.arith_shift_right), "tiles1")
            turn(v, v.tensor_copy(tiles_f[:], tiles_i[:]), "tiles2")
            turn(v, v.tensor_tensor_scan(ends[:], one8[:], tiles_f[:], 0.0, ALU.mult, ALU.add), "ends")
            turn(v, v.tensor_tensor(starts[:], ends[:], tiles_f[:], ALU.subtract), "starts")
            turn(v, v.tensor_tensor(cum[:], cum[:], totals[:], ALU.subtract), "excl")
            turn(v, v.scalar_tensor_tensor(cum[:], starts[:].unsqueeze(2).to_broadcast([128, E, NTT]), 128.0, cum[:], ALU.mult, ALU.add), "off")
            turn(v, v.tensor_tensor(slotmap[:], cnt[:, 0:NTT * E].rearrange("p (t e) -> p t e", e=E), cum[:].rearrange("p e t -> p t e"), ALU.add), "map")
            for k in range(2):
                turn(v, v.tensor_tensor(cand[:], pick[k][:], slotmap[:], ALU.mult), f"s{k}")
                turn(v, v.tensor_reduce(slot_f[:], cand[:], AX.X, ALU.add), f"slots{k}")
                turn(v, v.tensor_copy(slot[k][:], slot_f[:]), f"place{k}")
            turn(v, v.tensor_tensor(le[:], tile_f[:].unsqueeze(2).to_broadcast([1, NJ, E]), ends[0:1, :].unsqueeze(1).to_broadcast([1, NJ, E]), ALU.is_ge), "ge")
            turn(v, v.tensor_reduce(owner_f[:], le[:], AX.X, ALU.add), "sum")
            turn(v, v.tensor_scalar(owner[:], owner_f[:], float(E - 1), None, ALU.min), "owner")

        LAST = NJ - 1

        def all_tiles(eng, step, last):
            for j in range(2):
                step(j, j, 0)
            with eng.Fori(0, (NJ - 3) // 4) as i:
                for r in range(4):
                    step(4 * i + 2 + r, r % 2, 2 * i + 1 + r // 2)
            last(LAST, LAST % 2, LAST // 2)

        @block.sync
        def _(sp):
            rows = dram["x3"].rearrange("p c (t d) -> p (c t) d", d=D)
            sp.dma_start(xe[:, :, 0:D], rows).then_inc(xe_in[0], 16)
            sp.dma_start(xe2[:, :, 0:D], rows).then_inc(xe_in[1], 16)
            for e in range(E):
                sp.dma_start(w13[:, e].rearrange("p k n -> p (k n)"), a["w13"][:, e, :]).then_inc(w_in, 16)
                sp.dma_start(wd[:, e].rearrange("p k n -> p (k n)"), a["wd"][:, e, :]).then_inc(w_in, 16)
            sp.wait_ge(scattered, 16 * 2 * NTT)

            def tile(j, b, n):
                sp_tile(sp, j, b)

            all_tiles(sp, tile, tile)
            for b in range(2):
                sp.wait_ge(y_out[b], 16 * (NJ // 2 + 1 - b))
        @block.gpsimd
        def _(gp):
            gp.iota(rev_i[:], pattern=[[-1, E]], base=E, channel_multiplier=0)
            gp.iota(tile_i[:], pattern=[[1, NJ]], base=0, channel_multiplier=0)
            gp.iota(dest[:], pattern=[[128 * NT, NCH], [1, NT]], base=0, channel_multiplier=NT)
            gp.memset(every[:], 1.0).then_inc(mk, 1)
            gp.wait_ge(mk, 1)
            gp.affine_select(out=tri[:], in_=every[:], compare_op=ALU.is_gt, fill=0.0, base=0, pattern=[[1, 128]], channel_multiplier=-1).then_inc(mk, 1)
            gp.wait_ge(mk_v, 2)
            for k in range(2):
                gp.wait_ge(xe_in[k], 16)
                gp.wait_ge(rv.sem, rv.after(f"place{k}", 0))
                for t in range(NTT):
                    gp.indirect_dma_start(dram["xs"].rearrange("j p x -> (j p) x"), bass.IndirectOffsetOnAxis(ap=slot[k][:, t:t + 1], axis=0), (xe, xe2)[k][:, t, :], None).then_inc(scattered, 16)

            def tile(j, b, n):
                pool_y(gp, j, b, n)

            all_tiles(gp, tile, tile)

        @block.scalar
        def _(act):
            act.wait_ge(rv.sem, rv.after("diff", 0))
            act.activation(wt[1][:], wt[1][:], ACT.Exp).then_inc(rt_a, 1)
            act_xT(act, 0, 0)

            def tile(j, b, n):
                act_gate(act, j)
                act_xT(act, j + 1, 1 - b)
                act_hT(act, j, b)

            def last(j, b, n):
                act_gate(act, j)
                act_hT(act, j, b)

            all_tiles(act, tile, last)

        @block.vector
        def _(v):
            dve_route(v)

            def tile(j, b, n):
                dve_hid(v, j)
                if not isinstance(j, int) or j > 0:
                    dve_y(v, j - 1, 1 - b, n - 1 + b)
                dve_idx(v, j, b, n)

            def last(j, b, n):
                tile(j, b, n)
                dve_y(v, j, b, n)

            all_tiles(v, tile, last)

        @block.tensor
        def _(pe):
            pe.wait_ge(mk, 2)
            pe.wait_ge(rv.sem, rv.after("both", 0))
            pe.matmul(cnt[:, 0:NTT * E], tri[:], both[:].rearrange("p t e -> p (t e)"), start=True, stop=True)
            pe.matmul(cnt[:, NTT * E:2 * NTT * E], every[:], both[:].rearrange("p t e -> p (t e)"), start=True, stop=True).then_inc(rt_p, 1)
            pe.wait_ge(w_in, 16 * 2 * E)
            pe.wait_ge(rv.sem, rv.after("owner", 0))
            pe_xT(pe, 0, 0, 1)
            ahead = {}

            def tile(j, b, n, follows=True, read_next=False):
                e = ahead.pop("expert") if ahead else owner_of(pe, j)
                pe_gu(pe, j, b, e)
                if follows:
                    pe_xT(pe, j + 1, 1 - b, n + 1 + b)
                if not isinstance(j, int) or j > 0:
                    pe_down(pe, j - 1, 1 - b, owner_of(pe, j - 1))
                if read_next:
                    ahead["expert"] = owner_of(pe, j + 1)
                pe_hT(pe, j)

            for j in range(2):
                tile(j, j, 0)
            with pe.Fori(0, (NJ - 3) // 4) as i:
                for r in range(4):
                    tile(4 * i + 2 + r, r % 2, 2 * i + 1 + r // 2, read_next=r < 3)
            tile(LAST, 0, LAST // 2, follows=False)
            pe_down(pe, LAST, 0, owner_of(pe, LAST))


INPUTS = ["p_tok", "p_T", "ids", "taus", "tok_emb", "seg_emb", "w_tau", "b_tau", "alpha", "projT", "tgam", "tbet", "projb",
          "bm_in", "inT", "outw", "bmoT", "xpw_bc", "xpw_dt", "dtw", "dtb", "cw", "cb", "dskip", "a_log",
          "outb", "ln_g", "ln_b", "rw", "w13", "wd"]


def fusion_block(nc, a, out):
    dram = {
        "x3": nc.dram_tensor("x3_scratch", [128, NCH, NT * D], F32, kind="Internal").ap(),
        "xs": nc.dram_tensor("slot_rows", [NJ, 128, XW], F32, kind="Internal").ap(),
        "out": out,
    }
    with ExitStack() as ctx:
        def sem(name):
            return ctx.enter_context(nc.semaphore(name))

        ident = ctx.enter_context(nc.sbuf_tensor("ident", [128, 128], F32))
        logits = ctx.enter_context(nc.sbuf_tensor("logits", [128, NTT, E], F32))
        build_mamba(nc, a, dram, ident, logits, sem)
        build_experts(nc, a, dram, ident, logits, sem)


def lay_out(f):
    import numpy as np

    def rows(x, p):
        x = x.reshape(-1, p, *x.shape[1:])
        return np.moveaxis(x, 1, 0).reshape(p, -1)

    patches = f["x"].reshape(B, 3, 4, 16, 4, 16).transpose(0, 2, 4, 3, 5, 1).reshape(NCH, 128, PD)

    def texts(x):
        return x.reshape(NCH, 2, 128)

    xpw = f["L0_attn_m_xproj_w"].T
    row = lambda n: f[n].reshape(1, -1)
    column = lambda n, p: rows(f[n].reshape(-1, 1), p)
    a = {
        "p_tok": patches,
        "p_T": patches.reshape(NCH, 128, PD // 128, 128).transpose(0, 3, 2, 1).reshape(NCH, 128, PD),
        "ids": np.concatenate([texts(f["x_txt"]), texts(f["itok_BS_0_3"])], 1).transpose(0, 2, 1),
        "taus": np.concatenate([texts(f["fside_BS_age"]), texts(f["fside_BS_position"])], 1).transpose(0, 2, 1),
        "tok_emb": f["L0_txt_token_emb"], "seg_emb": f["L0_txt_seg_emb"],
        "w_tau": np.concatenate([f["L0_txt_w_age"], f["L0_txt_w0_age"], f["L0_txt_w_abs"], f["L0_txt_w0_abs"]], 1),
        "b_tau": np.concatenate([f["L0_txt_b_age"], f["L0_txt_b0_age"], f["L0_txt_b_abs"], f["L0_txt_b0_abs"]], 1),
        "alpha": np.stack([f["L0_txt_alpha_age"], f["L0_txt_alpha_abs"], f["L0_txt_alpha_seg"]]).reshape(1, 3),
        "projT": rows(f["L0_tok_W_proj"].T, 128), "tgam": column("L0_tok_gamma", 128), "tbet": column("L0_tok_beta", 128),
        "projb": row("L0_tok_b_proj"),
        "bm_in": rows(np.concatenate([f["L0_attn_bm_in_w"], f["L0_attn_bm_in_b"].reshape(-1, 1)], 1), KH), "inT": rows(f["L0_attn_m_in_w"].T, KH),
        "outw": rows(f["L0_attn_m_out_w"], KH), "bmoT": rows(f["L0_attn_bm_out_w"].T, KH),
        "xpw_bc": rows(xpw[:, R:], 128).reshape(128, NC, 2 * NS), "xpw_dt": rows(xpw[:, :R], 128).reshape(128, NC, R),
        "dtw": f["L0_attn_m_dt_w"].T, "dtb": column("L0_attn_m_dt_b", 128),
        "cw": rows(f["L0_attn_m_conv_w"], 128), "cb": column("L0_attn_m_conv_b", 128),
        "dskip": column("L0_attn_m_D", 128), "a_log": rows(f["L0_attn_m_A_log"], 128),
        "outb": row("L0_attn_bm_out_b"), "ln_g": row("L0_attn_ln_g"), "ln_b": row("L0_attn_ln_b"),
        "rw": rows(f["L0_ffn_router_w"].T, KH),
        "w13": np.stack([f["L0_ffn_Wg"], f["L0_ffn_Wu"]], 1).reshape(E, 2, HF, 2, KH).transpose(4, 0, 3, 1, 2).reshape(KH, E, 4 * HF),
        "wd": f["L0_ffn_Wd"].reshape(E, D, HF // 128, 128).transpose(3, 0, 2, 1).reshape(128, E, (HF // 128) * D),
    }
    return {n: np.ascontiguousarray(x) for n, x in a.items()}


def kernel(**inputs):
    import numpy as np
    import concourse.bacc as bacc
    from concourse.bass_utils import run_bass_kernel_spmd

    nc = bacc.Bacc("TRN2", target_bir_lowering=False, num_devices=1)
    laid = lay_out({n: np.asarray(x) for n, x in inputs.items()})
    args = {n: nc.dram_tensor(f"in_{n}", laid[n].shape, mybir.dt.from_np(laid[n].dtype), kind="ExternalInput").ap() for n in INPUTS}
    out = nc.dram_tensor("out_tokens", [NTOK + 128, D], F32, kind="ExternalOutput").ap()
    fusion_block(nc, args, out)
    r = run_bass_kernel_spmd(nc, [{f"in_{n}": laid[n] for n in INPUTS}], core_ids=[0])
    y = np.asarray(r.results[0]["out_tokens"])[:NTOK].reshape(NCH, 128, NT, D)
    image = y[:, :, 0].reshape(NCH, CB, LI, D)
    text = y[:, :, 1:].transpose(0, 2, 1, 3).reshape(NCH, CB, LT, D)
    return np.concatenate([image, text], 2).reshape(B, L, D)
```
